# Optimizing a Trainium2 kernel written in Bass

```python
import numpy as np
import jax
import jax.numpy as jnp

def _softmax(x, axis=-1):
    return jax.nn.softmax(x, axis=axis)

def _gelu(x):
    return jax.nn.gelu(x, approximate=True)

def _silu(x):
    return jax.nn.silu(x)

def _sigmoid(x):
    return jax.nn.sigmoid(x)

def _layernorm(x, axis=-1, eps=1e-05):
    m = jnp.mean(x, axis=axis, keepdims=True)
    v = jnp.var(x, axis=axis, keepdims=True)
    return (x - m) / jnp.sqrt(v + eps)

def _scatter_add(tgt, idx, src, axis=0):
    return tgt.at[idx].add(src)

def _segment_sum(src, seg, n):
    return jax.ops.segment_sum(src, seg, n)
kernel_name = 'mk_seq_preln_d4_jaxref_r8_3e2077'

def setup_inputs(seed: int=0):
    np.random.seed(seed)
    _w = jnp.asarray

    def _L0_attn_setup():
        import jax, jax.numpy as jnp
        import numpy as np
        NUM_HEADS = 16
        NEG = -1000000000.0

        def _split_heads(t, h):
            *lead, s, hd = t.shape
            return jnp.swapaxes(t.reshape(*lead, s, h, hd // h), -3, -2)
        key = jax.random.key(seed)
        ks = jax.random.split(key, 5)
        B, S, D = (4, 256, 128)
        scale = 1.0 / np.sqrt(D)
        return {'x': jax.random.normal(ks[0], (B, S, D), dtype=jnp.float32), 'WQ': jax.random.normal(ks[1], (D, D), dtype=jnp.float32) * scale, 'WK': jax.random.normal(ks[2], (D, D), dtype=jnp.float32) * scale, 'WV': jax.random.normal(ks[3], (D, D), dtype=jnp.float32) * scale, 'WO': jax.random.normal(ks[4], (D, D), dtype=jnp.float32) * scale}
    _L0_attn_in = _L0_attn_setup()

    def _L0_ffn_setup():
        import jax, jax.numpy as jnp
        import numpy as np
        E = 8
        K = 2
        CAPACITY_FACTOR = 1.25
        key = jax.random.key(seed)
        ks = jax.random.split(key, 4)
        B, T, C, H = (8, 256, 128, 512)
        x = jax.random.normal(ks[0], (B, T, C), jnp.float32)
        Wr = jax.random.normal(ks[1], (C, E), jnp.float32) * 0.02
        br = jnp.zeros((E,), jnp.float32)
        W1 = jax.random.normal(ks[2], (E, C, H), jnp.float32) * 0.02
        b1 = jnp.zeros((E, H), jnp.float32)
        W2 = jax.random.normal(ks[3], (E, H, C), jnp.float32) * 0.02
        b2 = jnp.zeros((E, C), jnp.float32)
        return {'x': x, 'Wr': Wr, 'br': br, 'W1': W1, 'b1': b1, 'W2': W2, 'b2': b2}
    _L0_ffn_in = _L0_ffn_setup()

    def _L1_attn_setup():
        import jax, jax.numpy as jnp
        import numpy as np
        D_MODEL = 128
        NUM_HEADS = 16
        HEAD_DIM = D_MODEL // NUM_HEADS
        NEG = -1000000000.0
        key = jax.random.key(seed)
        kx, kq, kk, kv, ko = jax.random.split(key, 5)
        scale = 1.0 / np.sqrt(D_MODEL)
        x = jax.random.normal(kx, (4, 256, D_MODEL), dtype=jnp.float32)
        Wq = jax.random.normal(kq, (D_MODEL, D_MODEL), dtype=jnp.float32) * scale
        Wk = jax.random.normal(kk, (D_MODEL, D_MODEL), dtype=jnp.float32) * scale
        Wv = jax.random.normal(kv, (D_MODEL, D_MODEL), dtype=jnp.float32) * scale
        Wo = jax.random.normal(ko, (D_MODEL, D_MODEL), dtype=jnp.float32) * scale
        return {'x': x, 'Wq': Wq, 'Wk': Wk, 'Wv': Wv, 'Wo': Wo}
    _L1_attn_in = _L1_attn_setup()

    def _L1_ffn_setup():
        import jax, jax.numpy as jnp
        import numpy as np
        D_MODEL = 128
        NUM_HEADS = 4
        NUM_EXPERTS = 8
        TOP_K = 2
        D_FF = 128
        EPS = 1e-06

        def _rmsnorm(x, g):
            return x * jax.lax.rsqrt(jnp.mean(x * x, axis=-1, keepdims=True) + EPS) * g

        def _swiglu(x, w1, w2, w3):
            return jax.nn.silu(x @ w1.T) * (x @ w3.T) @ w2.T
        key = jax.random.key(seed)
        ks = jax.random.split(key, 16)
        d, e, f = (D_MODEL, NUM_EXPERTS, D_FF)
        dc = d // 4
        s = 0.02
        return {'X': jax.random.normal(ks[0], (2, 128, d), dtype=jnp.float32), 'g1': jnp.ones((d,), jnp.float32), 'g2': jnp.ones((d,), jnp.float32), 'Wq': jax.random.normal(ks[1], (d, d), jnp.float32) * s, 'Wkc': jax.random.normal(ks[2], (dc, d), jnp.float32) * s, 'Wvc': jax.random.normal(ks[3], (dc, d), jnp.float32) * s, 'Wo': jax.random.normal(ks[4], (d, d), jnp.float32) * s, 'Wr': jax.random.normal(ks[5], (e, d), jnp.float32) * s, 'expert_bias': jnp.zeros((e,), jnp.float32), 'sW1': jax.random.normal(ks[6], (f, d), jnp.float32) * s, 'sW2': jax.random.normal(ks[7], (d, f), jnp.float32) * s, 'sW3': jax.random.normal(ks[8], (f, d), jnp.float32) * s, 'eW1': jax.random.normal(ks[9], (e, f, d), jnp.float32) * s, 'eW2': jax.random.normal(ks[10], (e, d, f), jnp.float32) * s, 'eW3': jax.random.normal(ks[11], (e, f, d), jnp.float32) * s}
    _L1_ffn_in = _L1_ffn_setup()

    def _L2_attn_setup():
        import jax, jax.numpy as jnp
        import numpy as np
        NUM_HEADS = 16
        EPS = 1e-05
        key = jax.random.key(seed)
        k1, k2, k3 = jax.random.split(key, 3)
        b, n, d = (2, 256, 128)
        x = jax.random.normal(k1, (b, n, d), dtype=jnp.float32)
        wqkv = jax.random.normal(k2, (d, 3 * d), dtype=jnp.float32) * (1.0 / np.sqrt(d))
        wo = jax.random.normal(k3, (d, d), dtype=jnp.float32) * (1.0 / np.sqrt(d))
        return {'x': x, 'wqkv': wqkv, 'wo': wo}
    _L2_attn_in = _L2_attn_setup()

    def _L2_ffn_setup():
        import jax, jax.numpy as jnp
        import numpy as np
        D, H, NE, K, ED = (128, 16, 8, 2, 512)
        B, S = (4, 128)
        EPS = 1e-06

        def rmsnorm(x, w):
            ms = jnp.mean(jnp.square(x.astype(jnp.float32)), axis=-1, keepdims=True)
            return x * jax.lax.rsqrt(ms + EPS).astype(x.dtype) * w

        def attn(x, qkv_w, o_w):
            b, s, d = x.shape
            hd = d // H
            qkv = (x @ qkv_w.T).reshape(b, s, 3, H, hd).transpose(2, 0, 3, 1, 4)
            q, k, v = (qkv[0], qkv[1], qkv[2])
            a = jnp.einsum('bhqd,bhkd->bhqk', q, k) * hd ** (-0.5)
            mask = jnp.triu(jnp.ones((s, s), dtype=bool), 1)
            a = jax.nn.softmax(jnp.where(mask, -1000000000.0, a), axis=-1)
            out = jnp.einsum('bhqk,bhkd->bhqd', a, v).transpose(0, 2, 1, 3).reshape(b, s, d)
            return out @ o_w.T

        def moe(x, gate_w, up_w, down_w):
            b, s, d = x.shape
            xf = x.reshape(b * s, d)
            gp = jax.nn.softmax(xf @ gate_w.T, axis=-1)
            ew, _ = jax.lax.top_k(gp, K)
            ew = ew / (jnp.sum(ew, axis=-1, keepdims=True) + 1e-09)
            ef = jax.nn.silu(xf @ up_w.T) @ down_w.T
            out = ef * jnp.sum(ew, axis=-1, keepdims=True)
            return out.reshape(b, s, d)
        key = jax.random.key(seed)
        ks = jax.random.split(key, 8)
        sd = 1.0 / np.sqrt(D)
        se = 1.0 / np.sqrt(ED)
        return {'x': jax.random.normal(ks[0], (B, S, D), dtype=jnp.float32), 'n1_w': jnp.ones((D,), jnp.float32), 'qkv_w': jax.random.normal(ks[1], (3 * D, D), jnp.float32) * sd, 'o_w': jax.random.normal(ks[2], (D, D), jnp.float32) * sd, 'n2_w': jnp.ones((D,), jnp.float32), 'gate_w': jax.random.normal(ks[3], (NE, D), jnp.float32) * sd, 'up_w': jax.random.normal(ks[4], (ED, D), jnp.float32) * sd, 'down_w': jax.random.normal(ks[5], (D, ED), jnp.float32) * se}
    _L2_ffn_in = _L2_ffn_setup()

    def _L3_attn_setup():
        import jax, jax.numpy as jnp
        import numpy as np
        ALPHA = 1.2
        A = 1.0
        BANDWIDTH = 1.0
        D_INTRINSIC = 2
        SPHERE_RADIUS = 1.0
        NUM_HEADS = 16
        HIDDEN = 128
        HEAD_DIM = HIDDEN // NUM_HEADS
        EPS = 1e-07

        def _l2norm(t):
            n = jnp.sqrt(jnp.sum(t * t, axis=-1, keepdims=True))
            return t / jnp.maximum(n, 1e-12)
        key = jax.random.key(seed)
        k1, k2, k3, k4, k5 = jax.random.split(key, 5)
        B, S = (2, 256)
        scale = 0.02
        return {'x': jax.random.normal(k1, (B, S, HIDDEN), dtype=jnp.float32), 'w_qkv': jax.random.normal(k2, (3 * HIDDEN, HIDDEN), dtype=jnp.float32) * scale, 'b_qkv': jnp.zeros((3 * HIDDEN,), dtype=jnp.float32), 'w_out': jax.random.normal(k3, (HIDDEN, HIDDEN), dtype=jnp.float32) * scale, 'b_out': jnp.zeros((HIDDEN,), dtype=jnp.float32)}
    _L3_attn_in = _L3_attn_setup()

    def _L3_ffn_setup():
        import jax, jax.numpy as jnp
        import numpy as np
        GROUP = 16
        EPS = 1e-05

        def _dequant(q, scale):
            w = q.astype(jnp.float32) / 7.5 - 1.0
            return w * jnp.repeat(scale, GROUP, axis=1)

        def _qlora_linear(x, q, scale, bias, la, lb):
            w = _dequant(q, scale)
            base = jnp.einsum('btd,od->bto', x, w) + bias
            lora = jnp.einsum('btr,or->bto', jnp.einsum('btd,rd->btr', x, la), lb)
            return base + lora

        def _layernorm(x, g, b):
            mu = jnp.mean(x, axis=-1, keepdims=True)
            var = jnp.mean(jnp.square(x - mu), axis=-1, keepdims=True)
            return (x - mu) * jax.lax.rsqrt(var + EPS) * g + b
        key = jax.random.key(seed)
        ks = jax.random.split(key, 6)
        D, R, B, T = (128, 32, 8, 512)
        x = jax.random.normal(ks[0], (B, T, D), dtype=jnp.float32)
        qweights = jax.random.randint(ks[1], (6, D, D), 0, 16, dtype=jnp.int32)
        scales = jax.random.uniform(ks[2], (6, D, D // GROUP), dtype=jnp.float32)
        biases = jax.random.normal(ks[3], (6, D), dtype=jnp.float32) * 0.02
        lora_a = jax.random.normal(ks[4], (6, R, D), dtype=jnp.float32) * 0.02
        lora_b = jax.random.normal(ks[5], (6, D, R), dtype=jnp.float32) * 0.02
        ln_gamma = jnp.ones((3, D), dtype=jnp.float32)
        ln_beta = jnp.zeros((3, D), dtype=jnp.float32)
        return {'x': x, 'qweights': qweights, 'scales': scales, 'biases': biases, 'lora_a': lora_a, 'lora_b': lora_b, 'ln_gamma': ln_gamma, 'ln_beta': ln_beta}
    _L3_ffn_in = _L3_ffn_setup()
    _d = {'L0_attn_x': _L0_attn_in['x'], 'L0_attn_WQ': _L0_attn_in['WQ'], 'L0_attn_WK': _L0_attn_in['WK'], 'L0_attn_WV': _L0_attn_in['WV'], 'L0_attn_WO': _L0_attn_in['WO'], 'L0_ffn_Wr': _L0_ffn_in['Wr'], 'L0_ffn_br': _L0_ffn_in['br'], 'L0_ffn_W1': _L0_ffn_in['W1'], 'L0_ffn_b1': _L0_ffn_in['b1'], 'L0_ffn_W2': _L0_ffn_in['W2'], 'L0_ffn_b2': _L0_ffn_in['b2'], 'L1_attn_Wq': _L1_attn_in['Wq'], 'L1_attn_Wk': _L1_attn_in['Wk'], 'L1_attn_Wv': _L1_attn_in['Wv'], 'L1_attn_Wo': _L1_attn_in['Wo'], 'L1_ffn_g1': _L1_ffn_in['g1'], 'L1_ffn_g2': _L1_ffn_in['g2'], 'L1_ffn_Wq': _L1_ffn_in['Wq'], 'L1_ffn_Wkc': _L1_ffn_in['Wkc'], 'L1_ffn_Wvc': _L1_ffn_in['Wvc'], 'L1_ffn_Wo': _L1_ffn_in['Wo'], 'L1_ffn_Wr': _L1_ffn_in['Wr'], 'L1_ffn_expert_bias': _L1_ffn_in['expert_bias'], 'L1_ffn_sW1': _L1_ffn_in['sW1'], 'L1_ffn_sW2': _L1_ffn_in['sW2'], 'L1_ffn_sW3': _L1_ffn_in['sW3'], 'L1_ffn_eW1': _L1_ffn_in['eW1'], 'L1_ffn_eW2': _L1_ffn_in['eW2'], 'L1_ffn_eW3': _L1_ffn_in['eW3'], 'L2_attn_wqkv': _L2_attn_in['wqkv'], 'L2_attn_wo': _L2_attn_in['wo'], 'L2_ffn_n1_w': _L2_ffn_in['n1_w'], 'L2_ffn_qkv_w': _L2_ffn_in['qkv_w'], 'L2_ffn_o_w': _L2_ffn_in['o_w'], 'L2_ffn_n2_w': _L2_ffn_in['n2_w'], 'L2_ffn_gate_w': _L2_ffn_in['gate_w'], 'L2_ffn_up_w': _L2_ffn_in['up_w'], 'L2_ffn_down_w': _L2_ffn_in['down_w'], 'L3_attn_w_qkv': _L3_attn_in['w_qkv'], 'L3_attn_b_qkv': _L3_attn_in['b_qkv'], 'L3_attn_w_out': _L3_attn_in['w_out'], 'L3_attn_b_out': _L3_attn_in['b_out'], 'L3_ffn_qweights': _L3_ffn_in['qweights'], 'L3_ffn_scales': _L3_ffn_in['scales'], 'L3_ffn_biases': _L3_ffn_in['biases'], 'L3_ffn_lora_a': _L3_ffn_in['lora_a'], 'L3_ffn_lora_b': _L3_ffn_in['lora_b'], 'L3_ffn_ln_gamma': _L3_ffn_in['ln_gamma'], 'L3_ffn_ln_beta': _L3_ffn_in['ln_beta']}
    _x0 = _d['L0_attn_x']
    _d['L0_attn_x'] = jax.random.normal(jax.random.fold_in(jax.random.key(seed), 1), (16, 256, 128), dtype=_x0.dtype)
    del _x0
    return _d

def reference(L0_attn_x, L0_attn_WQ, L0_attn_WK, L0_attn_WV, L0_attn_WO, L0_ffn_Wr, L0_ffn_br, L0_ffn_W1, L0_ffn_b1, L0_ffn_W2, L0_ffn_b2, L1_attn_Wq, L1_attn_Wk, L1_attn_Wv, L1_attn_Wo, L1_ffn_g1, L1_ffn_g2, L1_ffn_Wq, L1_ffn_Wkc, L1_ffn_Wvc, L1_ffn_Wo, L1_ffn_Wr, L1_ffn_expert_bias, L1_ffn_sW1, L1_ffn_sW2, L1_ffn_sW3, L1_ffn_eW1, L1_ffn_eW2, L1_ffn_eW3, L2_attn_wqkv, L2_attn_wo, L2_ffn_n1_w, L2_ffn_qkv_w, L2_ffn_o_w, L2_ffn_n2_w, L2_ffn_gate_w, L2_ffn_up_w, L2_ffn_down_w, L3_attn_w_qkv, L3_attn_b_qkv, L3_attn_w_out, L3_attn_b_out, L3_ffn_qweights, L3_ffn_scales, L3_ffn_biases, L3_ffn_lora_a, L3_ffn_lora_b, L3_ffn_ln_gamma, L3_ffn_ln_beta):

    def _L0_attn_ref(x, WQ, WK, WV, WO):
        import jax, jax.numpy as jnp
        import numpy as np
        NUM_HEADS = 16
        NEG = -1000000000.0

        def _split_heads(t, h):
            *lead, s, hd = t.shape
            return jnp.swapaxes(t.reshape(*lead, s, h, hd // h), -3, -2)
        h = NUM_HEADS
        S = x.shape[-2]
        Q = _split_heads(x @ WQ.T, h)
        K = _split_heads(x @ WK.T, h)
        V = _split_heads(x @ WV.T, h)
        dk = Q.shape[-1]
        scores = jnp.einsum('bhqd,bhkd->bhqk', Q, K) / jnp.sqrt(jnp.float32(dk))
        causal = jnp.tril(jnp.ones((S, S), dtype=bool))
        scores = jnp.where(causal, scores, NEG)
        m = jnp.max(scores, axis=-1, keepdims=True)
        e = jnp.exp(scores - m)
        attn = e / jnp.sum(e, axis=-1, keepdims=True)
        out = jnp.einsum('bhqk,bhkd->bhqd', attn, V)
        out = jnp.swapaxes(out, -3, -2).reshape(*x.shape[:-1], -1)
        return out @ WO.T

    def _L0_ffn_ref(x, Wr, br, W1, b1, W2, b2):
        import jax, jax.numpy as jnp
        import numpy as np
        E = 8
        K = 2
        CAPACITY_FACTOR = 1.25
        B, T, C = x.shape
        cap = max(1, int(T / E * CAPACITY_FACTOR))
        probs = jax.nn.softmax(x @ Wr + br, axis=-1)
        topk_p, topk_e = jax.lax.top_k(probs, K)
        e_flat = topk_e.reshape(B, T * K)
        p_flat = topk_p.reshape(B, T * K)
        oh = jax.nn.one_hot(e_flat, E, dtype=jnp.int32)
        pos_all = jnp.cumsum(oh, axis=1) - oh
        pos = jnp.take_along_axis(pos_all, e_flat[:, :, None], axis=2)[:, :, 0]
        keep = pos < cap
        b_idx = jnp.arange(B)[:, None]
        flat_idx = (e_flat * B + b_idx) * cap + jnp.minimum(pos, cap - 1)
        x_rep = jnp.broadcast_to(x[:, :, None, :], (B, T, K, C)).reshape(B, T * K, C)
        buf = jnp.zeros((E * B * cap, C), x.dtype).at[flat_idx.reshape(-1)].add((x_rep * keep[:, :, None].astype(x.dtype)).reshape(-1, C))
        buf = buf.reshape(E, B * cap, C)
        h = jax.nn.relu(jnp.einsum('enc,ech->enh', buf, W1) + b1[:, None, :])
        y = jnp.einsum('enh,ehc->enc', h, W2) + b2[:, None, :]
        y_tok = y.reshape(E * B * cap, C)[flat_idx.reshape(-1)].reshape(B, T * K, C)
        y_tok = y_tok * (p_flat * keep.astype(x.dtype))[:, :, None]
        return y_tok.reshape(B, T, K, C).sum(axis=2)

    def _L1_attn_ref(x, Wq, Wk, Wv, Wo):
        import jax, jax.numpy as jnp
        import numpy as np
        D_MODEL = 128
        NUM_HEADS = 16
        HEAD_DIM = D_MODEL // NUM_HEADS
        NEG = -1000000000.0
        B, S, _ = x.shape
        q = (x @ Wq.T).reshape(B, S, NUM_HEADS, HEAD_DIM).transpose(0, 2, 1, 3)
        k = (x @ Wk.T).reshape(B, S, NUM_HEADS, HEAD_DIM).transpose(0, 2, 1, 3)
        v = (x @ Wv.T).reshape(B, S, NUM_HEADS, HEAD_DIM).transpose(0, 2, 1, 3)
        scores = jnp.einsum('bhqd,bhkd->bhqk', q, k) / jnp.sqrt(jnp.float32(HEAD_DIM))
        mask = jnp.triu(jnp.ones((S, S), dtype=scores.dtype), k=1) * NEG
        scores = scores + mask
        attn = jax.nn.softmax(scores, axis=-1)
        out = jnp.einsum('bhqk,bhkd->bhqd', attn, v)
        out = out.transpose(0, 2, 1, 3).reshape(B, S, D_MODEL)
        return out @ Wo.T

    def _L1_ffn_ref(X, g1, g2, Wq, Wkc, Wvc, Wo, Wr, expert_bias, sW1, sW2, sW3, eW1, eW2, eW3):
        import jax, jax.numpy as jnp
        import numpy as np
        D_MODEL = 128
        NUM_HEADS = 4
        NUM_EXPERTS = 8
        TOP_K = 2
        D_FF = 128
        EPS = 1e-06

        def _rmsnorm(x, g):
            return x * jax.lax.rsqrt(jnp.mean(x * x, axis=-1, keepdims=True) + EPS) * g

        def _swiglu(x, w1, w2, w3):
            return jax.nn.silu(x @ w1.T) * (x @ w3.T) @ w2.T
        B, S, d = X.shape
        H = NUM_HEADS
        dk = d // H
        scale = 1.0 / jnp.sqrt(jnp.float32(dk))
        nx = _rmsnorm(X, g1)
        Q = (nx @ Wq.T).reshape(B, S, H, dk).transpose(0, 2, 1, 3)
        Kc = nx @ Wkc.T
        Vc = nx @ Wvc.T
        scores = jnp.einsum('bhsd,btd->bhst', Q, Kc) * scale
        attn = jax.nn.softmax(scores, axis=-1)
        out = jnp.einsum('bhst,btd->bhsd', attn, Vc)
        out = out.transpose(0, 2, 1, 3).reshape(B, S, d) @ Wo.T
        X = X + out
        nx = _rmsnorm(X, g2)
        xf = nx.reshape(-1, d)
        logits = xf @ Wr.T + expert_bias
        rw = jax.nn.softmax(logits, axis=-1)
        topw, topi = jax.lax.top_k(rw, TOP_K)
        topw = jax.nn.softmax(topw, axis=-1)
        combine = jnp.sum(jax.nn.one_hot(topi, NUM_EXPERTS, dtype=xf.dtype) * topw[..., None], axis=1)
        shared = _swiglu(xf, sW1, sW2, sW3)
        h = jax.nn.silu(jnp.einsum('td,efd->etf', xf, eW1)) * jnp.einsum('td,efd->etf', xf, eW3)
        eo = jnp.einsum('etf,edf->etd', h, eW2)
        specialist = jnp.einsum('te,etd->td', combine, eo)
        moe_out = (shared + specialist).reshape(B, S, d)
        return X + moe_out

    def _L2_attn_ref(x, wqkv, wo):
        import jax, jax.numpy as jnp
        import numpy as np
        NUM_HEADS = 16
        EPS = 1e-05
        b, n, d = x.shape
        h = NUM_HEADS
        hd = d // h
        qkv = x @ wqkv
        q, k, v = jnp.split(qkv, 3, axis=-1)
        q = jax.nn.relu(q)
        k = jax.nn.relu(k)
        split_heads = lambda t: t.reshape(b, n, h, hd).transpose(0, 2, 1, 3)
        q, k, v = (split_heads(q), split_heads(k), split_heads(v))
        kv = jnp.cumsum(k[..., :, None] * v[..., None, :], axis=2)
        num = jnp.einsum('bhnd,bhnde->bhne', q, kv)
        k_sum = jnp.cumsum(k, axis=2)
        den = jnp.einsum('bhnd,bhnd->bhn', q, k_sum)[..., None] + EPS
        y = num / den
        y = y.transpose(0, 2, 1, 3).reshape(b, n, d)
        return y @ wo

    def _L2_ffn_ref(x, n1_w, qkv_w, o_w, n2_w, gate_w, up_w, down_w):
        import jax, jax.numpy as jnp
        import numpy as np
        D, H, NE, K, ED = (128, 16, 8, 2, 512)
        B, S = (4, 128)
        EPS = 1e-06

        def rmsnorm(x, w):
            ms = jnp.mean(jnp.square(x.astype(jnp.float32)), axis=-1, keepdims=True)
            return x * jax.lax.rsqrt(ms + EPS).astype(x.dtype) * w

        def attn(x, qkv_w, o_w):
            b, s, d = x.shape
            hd = d // H
            qkv = (x @ qkv_w.T).reshape(b, s, 3, H, hd).transpose(2, 0, 3, 1, 4)
            q, k, v = (qkv[0], qkv[1], qkv[2])
            a = jnp.einsum('bhqd,bhkd->bhqk', q, k) * hd ** (-0.5)
            mask = jnp.triu(jnp.ones((s, s), dtype=bool), 1)
            a = jax.nn.softmax(jnp.where(mask, -1000000000.0, a), axis=-1)
            out = jnp.einsum('bhqk,bhkd->bhqd', a, v).transpose(0, 2, 1, 3).reshape(b, s, d)
            return out @ o_w.T

        def moe(x, gate_w, up_w, down_w):
            b, s, d = x.shape
            xf = x.reshape(b * s, d)
            gp = jax.nn.softmax(xf @ gate_w.T, axis=-1)
            ew, _ = jax.lax.top_k(gp, K)
            ew = ew / (jnp.sum(ew, axis=-1, keepdims=True) + 1e-09)
            ef = jax.nn.silu(xf @ up_w.T) @ down_w.T
            out = ef * jnp.sum(ew, axis=-1, keepdims=True)
            return out.reshape(b, s, d)
        x = x + attn(rmsnorm(x, n1_w), qkv_w, o_w)
        x = x + moe(rmsnorm(x, n2_w), gate_w, up_w, down_w)
        return x

    def _L3_attn_ref(x, w_qkv, b_qkv, w_out, b_out):
        import jax, jax.numpy as jnp
        import numpy as np
        ALPHA = 1.2
        A = 1.0
        BANDWIDTH = 1.0
        D_INTRINSIC = 2
        SPHERE_RADIUS = 1.0
        NUM_HEADS = 16
        HIDDEN = 128
        HEAD_DIM = HIDDEN // NUM_HEADS
        EPS = 1e-07

        def _l2norm(t):
            n = jnp.sqrt(jnp.sum(t * t, axis=-1, keepdims=True))
            return t / jnp.maximum(n, 1e-12)
        B, S, H = x.shape
        qkv = x @ w_qkv.T + b_qkv
        q, k, v = jnp.split(qkv, 3, axis=-1)
        to_heads = lambda t: t.reshape(B, S, NUM_HEADS, HEAD_DIM).transpose(0, 2, 1, 3)
        q = _l2norm(to_heads(q))
        k = _l2norm(to_heads(k))
        v = to_heads(v)
        cos = jnp.einsum('bhsd,bhtd->bhst', q, k)
        g_dist = jnp.arccos(jnp.clip(cos, -1.0 + EPS, 1.0 - EPS)) * SPHERE_RADIUS
        attn_score = (1.0 + g_dist / BANDWIDTH ** 0.5) ** (-D_INTRINSIC - ALPHA)
        n_r = jnp.sum(attn_score, axis=-1)
        n_c = jnp.sum(attn_score, axis=-2)
        k_tilde = (n_r ** (-A))[..., :, None] * attn_score * (n_c ** (-A))[..., None, :]
        probs = k_tilde / jnp.maximum(jnp.sum(k_tilde, axis=-1, keepdims=True), 1e-12)
        out = jnp.einsum('bhst,bhtd->bhsd', probs, v)
        out = out.transpose(0, 2, 1, 3).reshape(B, S, H)
        return out @ w_out.T + b_out

    def _L3_ffn_ref(x, qweights, scales, biases, lora_a, lora_b, ln_gamma, ln_beta):
        import jax, jax.numpy as jnp
        import numpy as np
        GROUP = 16
        EPS = 1e-05

        def _dequant(q, scale):
            w = q.astype(jnp.float32) / 7.5 - 1.0
            return w * jnp.repeat(scale, GROUP, axis=1)

        def _qlora_linear(x, q, scale, bias, la, lb):
            w = _dequant(q, scale)
            base = jnp.einsum('btd,od->bto', x, w) + bias
            lora = jnp.einsum('btr,or->bto', jnp.einsum('btd,rd->btr', x, la), lb)
            return base + lora

        def _layernorm(x, g, b):
            mu = jnp.mean(x, axis=-1, keepdims=True)
            var = jnp.mean(jnp.square(x - mu), axis=-1, keepdims=True)
            return (x - mu) * jax.lax.rsqrt(var + EPS) * g + b
        h = x
        for blk in range(3):
            i0, i1 = (2 * blk, 2 * blk + 1)
            y = _qlora_linear(h, qweights[i0], scales[i0], biases[i0], lora_a[i0], lora_b[i0])
            y = _layernorm(y, ln_gamma[blk], ln_beta[blk])
            y = jax.nn.gelu(y, approximate=False)
            y = _qlora_linear(y, qweights[i1], scales[i1], biases[i1], lora_a[i1], lora_b[i1])
            h = y + h
        return h
    x = L0_attn_x
    x = x + _L0_attn_ref(_layernorm(x, axis=-1), L0_attn_WQ, L0_attn_WK, L0_attn_WV, L0_attn_WO)
    x = x + _L0_ffn_ref(_layernorm(x, axis=-1), L0_ffn_Wr, L0_ffn_br, L0_ffn_W1, L0_ffn_b1, L0_ffn_W2, L0_ffn_b2)
    x = x + _L1_attn_ref(_layernorm(x, axis=-1), L1_attn_Wq, L1_attn_Wk, L1_attn_Wv, L1_attn_Wo)
    x = x + _L1_ffn_ref(_layernorm(x, axis=-1), L1_ffn_g1, L1_ffn_g2, L1_ffn_Wq, L1_ffn_Wkc, L1_ffn_Wvc, L1_ffn_Wo, L1_ffn_Wr, L1_ffn_expert_bias, L1_ffn_sW1, L1_ffn_sW2, L1_ffn_sW3, L1_ffn_eW1, L1_ffn_eW2, L1_ffn_eW3)
    x = x + _L2_attn_ref(_layernorm(x, axis=-1), L2_attn_wqkv, L2_attn_wo)
    x = x + _L2_ffn_ref(_layernorm(x, axis=-1), L2_ffn_n1_w, L2_ffn_qkv_w, L2_ffn_o_w, L2_ffn_n2_w, L2_ffn_gate_w, L2_ffn_up_w, L2_ffn_down_w)
    x = x + _L3_attn_ref(_layernorm(x, axis=-1), L3_attn_w_qkv, L3_attn_b_qkv, L3_attn_w_out, L3_attn_b_out)
    x = x + _L3_ffn_ref(_layernorm(x, axis=-1), L3_ffn_qweights, L3_ffn_scales, L3_ffn_biases, L3_ffn_lora_a, L3_ffn_lora_b, L3_ffn_ln_gamma, L3_ffn_ln_beta)
    return x

_drawn_inputs = setup_inputs


def setup_inputs(seed=0):
    import zlib

    import numpy as np

    out = dict(_drawn_inputs(seed))
    spreads = {'L0_ffn_br': (0.0, 0.348),
     'L0_ffn_b1': (0.0, 0.8),
     'L0_ffn_b2': (0.0, 0.379),
     'L1_ffn_g1': (1.0, 0.6),
     'L1_ffn_g2': (1.0, 0.6),
     'L1_ffn_expert_bias': (0.0, 0.8),
     'L2_ffn_n1_w': (1.0, 0.6),
     'L2_ffn_n2_w': (1.0, 0.6),
     'L3_attn_b_qkv': (0.0, 0.8),
     'L3_attn_b_out': (0.0, 0.8),
     'L3_ffn_ln_gamma': (1.0, 0.2),
     'L3_ffn_ln_beta': (0.0, 0.1)}
    factors = {'L0_ffn_Wr': 3.181,
     'L0_ffn_W1': 5.323,
     'L0_ffn_W2': 3.896,
     'L1_ffn_Wq': 8.0,
     'L1_ffn_Wkc': 8.0,
     'L1_ffn_Wvc': 8.0,
     'L1_ffn_Wo': 8.0,
     'L1_ffn_Wr': 8.0,
     'L1_ffn_sW1': 8.0,
     'L1_ffn_sW2': 8.0,
     'L1_ffn_sW3': 8.0,
     'L1_ffn_eW1': 8.0,
     'L1_ffn_eW2': 8.0,
     'L1_ffn_eW3': 8.0,
     'L2_ffn_gate_w': 64.0,
     'L3_attn_w_qkv': 8.0,
     'L3_attn_w_out': 6.481,
     'L3_ffn_biases': 6.291,
     'L3_ffn_lora_a': 6.316,
     'L3_ffn_lora_b': 6.516}
    for name, (base, spread) in spreads.items():
        noise = np.random.default_rng([zlib.crc32(name.encode()), seed]).standard_normal(out[name].shape)
        drawn = base * np.exp(spread * noise) if base else spread * noise
        out[name] = jnp.asarray(drawn.astype(out[name].dtype))
    for name, factor in factors.items():
        out[name] = (out[name] * factor).astype(out[name].dtype)
    return out
```

```python
from contextlib import ExitStack

import numpy as np

import concourse.bass as bass
from concourse import mybir

ALU = mybir.AluOpType
ACT = mybir.ActivationFunctionType
F32 = mybir.dt.float32
BF16 = mybir.dt.bfloat16
U32 = mybir.dt.uint32
I32 = mybir.dt.int32
AX = mybir.AxisListType

P = 128
BATCH, SEQ = 16, 256
PAIR = 2
TOK = PAIR * SEQ
TILES = TOK // P
PASSES = BATCH // PAIR
HEADS, HD = 16, 8
GROUPS, QUAD = 4, 32
HPG = HEADS // GROUPS
V1 = HD + 1
EXPERTS = 8
FF0 = 512
CH0 = FF0 // P
CAP = max(1, int(SEQ / EXPERTS * 1.25))
MQH, MQD = 4, 32
MV1 = MQD + 1
NEG = -1.0e30
RANK, QGROUP = 32, 16
LIN_EPS = 1e-5
CLIP = float(np.float32(1.0) - np.float32(1e-7))
CLIP_LO = float(np.float32(-1.0) + np.float32(1e-7))
GEO_POWER = -3.2

CONST = [("ident", P), ("blk8", P), ("esel", GROUPS * P), ("keep_kq", 3 * P), ("mean", P), ("aug", 1),
         ("iota", EXPERTS), ("eps5", 1), ("eps6", 1), ("half", 1), ("one", 1), ("ln1024", 1)]
MASKS = [("mask_qk", 2 * P), ("mask_kq", 3 * P), ("before", P), ("ones", P)]
HEADED = [("q", GROUPS * P), ("k", GROUPS * P), ("v", P), ("o", P)]
STAGES = {
    "masks": MASKS,
    "const": CONST,
    "causal0": HEADED,
    "moe0": [("router", EXPERTS), ("rbias", EXPERTS), ("w1", EXPERTS * FF0), ("b1", EXPERTS * CH0),
             ("w2", EXPERTS * FF0), ("b2", EXPERTS)],
    "causal1": HEADED,
    "mqa": [("g", 1), ("q", P), ("k", P), ("v", MQD), ("o", P)],
    "moe1": [("g", 1), ("router", EXPERTS), ("rbias", EXPERTS), ("w1", (EXPERTS + 1) * P), ("w3", (EXPERTS + 1) * P),
             ("w2", (EXPERTS + 1) * P)],
    "linear": HEADED,
    "causal2": [("g", 1)] + HEADED,
    "mlp": [("g", 1), ("router", EXPERTS), ("up", FF0), ("down", FF0)],
    "arccos": [("q", P), ("k", P), ("v", P), ("o", P), ("bq", 1), ("bk", 1), ("bv", P), ("bo", 1)],
    "qlora": [("bias", 6), ("gamma", 3), ("beta", 3), ("scale", 6 * P), ("la", 6 * P), ("lb", 6 * P)],
}


def columns():
    out, at = {}, 0
    for stage, parts in STAGES.items():
        first, names = at, {}
        for name, width in parts:
            names[name] = (at, width)
            at += width
        out[stage] = (first, at, names)
    return out, at


class Signal:

    def __init__(self, sem, counts, ahead=0):
        self.sem, self.base, self.total, self.ahead = sem, {}, 0, ahead
        for stage in sorted(counts, key=ORDER.index):
            self.base[stage] = self.total
            self.total += counts[stage]

    def at(self, it, stage, n=1):
        return it * self.total + (self.ahead + self.base[stage] + n)


ORDER = ["load", "causal0", "moe0", "causal1", "mqa_in", "mqa", "moe1", "linear", "causal2_in", "causal2", "mlp",
         "arccos", "qlora", "block0_in", "block0", "block1_in", "block1", "block2_in", "block2"]
CAUSAL = ("causal0", "causal1", "causal2")
HEADED_STAGES = ("causal0", "causal1", "linear", "causal2")
NORMS = {
    "causal0": ("x", "xn", True, ("resid", "load")),
    "moe0": ("x", "xn", True, ("resid", "causal0")),
    "causal1": ("x", "xn", True, ("resid", "moe0")),
    "mqa_in": ("x", "z", True, ("resid", "causal1")),
    "mqa": ("z", "xn", False, ("norm", "mqa_in")),
    "moe1": ("z", "xn", False, ("resid", "mqa")),
    "linear": ("x", "xn", True, ("resid", "moe1")),
    "causal2_in": ("x", "z", True, ("resid", "linear")),
    "causal2": ("z", "xn", False, ("norm", "causal2_in")),
    "mlp": ("z", "xn", False, ("resid", "causal2")),
    "arccos": ("x", "xn", True, ("resid", "mlp")),
    "qlora": ("x", "z", True, ("resid", "arccos")),
    "block0": ("y", "xn", True, ("resid", "block0_in")),
    "block1": ("y", "xn", True, ("resid", "block1_in")),
    "block2": ("y", "xn", True, ("resid", "block2_in")),
}
RESID = ["load", "causal0", "moe0", "causal1", "mqa", "moe1", "linear", "causal2", "mlp", "arccos",
         "block0_in", "block0", "block1_in", "block1", "block2_in", "block2"]
ESETS = PAIR * GROUPS * 2
MSETS = PAIR * 3
QSETS = PAIR * 2
ASETS = PAIR * 8
ARC_STEPS = 6


def build(nc, x_dram, w_dram, qw_dram, out_dram):
    cols, width = columns()
    with ExitStack() as ctx:
        def sb(name, shape, dt=F32):
            return ctx.enter_context(nc.sbuf_tensor(name, shape, dt))

        def sem(name):
            return ctx.enter_context(nc.semaphore(name))

        def signal(name, counts, ahead=0):
            return Signal(sem(name), counts, ahead)

        skip = cols["masks"][1]
        wts = sb("wts", [P, width - skip])
        weff = sb("weff", [P, 6 * P])

        def W(stage, name):
            at, n = cols[stage][2][name]
            return wts[:, at - skip:at - skip + n]

        def C(name):
            return W("const", name)

        ident_bf = sb("ident_bf", [P, P], BF16)
        mask_qk = sb("mask_qk", [P, 2 * P], BF16)
        mask_kq = sb("mask_kq", [P, 3 * P], BF16)
        before_bf = sb("before_bf", [P, P], BF16)
        ones_bf = sb("ones_bf", [P, P], BF16)

        xin = sb("xin", [P, TOK])
        buf = {n: sb(n, [P, TOK]) for n in ("x", "z", "xn", "y")}
        x, z, xn, y = (buf[n] for n in ("x", "z", "xn", "y"))
        cen = sb("cen", [P, TOK])
        sq = sb("sq", [P, TOK])
        rstd = sb("rstd", [P, TOK])
        q4 = sb("q4", [P, GROUPS, TOK])
        k4 = sb("k4", [P, GROUPS, TOK])
        v9 = sb("v9", [P, TILES, HEADS, V1])
        v33 = sb("v33", [P, TILES, MV1])
        negm = sb("negm", [P, TILES, GROUPS, P])
        rden = sb("rden", [P, PAIR, 2 * HEADS])
        ytok = sb("ytok", [P, TILES, P])
        yT = y
        vs = sb("vs", [P, PAIR, 2, HEADS, V1])
        nsum = sb("nsum", [P, PAIR, 2, HEADS])
        cosines = sb("cosines", [P, PAIR, 2 * HEADS * SEQ])
        wbc = cosines[:, 0, 0:EXPERTS * TOK].rearrange("p (e t) -> p e t", e=EXPERTS)
        hid = cosines[:, 0, EXPERTS * TOK:].rearrange("p (s c t) -> p s c t", s=2, c=CH0)
        probs = cosines[:, 1, 0:3 * 2 * TOK].rearrange("p (s i t) -> p s i t", s=3, i=2)
        tmp = cosines[:, 1, 4096:4096 + TOK]
        gate = cosines[:, 1, 5120:5120 + 2 * TOK].rearrange("p (s t) -> p s t", s=2)
        masks = cosines[:, 1, 0:skip]
        qint = cosines[:, 0, 0:6 * P].bitcast(I32)

        def M(name):
            at, n = cols["masks"][2][name]
            return masks[:, at:at + n]

        lg = sb("lg", [P, TILES, EXPERTS])
        pr = sb("pr", [P, TILES, EXPERTS])
        t8 = sb("t8", [P, TILES, EXPERTS])
        ix = sb("ix", [P, TILES, EXPERTS], U32)
        ixf = sb("ixf", [P, TILES, EXPERTS])
        oh1 = sb("oh1", [P, TILES, EXPERTS])
        oh2 = sb("oh2", [P, TILES, EXPERTS])
        ohs = sb("ohs", [P, TILES, EXPERTS])
        ohs_bf = sb("ohs_bf", [P, TILES, EXPERTS], BF16)
        wtok = sb("wtok", [P, TILES, EXPERTS])
        s1 = sb("s1", [P, TILES, 1])
        s2 = sb("s2", [P, TILES, 1])
        s3 = sb("s3", [P, TILES, 1])
        s4 = sb("s4", [P, TILES, 1])

        ps = ctx.enter_context(nc.psum_tensor("ps", [P, 8, 512], F32))

        loaded = {s: sem(f"loaded_{s}") for s in STAGES}
        qint_loaded = sem("qint_loaded")
        consts_ready = sem("consts_ready")
        wait_carrier = sem("wait_carrier")
        dequant_step = sem("dequant_step")
        lora_ps = sem("lora_ps")
        weff_ready = sem("weff_ready")
        xin_loaded = sem("xin_loaded")
        out_stored = sem("out_stored")
        LNS = [n for n in NORMS if NORMS[n][2]]
        resid = signal("resid", {r: 1 for r in RESID}, ahead=1)
        norm_mean = signal("norm_mean", {n: 1 for n in LNS})
        norm_cen = signal("norm_cen", {n: 1 for n in LNS})
        norm_sq = signal("norm_sq", {n: 1 for n in NORMS})
        norm_var = signal("norm_var", {n: 1 for n in NORMS})
        norm_ln = signal("norm_ln", {n: 1 for n in NORMS})
        norm_rstd = signal("norm_rstd", {n: 1 for n in NORMS})
        norm_out = signal("norm_out", {n: 1 for n in NORMS})
        qk_ps = signal("qk_ps", {s: 2 * GROUPS for s in HEADED_STAGES} | {"mqa": 2, "arccos": 2 * GROUPS})
        q_ready = signal("q_ready", {s: GROUPS for s in HEADED_STAGES} | {"mqa": 1, "arccos": GROUPS})
        k_ready = signal("k_ready", {s: GROUPS for s in HEADED_STAGES} | {"mqa": 1, "arccos": GROUPS})
        v_ps = signal("v_ps", {s: 1 for s in HEADED_STAGES + ("mqa", "arccos")})
        v_ready = signal("v_ready", {s: 1 for s in HEADED_STAGES + ("mqa", "arccos")})
        max_ps = signal("max_ps", {s: MSETS for s in CAUSAL} | {"mqa": TILES})
        max_done = signal("max_done", {s: MSETS for s in CAUSAL} | {"mqa": TILES})
        negm_ps = signal("negm_ps", {s: 1 for s in CAUSAL + ("mqa",)})
        negm_ready = signal("negm_ready", {s: 1 for s in CAUSAL + ("mqa",)})
        score_ps = signal("score_ps", {s: ESETS for s in HEADED_STAGES} | {"mqa": QSETS, "arccos": ASETS})
        probs_ready = signal("probs_ready", {s: ESETS for s in HEADED_STAGES} | {"mqa": QSETS})
        pv_ps = signal("pv_ps", {s: ESETS for s in HEADED_STAGES} | {"mqa": QSETS, "arccos": PAIR})
        den_step = signal("den_step", {s: 2 * PAIR for s in HEADED_STAGES + ("mqa", "arccos")})
        y_ready = signal("y_ready", {s: PAIR for s in HEADED_STAGES + ("mqa", "arccos")})
        yT_ps = signal("yT_ps", {s: 1 for s in HEADED_STAGES + ("mqa", "arccos")})
        yT_ready = signal("yT_ready", {s: 1 for s in HEADED_STAGES + ("mqa", "arccos")})
        o_ps = signal("o_ps", {s: 1 for s in HEADED_STAGES + ("mqa", "arccos")})
        logits_ps = signal("logits_ps", {s: 1 for s in ("moe0", "moe1", "mlp")})
        route_step = signal("route_step", {"moe0": 18, "moe1": 21, "mlp": 14})
        route_shift = signal("route_shift", {s: 1 for s in ("moe0", "moe1", "mlp")})
        route_exp = signal("route_exp", {s: 1 for s in ("moe0", "moe1", "mlp")})
        gap_ready = signal("gap_ready", {"moe1": 1})
        gap_exp = signal("gap_exp", {"moe1": 1})
        chosen_ready = signal("chosen_ready", {"moe0": 1})
        place_ps = signal("place_ps", {"moe0": 1})
        weight_ready = signal("weight_ready", {s: 1 for s in ("moe0", "moe1", "mlp")})
        wbc_ps = signal("wbc_ps", {"moe0": 2, "moe1": 2, "mlp": 1})
        wbc_lo = signal("wbc_lo", {"moe0": 1, "moe1": 1, "mlp": 1})
        wbc_hi = signal("wbc_hi", {"moe0": 1, "moe1": 1})
        hid_ps = signal("hid_ps", {"moe0": EXPERTS * CH0, "moe1": EXPERTS + 1, "mlp": CH0})
        gate_ready = signal("gate_ready", {"moe1": EXPERTS + 1})
        hid_ready = signal("hid_ready", {"moe0": EXPERTS * CH0, "moe1": EXPERTS + 1, "mlp": CH0})
        ffn_ps = signal("ffn_ps", {"moe0": EXPERTS, "moe1": EXPERTS + 1, "mlp": 1})
        ffn_taken = signal("ffn_taken", {"moe0": EXPERTS, "moe1": EXPERTS + 1, "mlp": 1})
        ffn_added = signal("ffn_added", {"moe0": EXPERTS - 1, "moe1": EXPERTS + 1, "mlp": 1})
        arc_qk_ps = signal("arc_qk_ps", {"arccos": 2})
        arc_raw = signal("arc_raw", {"arccos": 2})
        arc_sq = signal("arc_sq", {"arccos": 2})
        arc_norm_ps = signal("arc_norm_ps", {"arccos": 2})
        arc_floor = signal("arc_floor", {"arccos": 2})
        arc_ln = signal("arc_ln", {"arccos": 2})
        arc_rn = signal("arc_rn", {"arccos": 2})
        arc_unit = signal("arc_unit", {"arccos": 2})
        cos_ready = signal("cos_ready", {"arccos": ASETS})
        arc_pass = signal("arc_pass", {"arccos": PAIR * 2 * ARC_STEPS})
        nsum_step = signal("nsum_step", {"arccos": PAIR * 2 * 3})
        vs_ready = signal("vs_ready", {"arccos": PAIR})
        lin_ps = signal("lin_ps", {f"block{i}": 2 for i in range(3)})
        gelu_ready = signal("gelu_ready", {f"block{i}": 1 for i in range(3)})
        signals = {"resid": resid, "norm": norm_out}

        block = ctx.enter_context(nc.Block())

        def resid_of(stage):
            return z if stage in ("mqa", "causal2") else x

        def norm_pe(pe, it, n):
            src, _, centred, (kind, after) = NORMS[n]
            pe.wait_ge(signals[kind].sem, signals[kind].at(it, after))
            if centred:
                nc.tensor.matmul(ps[:, 0, :], C("mean"), buf[src][:], start=True, stop=True).then_inc(norm_mean.sem, 1)
            pe.wait_ge(norm_sq.sem, norm_sq.at(it, n))
            nc.tensor.matmul(ps[:, 1, :], C("mean"), sq[:], start=True, stop=True).then_inc(norm_var.sem, 1)

        def norm_act(act, it, n, eps):
            src, _, centred, (kind, after) = NORMS[n]
            if centred:
                act.wait_ge(norm_cen.sem, norm_cen.at(it, n))
            else:
                act.wait_ge(signals[kind].sem, signals[kind].at(it, after))
            nc.scalar.activation(sq[:], cen[:] if centred else buf[src][:], ACT.Square).then_inc(norm_sq.sem, 1)
            act.wait_ge(norm_var.sem, norm_var.at(it, n))
            nc.scalar.activation(rstd[:], ps[:, 1, :], ACT.Ln, bias=C(eps)).then_inc(norm_ln.sem, 1)
            act.wait_ge(norm_ln.sem, norm_ln.at(it, n))
            nc.scalar.activation(rstd[:], rstd[:], ACT.Exp, scale=-0.5).then_inc(norm_rstd.sem, 1)

        def norm_dve(dve, it, n, gain=None):
            src, dst, centred, (kind, after) = NORMS[n]
            if centred:
                dve.wait_ge(signals[kind].sem, signals[kind].at(it, after))
                dve.wait_ge(norm_mean.sem, norm_mean.at(it, n))
                nc.vector.tensor_tensor(cen[:], buf[src][:], ps[:, 0, :], ALU.subtract).then_inc(norm_cen.sem, 1)
            dve.wait_ge(norm_rstd.sem, norm_rstd.at(it, n))
            if centred:
                nc.vector.tensor_tensor(buf[dst][:], cen[:], rstd[:], ALU.mult).then_inc(norm_out.sem, 1)
            else:
                nc.vector.scalar_tensor_tensor(out=buf[dst][:], in0=buf[src][:], scalar=gain, in1=rstd[:],
                                               op0=ALU.mult, op1=ALU.mult).then_inc(norm_out.sem, 1)

        def rows(j, n):
            return slice(QUAD * j, QUAD * j + n)

        def eset(e):
            return e // (2 * GROUPS), e // 2 % GROUPS, e % 2

        def headed_project_pe(pe, it, s):
            pe.wait_ge(loaded[s], 16)
            pe.wait_ge(norm_out.sem, norm_out.at(it, s))
            for i, w in enumerate(("q", "k")):
                for g in range(GROUPS):
                    nc.tensor.matmul(ps[:, GROUPS * i + g, :], W(s, w)[:, g * P:(g + 1) * P], xn[:],
                                     start=True, stop=True).then_inc(qk_ps.sem, 1)
            pe.wait_ge(q_ready.sem, q_ready.at(it, s, 1))
            values_pe(s, xn, W(s, "v"), P)

        def values_pe(s, src, w, n):
            for t in range(TILES):
                last = nc.tensor.matmul(ps[:, 0, t * n:(t + 1) * n], src[:, t * P:(t + 1) * P], w,
                                        start=True, stop=True)
            last.then_inc(v_ps.sem, 1)

        def headed_project_act(act, it, s):
            for g in range(GROUPS):
                act.wait_ge(qk_ps.sem, qk_ps.at(it, s, g + 1))
                if s == "linear":
                    nc.scalar.activation(q4[:, g, :], ps[:, g, :], ACT.Relu).then_inc(q_ready.sem, 1)
                else:
                    nc.scalar.activation(q4[:, g, :], ps[:, g, :], ACT.Copy,
                                         scale=float(HD) ** -0.5).then_inc(q_ready.sem, 1)
            act.wait_ge(v_ps.sem, v_ps.at(it, s))
            nc.scalar.activation(v9[:].rearrange("p t h d -> p (t h) d")[:, :, 0:HD],
                                 ps[:, 0, :].rearrange("p (h d) -> p h d", d=HD), ACT.Copy).then_inc(v_ready.sem, 1)

        def headed_project_dve(dve, it, s):
            for g in range(GROUPS):
                dve.wait_ge(qk_ps.sem, qk_ps.at(it, s, GROUPS + g + 1))
                if s == "linear":
                    nc.vector.tensor_scalar(k4[:, g, :], ps[:, GROUPS + g, :], 0.0, None, ALU.max)\
                        .then_inc(k_ready.sem, 1)
                else:
                    nc.vector.tensor_scalar(k4[:, g, :], ps[:, GROUPS + g, :], C("aug"), None, ALU.add)\
                        .then_inc(k_ready.sem, 1)

        def qkv_wait_pe(pe, it, s):
            pe.wait_ge(q_ready.sem, q_ready.at(it, s, GROUPS))
            pe.wait_ge(k_ready.sem, k_ready.at(it, s, GROUPS))
            pe.wait_ge(v_ready.sem, v_ready.at(it, s))

        def mset(m):
            b, part = m // 3, m % 3
            return (b, 0, P, 0, GROUPS) if part == 0 else (b, 1, SEQ, 2 * (part - 1), 2)

        def max_pe(pe, it, s):
            for m in range(MSETS):
                b, qt, keys, g0, ng = mset(m)
                base = HPG * (m % 2)
                if m >= 2:
                    pe.wait_ge(max_done.sem, max_done.at(it, s, m - 1))
                mask = mask_qk[:, 2 * P - keys:2 * P]
                for j in range(HPG):
                    nc.tensor.matmul(ps[:, base + j, :].rearrange("p (g k) -> p g k", k=keys), ident_bf[:],
                                     mask.unsqueeze(1).broadcast_to([P, ng, keys]),
                                     start=True, stop=False, skip_group_check=True)
                for gi in range(ng):
                    for j in range(HPG):
                        last = nc.tensor.matmul(
                            ps[:, base + j, gi * keys:(gi + 1) * keys],
                            q4[rows(j, HD), g0 + gi, b * SEQ + qt * P:b * SEQ + (qt + 1) * P],
                            k4[rows(j, HD), g0 + gi, b * SEQ:b * SEQ + keys],
                            start=False, stop=True, skip_group_check=True)
                last.then_inc(max_ps.sem, 1)
            pe.wait_ge(max_done.sem, max_done.at(it, s, MSETS))
            for g in range(GROUPS):
                for t in range(TILES):
                    last = nc.tensor.transpose(ps[:, g, t * P:(t + 1) * P], negm[:, t, g, :], C("ident"))
            last.then_inc(negm_ps.sem, 1)

        def max_dve(dve, it, s):
            for m in range(MSETS):
                b, qt, keys, g0, ng = mset(m)
                base = HPG * (m % 2)
                dve.wait_ge(max_ps.sem, max_ps.at(it, s, m + 1))
                into = negm[:, 2 * b + qt, g0:g0 + ng, :].rearrange("p g (j r) -> p j g r", r=QUAD)[:, :, :, HD]
                nc.vector.tensor_reduce(into, ps[:, base:base + HPG, :].rearrange("p j (g k) -> p j g k", k=keys),
                                        AX.X, ALU.max, negate=True).then_inc(max_done.sem, 1)
            dve.wait_ge(negm_ps.sem, negm_ps.at(it, s))
            dve.wait_ge(q_ready.sem, q_ready.at(it, s, GROUPS))
            nc.vector.tensor_tensor(q4[:], q4[:], ps[:, 0:GROUPS, :], ALU.add).then_inc(negm_ready.sem, 1)

        def headed_scores_pe(pe, it, s):
            if s in CAUSAL:
                pe.wait_ge(negm_ready.sem, negm_ready.at(it, s))
            kr = HD + 1 if s in CAUSAL else HD
            for e in range(ESETS + 2):
                if e < ESETS:
                    b, g, jp = eset(e)
                    bank = 2 * (e % 3)
                    if e >= 3:
                        pe.wait_ge(probs_ready.sem, probs_ready.at(it, s, e - 2))
                    if s in CAUSAL:
                        for i in range(2):
                            nc.tensor.matmul(ps[:, bank + i, 0:3 * P], ident_bf[:], mask_kq[:],
                                             start=True, stop=False, skip_group_check=True)
                    for kt in range(2):
                        for i in range(2):
                            r = rows(2 * jp + i, kr)
                            at = b * SEQ + kt * P
                            last = nc.tensor.matmul(
                                ps[:, bank + i, 2 * kt * P:(2 + kt) * P],
                                k4[r, g, at:at + P], q4[r, g, at:(b + 1) * SEQ],
                                start=s not in CAUSAL, stop=True, skip_group_check=True)
                    last.then_inc(score_ps.sem, 1)
                if e >= 2:
                    headed_pv_pe(pe, it, s, e - 2)

        def headed_pv_pe(pe, it, s, e):
            b, g, jp = eset(e)
            pe.wait_ge(probs_ready.sem, probs_ready.at(it, s, e + 1))
            for i in range(2):
                h = HPG * g + 2 * jp + i
                pw = probs[:, e % 3, i, :]
                for qt in range(2):
                    o = ps[:, 6 + b, (qt * HEADS + h) * V1:(qt * HEADS + h + 1) * V1]
                    for kt in range(qt + 1):
                        c = (qt + kt) * P
                        last = nc.tensor.matmul(o, pw[:, c:c + P], v9[:, 2 * b + kt, h, :], start=(kt == 0),
                                                stop=(kt == qt), skip_group_check=True)
            last.then_inc(pv_ps.sem, 1)

        def headed_exp_act(act, it, s):
            for e in range(ESETS):
                act.wait_ge(score_ps.sem, score_ps.at(it, s, e + 1))
                if e >= 3:
                    act.wait_ge(pv_ps.sem, pv_ps.at(it, s, e - 2))
                bank = 2 * (e % 3)
                nc.scalar.activation(probs[:, e % 3, :, 0:3 * P], ps[:, bank:bank + 2, 0:3 * P], ACT.Exp)\
                    .then_inc(probs_ready.sem, 1)

        def linear_mask_dve(dve, it, s):
            keep = C("keep_kq").unsqueeze(1).broadcast_to([P, 2, 3 * P])
            for e in range(ESETS):
                dve.wait_ge(score_ps.sem, score_ps.at(it, s, e + 1))
                if e >= 3:
                    dve.wait_ge(pv_ps.sem, pv_ps.at(it, s, e - 2))
                bank = 2 * (e % 3)
                nc.vector.tensor_tensor(probs[:, e % 3, :, 0:3 * P], ps[:, bank:bank + 2, 0:3 * P], keep, ALU.mult)\
                    .then_inc(probs_ready.sem, 1)
                if e == ESETS // 2 + 2:
                    headed_norm_dve(dve, it, s, 0)

        def headed_norm_dve(dve, it, s, b):
            n = {"arccos": 1}.get(s, ESETS // PAIR)
            dve.wait_ge(pv_ps.sem, pv_ps.at(it, s, n * (b + 1)))
            o = ps[:, 6 + b, 0:2 * HEADS * V1].rearrange("p (h d) -> p h d", d=V1)
            r = rden[:, b, :].unsqueeze(2)
            if s == "linear":
                nc.vector.tensor_scalar(r, o[:, :, HD:V1], LIN_EPS, None, ALU.add).then_inc(den_step.sem, 1)
            else:
                nc.vector.tensor_copy(r, o[:, :, HD:V1]).then_inc(den_step.sem, 1)
            dve.wait_ge(den_step.sem, den_step.at(it, s, 2 * b + 1))
            nc.vector.reciprocal(r, r).then_inc(den_step.sem, 1)
            dve.wait_ge(den_step.sem, den_step.at(it, s, 2 * b + 2))
            nc.vector.tensor_tensor(ytok[:, 2 * b:2 * b + 2, :].rearrange("p t (h d) -> p (t h) d", d=HD),
                                    o[:, :, 0:HD], r.broadcast_to([P, 2 * HEADS, HD]), ALU.mult)\
                .then_inc(y_ready.sem, 1)

        def attn_out_pe(pe, it, s):
            pe.wait_ge(y_ready.sem, y_ready.at(it, s, PAIR))
            for t in range(TILES):
                last = nc.tensor.transpose(ps[:, 0, t * P:(t + 1) * P], ytok[:, t, :], C("ident"))
            last.then_inc(yT_ps.sem, 1)
            pe.wait_ge(yT_ready.sem, yT_ready.at(it, s))
            nc.tensor.matmul(ps[:, 1, :], W(s, "o"), yT[:], start=True, stop=True).then_inc(o_ps.sem, 1)

        def attn_out_act(act, it, s):
            act.wait_ge(yT_ps.sem, yT_ps.at(it, s))
            nc.scalar.activation(yT[:], ps[:, 0, :], ACT.Copy).then_inc(yT_ready.sem, 1)

        def attn_out_dve(dve, it, s):
            dve.wait_ge(o_ps.sem, o_ps.at(it, s))
            r = resid_of(s)
            if s == "arccos":
                nc.vector.scalar_tensor_tensor(out=r[:], in0=ps[:, 1, :], scalar=W(s, "bo"), in1=r[:],
                                               op0=ALU.add, op1=ALU.add).then_inc(resid.sem, 1)
            else:
                nc.vector.tensor_tensor(r[:], r[:], ps[:, 1, :], ALU.add).then_inc(resid.sem, 1)

        def headed_pe(pe, it, s):
            headed_project_pe(pe, it, s)
            qkv_wait_pe(pe, it, s)
            if s in CAUSAL:
                max_pe(pe, it, s)
            headed_scores_pe(pe, it, s)
            attn_out_pe(pe, it, s)

        def headed_act(act, it, s):
            headed_project_act(act, it, s)
            if s in CAUSAL:
                headed_exp_act(act, it, s)
            attn_out_act(act, it, s)

        def headed_dve(dve, it, s):
            headed_project_dve(dve, it, s)
            if s in CAUSAL:
                max_dve(dve, it, s)
                headed_norm_dve(dve, it, s, 0)
            else:
                linear_mask_dve(dve, it, s)
            headed_norm_dve(dve, it, s, 1)
            attn_out_dve(dve, it, s)

        def mqa_pe(pe, it):
            s = "mqa"
            pe.wait_ge(loaded[s], 16)
            pe.wait_ge(norm_out.sem, norm_out.at(it, s))
            nc.tensor.matmul(ps[:, 2, :], W(s, "q"), xn[:], start=True, stop=True).then_inc(qk_ps.sem, 1)
            nc.tensor.matmul(ps[:, 3, :], W(s, "k"), xn[:], start=True, stop=True).then_inc(qk_ps.sem, 1)
            values_pe(s, xn, W(s, "v"), MQD)
            pe.wait_ge(q_ready.sem, q_ready.at(it, s))
            pe.wait_ge(k_ready.sem, k_ready.at(it, s))
            pe.wait_ge(v_ready.sem, v_ready.at(it, s))
            for m in range(TILES):
                if m >= 2:
                    pe.wait_ge(max_done.sem, max_done.at(it, s, m - 1))
                for j in range(MQH):
                    last = nc.tensor.matmul(ps[:, MQH * (m % 2) + j, 0:SEQ], q4[rows(j, MQD), 0, m * P:(m + 1) * P],
                                            k4[rows(j, MQD), 0, m // 2 * SEQ:(m // 2 + 1) * SEQ],
                                            start=True, stop=True)
                last.then_inc(max_ps.sem, 1)
            pe.wait_ge(max_done.sem, max_done.at(it, s, TILES))
            for t in range(TILES):
                last = nc.tensor.transpose(ps[:, 0, t * P:(t + 1) * P], negm[:, t, 0, :], C("ident"))
            last.then_inc(negm_ps.sem, 1)
            pe.wait_ge(negm_ready.sem, negm_ready.at(it, s))
            for e in range(QSETS + 1):
                if e < QSETS:
                    b, jp = e // 2, e % 2
                    bank = 2 * (e % 3)
                    if e >= 3:
                        pe.wait_ge(probs_ready.sem, probs_ready.at(it, s, e - 2))
                    for kt in range(2):
                        for i in range(2):
                            j = 2 * jp + i
                            o = ps[:, bank + i, kt * SEQ:(kt + 1) * SEQ]
                            qs = slice(b * SEQ, (b + 1) * SEQ)
                            nc.tensor.matmul(o, k4[rows(j, MQD), 0, b * SEQ + kt * P:b * SEQ + (kt + 1) * P],
                                             q4[rows(j, MQD), 0, qs], start=True, stop=False, skip_group_check=True)
                            last = nc.tensor.matmul(o, C("aug")[rows(j, MQD), :].broadcast_to([MQD, P]), q4[rows(j, MQD), 1, qs],
                                                    start=False, stop=True, skip_group_check=True)
                    last.then_inc(score_ps.sem, 1)
                if e >= 1:
                    b, jp = (e - 1) // 2, (e - 1) % 2
                    pe.wait_ge(probs_ready.sem, probs_ready.at(it, s, e))
                    for i in range(2):
                        for qt in range(2):
                            c = (qt * MQH + 2 * jp + i) * MV1
                            for kt in range(2):
                                w = kt * SEQ + qt * P
                                last = nc.tensor.matmul(ps[:, 6 + b, c:c + MV1], probs[:, (e - 1) % 3, i, w:w + P],
                                                        v33[:, 2 * b + kt, :], start=(kt == 0), stop=(kt == 1),
                                                        skip_group_check=True)
                    last.then_inc(pv_ps.sem, 1)
            attn_out_pe(pe, it, s)

        def mqa_act(act, it):
            s = "mqa"
            act.wait_ge(qk_ps.sem, qk_ps.at(it, s, 1))
            nc.scalar.activation(q4[:, 0, :], ps[:, 2, :], ACT.Copy, scale=float(MQD) ** -0.5).then_inc(q_ready.sem, 1)
            act.wait_ge(v_ps.sem, v_ps.at(it, s))
            nc.scalar.activation(v33[:, :, 0:MQD], ps[:, 0, 0:TILES * MQD].rearrange("p (t d) -> p t d", d=MQD),
                                 ACT.Copy).then_inc(v_ready.sem, 1)
            for e in range(QSETS):
                act.wait_ge(score_ps.sem, score_ps.at(it, s, e + 1))
                if e >= 3:
                    act.wait_ge(pv_ps.sem, pv_ps.at(it, s, e - 2))
                bank = 2 * (e % 3)
                nc.scalar.activation(probs[:, e % 3, :, :], ps[:, bank:bank + 2, :], ACT.Exp)\
                    .then_inc(probs_ready.sem, 1)
            attn_out_act(act, it, s)

        def mqa_dve(dve, it):
            s = "mqa"
            dve.wait_ge(qk_ps.sem, qk_ps.at(it, s, 2))
            nc.vector.tensor_copy(k4[:, 0, :], ps[:, 3, :]).then_inc(k_ready.sem, 1)
            for m in range(TILES):
                dve.wait_ge(max_ps.sem, max_ps.at(it, s, m + 1))
                base = MQH * (m % 2)
                nc.vector.tensor_reduce(negm[:, m, 0, :].rearrange("p (j r) -> p j r", r=QUAD)[:, :, HD],
                                        ps[:, base:base + MQH, 0:SEQ], AX.X, ALU.max, negate=True)\
                    .then_inc(max_done.sem, 1)
            dve.wait_ge(negm_ps.sem, negm_ps.at(it, s))
            nc.vector.tensor_copy(q4[:, 1, :], ps[:, 0, :]).then_inc(negm_ready.sem, 1)
            for b in range(PAIR):
                dve.wait_ge(pv_ps.sem, pv_ps.at(it, s, 2 * (b + 1)))
                o = ps[:, 6 + b, 0:2 * MQH * MV1].rearrange("p (h d) -> p h d", d=MV1)
                r = rden[:, b, 0:2 * MQH].unsqueeze(2)
                nc.vector.tensor_copy(r, o[:, :, MQD:MV1]).then_inc(den_step.sem, 1)
                dve.wait_ge(den_step.sem, den_step.at(it, s, 2 * b + 1))
                nc.vector.reciprocal(r, r).then_inc(den_step.sem, 1)
                dve.wait_ge(den_step.sem, den_step.at(it, s, 2 * b + 2))
                nc.vector.tensor_tensor(ytok[:, 2 * b:2 * b + 2, :].rearrange("p t (h d) -> p (t h) d", d=MQD),
                                        o[:, :, 0:MQD], r.broadcast_to([P, 2 * MQH, MQD]), ALU.mult)\
                    .then_inc(y_ready.sem, 1)
            attn_out_dve(dve, it, s)

        def aset(a):
            return a // 8, a // 4 % 2, 2 * (a // 2 % 2), a % 2

        def arccos_pe(pe, it):
            s = "arccos"
            pe.wait_ge(loaded[s], 16)
            pe.wait_ge(norm_out.sem, norm_out.at(it, s))
            for i, w in enumerate(("q", "k")):
                nc.tensor.matmul(ps[:, 2 + i, :], W(s, w), xn[:], start=True, stop=True).then_inc(arc_qk_ps.sem, 1)
            values_pe(s, xn, W(s, "v"), P)
            for i in range(2):
                pe.wait_ge(arc_sq.sem, arc_sq.at(it, s, i + 1))
                nc.tensor.matmul(ps[:, 4 + i, :], C("blk8"), sq[:] if i == 0 else cen[:], start=True, stop=True)\
                    .then_inc(arc_norm_ps.sem, 1)
            pe.wait_ge(v_ready.sem, v_ready.at(it, s))
            for i in range(2):
                pe.wait_ge(arc_unit.sem, arc_unit.at(it, s, i + 1))
                for g in range(GROUPS):
                    nc.tensor.matmul(ps[:, GROUPS * i + g, :], C("esel")[:, g * P:(g + 1) * P],
                                     y[:] if i == 0 else z[:], start=True, stop=True).then_inc(qk_ps.sem, 1)
            pe.wait_ge(q_ready.sem, q_ready.at(it, s, GROUPS))
            pe.wait_ge(k_ready.sem, k_ready.at(it, s, GROUPS))
            for a in range(ASETS):
                b, kt, g0, jp = aset(a)
                bank = 2 * (a % 3)
                if a >= 3:
                    pe.wait_ge(cos_ready.sem, cos_ready.at(it, s, a - 2))
                for g2 in range(2):
                    for i in range(2):
                        r = rows(2 * jp + i, HD)
                        last = nc.tensor.matmul(
                            ps[:, bank + i, g2 * SEQ:(g2 + 1) * SEQ],
                            k4[r, g0 + g2, b * SEQ + kt * P:b * SEQ + (kt + 1) * P],
                            q4[r, g0 + g2, b * SEQ:(b + 1) * SEQ], start=True, stop=True, skip_group_check=True)
                last.then_inc(score_ps.sem, 1)
            for b in range(PAIR):
                pe.wait_ge(vs_ready.sem, vs_ready.at(it, s, b + 1))
                for h in range(HEADS):
                    gp, g2, jp, i = h // 8, h // 4 % 2, h // 2 % 2, h % 2
                    slot = gp * 8 + jp * 4 + i * 2 + g2
                    for qt in range(2):
                        c = (qt * HEADS + h) * V1
                        for kt in range(2):
                            w = (kt * HEADS + slot) * SEQ + qt * P
                            last = nc.tensor.matmul(ps[:, 6 + b, c:c + V1], cosines[:, b, w:w + P], vs[:, b, kt, h, :],
                                                    start=(kt == 0), stop=(kt == 1), skip_group_check=True)
                last.then_inc(pv_ps.sem, 1)
            attn_out_pe(pe, it, s)

        def arccos_act(act, it):
            s = "arccos"
            for i, (bias, raw, square) in enumerate((("bq", y, sq), ("bk", z, cen))):
                act.wait_ge(arc_qk_ps.sem, arc_qk_ps.at(it, s, i + 1))
                nc.scalar.activation(raw[:], ps[:, 2 + i, :], ACT.Identity, bias=W(s, bias)).then_inc(arc_raw.sem, 1)
                act.wait_ge(arc_raw.sem, arc_raw.at(it, s, i + 1))
                nc.scalar.activation(square[:], raw[:], ACT.Square).then_inc(arc_sq.sem, 1)
            for i in range(2):
                act.wait_ge(arc_floor.sem, arc_floor.at(it, s, i + 1))
                rn = rstd if i == 0 else xn
                nc.scalar.activation(rn[:], rn[:], ACT.Ln, scale=float(2 ** 20)).then_inc(arc_ln.sem, 1)
                act.wait_ge(arc_ln.sem, arc_ln.at(it, s, i + 1))
                nc.scalar.activation(rn[:], rn[:], ACT.Exp, scale=-0.5, bias=C("ln1024")).then_inc(arc_rn.sem, 1)
            for g in range(GROUPS):
                act.wait_ge(qk_ps.sem, qk_ps.at(it, s, g + 1))
                nc.scalar.activation(q4[:, g, :], ps[:, g, :], ACT.Copy).then_inc(q_ready.sem, 1)
            for b in range(PAIR):
                halves = [cosines[:, b, kt * HEADS * SEQ:(kt + 1) * HEADS * SEQ] for kt in range(2)]
                steps = [(ACT.Ln, 0.5, C("half")), (ACT.Tanh, -0.25, None), (ACT.Sqrt, 1.0, None),
                         (ACT.Arctan, 1.0, None), (ACT.Ln, 4.0, C("one")), (ACT.Exp, GEO_POWER, None)]
                for n, (func, scale, bias) in enumerate(steps):
                    for kt in range(2):
                        k = (b * ARC_STEPS + n) * 2 + kt
                        if n == 0:
                            act.wait_ge(cos_ready.sem, cos_ready.at(it, s, 8 * b + 4 * kt + 4))
                        else:
                            act.wait_ge(arc_pass.sem, arc_pass.at(it, s, k - 1))
                        if bias is None:
                            ins = nc.scalar.activation(halves[kt], halves[kt], func, scale=scale)
                        else:
                            ins = nc.scalar.activation(halves[kt], halves[kt], func, scale=scale, bias=bias)
                        ins.then_inc(arc_pass.sem, 1)
            attn_out_act(act, it, s)

        def arccos_dve(dve, it):
            s = "arccos"
            dve.wait_ge(v_ps.sem, v_ps.at(it, s))
            nc.vector.tensor_tensor(v9[:, :, :, 0:HD].rearrange("p t h d -> p (t h) d"),
                                    ps[:, 0, :].rearrange("p (h d) -> p h d", d=HD),
                                    W(s, "bv").unsqueeze(1).broadcast_to([P, TILES, P])
                                    .rearrange("p t (h d) -> p t h d", d=HD), ALU.add).then_inc(v_ready.sem, 1)
            for i in range(2):
                dve.wait_ge(arc_norm_ps.sem, arc_norm_ps.at(it, s, i + 1))
                rn = rstd if i == 0 else xn
                nc.vector.tensor_scalar(rn[:], ps[:, 4 + i, :], 1e-24, None, ALU.max).then_inc(arc_floor.sem, 1)
            for i, raw in enumerate((y, z)):
                dve.wait_ge(arc_rn.sem, arc_rn.at(it, s, i + 1))
                rn = rstd if i == 0 else xn
                nc.vector.tensor_tensor(raw[:], raw[:], rn[:], ALU.mult).then_inc(arc_unit.sem, 1)
            for g in range(GROUPS):
                dve.wait_ge(qk_ps.sem, qk_ps.at(it, s, GROUPS + g + 1))
                nc.vector.tensor_copy(k4[:, g, :], ps[:, GROUPS + g, :]).then_inc(k_ready.sem, 1)
            for a in range(ASETS):
                b = a // 8
                dve.wait_ge(score_ps.sem, score_ps.at(it, s, a + 1))
                bank = 2 * (a % 3)
                nc.vector.tensor_scalar(cosines[:, b, (a % 8) * 1024:(a % 8 + 1) * 1024].rearrange(
                    "p (i t) -> p i t", i=2), ps[:, bank:bank + 2, :], CLIP, CLIP_LO, ALU.min, ALU.max)\
                    .then_inc(cos_ready.sem, 1)
            for b in range(PAIR):
                for kt in range(2):
                    n = (2 * b + kt) * 3
                    dve.wait_ge(arc_pass.sem, arc_pass.at(it, s, (b * ARC_STEPS + ARC_STEPS - 1) * 2 + kt + 1))
                    for gp in range(2):
                        at = (kt * HEADS + 8 * gp) * SEQ
                        nc.vector.tensor_reduce(
                            nsum[:, b, kt, 8 * gp:8 * gp + 8].rearrange("p (g2 ji) -> p ji g2", g2=2),
                            cosines[:, b, at:at + 8 * SEQ].rearrange("p (ji g2 q) -> p ji g2 q", g2=2, q=SEQ),
                            AX.X, ALU.add).then_inc(nsum_step.sem, 1)
                    dve.wait_ge(nsum_step.sem, nsum_step.at(it, s, n + 2))
                    nc.vector.reciprocal(nsum[:, b, kt, :], nsum[:, b, kt, :]).then_inc(nsum_step.sem, 1)
                    dve.wait_ge(nsum_step.sem, nsum_step.at(it, s, n + 3))
                    dve.wait_ge(v_ready.sem, v_ready.at(it, s))
                    last = nc.vector.tensor_tensor(vs[:, b, kt, :, :], v9[:, 2 * b + kt, :, :],
                                                   nsum[:, b, kt, :].unsqueeze(2).broadcast_to([P, HEADS, V1]),
                                                   ALU.mult)
                last.then_inc(vs_ready.sem, 1)
            for b in range(PAIR):
                headed_norm_dve(dve, it, s, b)
            attn_out_dve(dve, it, s)

        def router_pe(pe, it, s):
            pe.wait_ge(norm_out.sem, norm_out.at(it, s))
            pe.wait_ge(loaded[s], 16)
            for t in range(TILES):
                last = nc.tensor.matmul(ps[:, 0, t * EXPERTS:(t + 1) * EXPERTS], xn[:, t * P:(t + 1) * P],
                                        W(s, "router"), start=True, stop=True)
            last.then_inc(logits_ps.sem, 1)
            if s == "moe0":
                pe.wait_ge(chosen_ready.sem, chosen_ready.at(it, s))
                for t in range(TILES):
                    o = ps[:, 1, t * EXPERTS:(t + 1) * EXPERTS]
                    last = nc.tensor.matmul(o, before_bf[:], ohs_bf[:, t, :], start=True, stop=(t % 2 == 0),
                                            skip_group_check=True)
                    if t % 2:
                        last = nc.tensor.matmul(o, ones_bf[:], ohs_bf[:, t - 1, :], start=False, stop=True,
                                                skip_group_check=True)
                last.then_inc(place_ps.sem, 1)
            pe.wait_ge(weight_ready.sem, weight_ready.at(it, s))
            n = 1 if s == "mlp" else EXPERTS
            for e in range(n):
                for t in range(TILES):
                    last = nc.tensor.matmul(ps[:, (e if n > 1 else 5), t * P:(t + 1) * P],
                                            wtok[:, t, e:e + 1].broadcast_to([P, P]), C("ident"),
                                            start=True, stop=True)
                if e in (EXPERTS // 2 - 1, n - 1):
                    last.then_inc(wbc_ps.sem, 1)

        def router_act(act, it, s):
            act.wait_ge(route_shift.sem, route_shift.at(it, s))
            nc.scalar.activation(pr[:], lg[:], ACT.Exp).then_inc(route_exp.sem, 1)
            if s == "moe1":
                act.wait_ge(gap_ready.sem, gap_ready.at(it, s))
                nc.scalar.activation(s2[:], s1[:], ACT.Exp).then_inc(gap_exp.sem, 1)
            act.wait_ge(wbc_ps.sem, wbc_ps.at(it, s))
            if s == "mlp":
                nc.scalar.activation(wbc[:, 0, :], ps[:, 5, :], ACT.Copy).then_inc(wbc_lo.sem, 1)
            else:
                nc.scalar.activation(wbc[:, 0:4, :], ps[:, 0:4, :], ACT.Copy).then_inc(wbc_lo.sem, 1)

        def router_dve(dve, it, s):
            n = 0

            def step(ins, then_max=False):
                nonlocal n
                n += 1
                ins.then_inc(route_step.sem, 1)
                dve.wait_ge(route_step.sem, route_step.at(it, s, n))
                if then_max:
                    dve.sem_inc(wait_carrier)

            full = [P, TILES, EXPERTS]
            dve.wait_ge(logits_ps.sem, logits_ps.at(it, s))
            logits = ps[:, 0, 0:TILES * EXPERTS].rearrange("p (t e) -> p t e", e=EXPERTS)
            if s == "mlp":
                step(nc.vector.tensor_copy(lg[:], logits))
            else:
                step(nc.vector.tensor_tensor(lg[:], logits, W(s, "rbias").unsqueeze(1).broadcast_to(full), ALU.add))
            step(nc.vector.tensor_reduce(s1[:], lg[:], AX.X, ALU.max, negate=True))
            nc.vector.tensor_tensor(lg[:], lg[:], s1[:].broadcast_to(full), ALU.add).then_inc(route_shift.sem, 1)
            dve.wait_ge(route_exp.sem, route_exp.at(it, s))
            step(nc.vector.tensor_reduce(s1[:], pr[:], AX.X, ALU.add))
            step(nc.vector.reciprocal(s2[:], s1[:]))
            step(nc.vector.tensor_tensor(pr[:], pr[:], s2[:].broadcast_to(full), ALU.mult), then_max=True)
            for t in range(TILES):
                nc.vector.max(t8[:, t, :], pr[:, t, :]).then_inc(route_step.sem, 1)
            n += TILES
            dve.wait_ge(route_step.sem, route_step.at(it, s, n))
            dve.sem_inc(wait_carrier)
            first, second = t8[:, :, 0:1], t8[:, :, 1:2]
            if s == "mlp":
                step(nc.vector.tensor_tensor(s1[:], first, second, ALU.add))
                step(nc.vector.tensor_scalar(s2[:], s1[:], 1e-9, None, ALU.add))
                step(nc.vector.reciprocal(s3[:], s2[:]))
                step(nc.vector.tensor_tensor(s4[:], first, s3[:], ALU.mult))
                step(nc.vector.tensor_tensor(s2[:], second, s3[:], ALU.mult))
                nc.vector.tensor_tensor(wtok[:, :, 0:1], s4[:], s2[:], ALU.add).then_inc(weight_ready.sem, 1)
                return
            for t in range(TILES):
                nc.vector.max_index(ix[:, t, :], t8[:, t, :], pr[:, t, :]).then_inc(route_step.sem, 1)
            n += TILES
            dve.wait_ge(route_step.sem, route_step.at(it, s, n))
            step(nc.vector.tensor_copy(ixf[:], ix[:]))
            iota = C("iota").unsqueeze(1).broadcast_to(full)
            step(nc.vector.tensor_tensor(oh1[:], iota, ixf[:, :, 0:1].broadcast_to(full), ALU.is_equal))
            step(nc.vector.tensor_tensor(oh2[:], iota, ixf[:, :, 1:2].broadcast_to(full), ALU.is_equal))
            if s == "moe0":
                step(nc.vector.tensor_tensor(ohs[:], oh1[:], oh2[:], ALU.add))
                nc.vector.tensor_copy(ohs_bf[:], ohs[:]).then_inc(chosen_ready.sem, 1)
                step(nc.vector.tensor_tensor(wtok[:], ohs[:], pr[:], ALU.mult))
                dve.wait_ge(place_ps.sem, place_ps.at(it, s))
                place = ps[:, 1, 0:TILES * EXPERTS].rearrange("p (t e) -> p t e", e=EXPERTS)
                nc.vector.scalar_tensor_tensor(out=wtok[:], in0=place, scalar=float(CAP), in1=wtok[:],
                                               op0=ALU.is_lt, op1=ALU.mult).then_inc(weight_ready.sem, 1)
            else:
                nc.vector.tensor_tensor(s1[:], second, first, ALU.subtract).then_inc(gap_ready.sem, 1)
                dve.wait_ge(gap_exp.sem, gap_exp.at(it, s))
                step(nc.vector.tensor_scalar(s3[:], s2[:], 1.0, None, ALU.add))
                step(nc.vector.reciprocal(s1[:], s3[:]))
                step(nc.vector.tensor_tensor(s4[:], s2[:], s1[:], ALU.mult))
                step(nc.vector.tensor_tensor(oh1[:], oh1[:], s1[:].broadcast_to(full), ALU.mult))
                step(nc.vector.tensor_tensor(oh2[:], oh2[:], s4[:].broadcast_to(full), ALU.mult))
                nc.vector.tensor_tensor(wtok[:], oh1[:], oh2[:], ALU.add).then_inc(weight_ready.sem, 1)

        def wbc_dve(dve, it, s):
            dve.wait_ge(wbc_ps.sem, wbc_ps.at(it, s, 2))
            nc.vector.tensor_copy(wbc[:, 4:8, :], ps[:, 4:8, :]).then_inc(wbc_hi.sem, 1)

        def moe0_pe(pe, it):
            s = "moe0"
            router_pe(pe, it, s)
            pe.wait_ge(wbc_lo.sem, wbc_lo.at(it, s))
            pe.wait_ge(wbc_hi.sem, wbc_hi.at(it, s))
            w1, w2 = W(s, "w1"), W(s, "w2")
            for e in range(EXPERTS + 1):
                if e < EXPERTS:
                    for c in range(CH0):
                        k = e * CH0 + c
                        if e >= 1:
                            pe.wait_ge(hid_ready.sem, hid_ready.at(it, s, k - CH0 + 1))
                        nc.tensor.matmul(ps[:, c, :], w1[:, k * P:(k + 1) * P], xn[:], start=True, stop=True)\
                            .then_inc(hid_ps.sem, 1)
                if e >= 1:
                    if e >= 3:
                        pe.wait_ge(ffn_taken.sem, ffn_taken.at(it, s, e - 2))
                    for c in range(CH0):
                        k = (e - 1) * CH0 + c
                        pe.wait_ge(hid_ready.sem, hid_ready.at(it, s, k + 1))
                        last = nc.tensor.matmul(ps[:, 4 + (e - 1) % 2, :], w2[:, k * P:(k + 1) * P],
                                                hid[:, (e - 1) % 2, c, :], start=(c == 0), stop=(c == CH0 - 1))
                    last.then_inc(ffn_ps.sem, 1)

        def moe0_act(act, it):
            s = "moe0"
            router_act(act, it, s)
            for k in range(EXPERTS * CH0):
                e, c = k // CH0, k % CH0
                act.wait_ge(hid_ps.sem, hid_ps.at(it, s, k + 1))
                if e >= 2:
                    act.wait_ge(ffn_ps.sem, ffn_ps.at(it, s, e - 1))
                nc.scalar.activation(hid[:, e % 2, c, :], ps[:, c, :], ACT.Relu, bias=W(s, "b1")[:, k:k + 1])\
                    .then_inc(hid_ready.sem, 1)

        def moe0_dve(dve, it):
            s = "moe0"
            router_dve(dve, it, s)
            wbc_dve(dve, it, s)
            dve.wait_ge(wbc_lo.sem, wbc_lo.at(it, s))
            dve.wait_ge(wbc_hi.sem, wbc_hi.at(it, s))
            for e in range(EXPERTS):
                dve.wait_ge(ffn_ps.sem, ffn_ps.at(it, s, e + 1))
                if e >= 1:
                    dve.wait_ge(ffn_added.sem, ffn_added.at(it, s, e))
                nc.vector.scalar_tensor_tensor(out=tmp, in0=ps[:, 4 + e % 2, :], scalar=W(s, "b2")[:, e:e + 1],
                                               in1=wbc[:, e, :], op0=ALU.add, op1=ALU.mult).then_inc(ffn_taken.sem, 1)
                dve.wait_ge(ffn_taken.sem, ffn_taken.at(it, s, e + 1))
                done = resid if e == EXPERTS - 1 else ffn_added
                nc.vector.tensor_tensor(x[:], x[:], tmp, ALU.add).then_inc(done.sem, 1)

        def moe1_pe(pe, it):
            s = "moe1"
            router_pe(pe, it, s)
            pe.wait_ge(wbc_lo.sem, wbc_lo.at(it, s))
            pe.wait_ge(wbc_hi.sem, wbc_hi.at(it, s))
            for e in range(EXPERTS + 2):
                if e <= EXPERTS:
                    if e >= 2:
                        pe.wait_ge(hid_ready.sem, hid_ready.at(it, s, e - 1))
                    cs = slice(e * P, (e + 1) * P)
                    nc.tensor.matmul(ps[:, 2 * (e % 2), :], W(s, "w1")[:, cs], xn[:], start=True, stop=True)
                    nc.tensor.matmul(ps[:, 2 * (e % 2) + 1, :], W(s, "w3")[:, cs], xn[:], start=True, stop=True)\
                        .then_inc(hid_ps.sem, 1)
                if e >= 1:
                    pe.wait_ge(hid_ready.sem, hid_ready.at(it, s, e))
                    if e >= 3:
                        pe.wait_ge(ffn_taken.sem, ffn_taken.at(it, s, e - 2))
                    nc.tensor.matmul(ps[:, 4 + (e - 1) % 2, :], W(s, "w2")[:, (e - 1) * P:e * P],
                                     hid[:, (e - 1) % 2, 0, :], start=True, stop=True).then_inc(ffn_ps.sem, 1)

        def moe1_act(act, it):
            s = "moe1"
            router_act(act, it, s)
            for e in range(EXPERTS + 1):
                act.wait_ge(hid_ps.sem, hid_ps.at(it, s, e + 1))
                if e >= 2:
                    act.wait_ge(hid_ready.sem, hid_ready.at(it, s, e - 1))
                nc.scalar.activation(gate[:, e % 2, :], ps[:, 2 * (e % 2), :], ACT.Silu).then_inc(gate_ready.sem, 1)

        def moe1_dve(dve, it):
            s = "moe1"
            router_dve(dve, it, s)
            wbc_dve(dve, it, s)
            dve.wait_ge(wbc_lo.sem, wbc_lo.at(it, s))
            dve.wait_ge(wbc_hi.sem, wbc_hi.at(it, s))
            for e in range(EXPERTS + 2):
                if e <= EXPERTS:
                    dve.wait_ge(gate_ready.sem, gate_ready.at(it, s, e + 1))
                    if e >= 2:
                        dve.wait_ge(ffn_ps.sem, ffn_ps.at(it, s, e - 1))
                    nc.vector.tensor_tensor(hid[:, e % 2, 0, :], gate[:, e % 2, :], ps[:, 2 * (e % 2) + 1, :], ALU.mult)\
                        .then_inc(hid_ready.sem, 1)
                if e >= 1:
                    f = e - 1
                    dve.wait_ge(ffn_ps.sem, ffn_ps.at(it, s, f + 1))
                    if f >= 1:
                        dve.wait_ge(ffn_added.sem, ffn_added.at(it, s, f))
                    if f < EXPERTS:
                        nc.vector.tensor_tensor(tmp, ps[:, 4 + f % 2, :], wbc[:, f, :], ALU.mult)\
                            .then_inc(ffn_taken.sem, 1)
                    else:
                        nc.vector.tensor_copy(tmp, ps[:, 4 + f % 2, :]).then_inc(ffn_taken.sem, 1)
                    dve.wait_ge(ffn_taken.sem, ffn_taken.at(it, s, f + 1))
                    nc.vector.tensor_tensor(z[:], z[:], tmp, ALU.add).then_inc(ffn_added.sem, 1)
            dve.wait_ge(ffn_added.sem, ffn_added.at(it, s, EXPERTS + 1))
            nc.vector.tensor_tensor(x[:], x[:], z[:], ALU.add).then_inc(resid.sem, 1)

        def mlp_pe(pe, it):
            s = "mlp"
            router_pe(pe, it, s)
            for c in range(CH0):
                nc.tensor.matmul(ps[:, c, :], W(s, "up")[:, c * P:(c + 1) * P], xn[:], start=True, stop=True)\
                    .then_inc(hid_ps.sem, 1)
            for c in range(CH0):
                pe.wait_ge(hid_ready.sem, hid_ready.at(it, s, c + 1))
                last = nc.tensor.matmul(ps[:, 4, :], W(s, "down")[:, c * P:(c + 1) * P], hid[:, 0, c, :],
                                        start=(c == 0), stop=(c == CH0 - 1))
            last.then_inc(ffn_ps.sem, 1)

        def mlp_act(act, it):
            s = "mlp"
            router_act(act, it, s)
            for c in range(CH0):
                act.wait_ge(hid_ps.sem, hid_ps.at(it, s, c + 1))
                nc.scalar.activation(hid[:, 0, c, :], ps[:, c, :], ACT.Silu).then_inc(hid_ready.sem, 1)

        def mlp_dve(dve, it):
            s = "mlp"
            router_dve(dve, it, s)
            dve.wait_ge(wbc_lo.sem, wbc_lo.at(it, s))
            dve.wait_ge(ffn_ps.sem, ffn_ps.at(it, s))
            nc.vector.tensor_tensor(tmp, ps[:, 4, :], wbc[:, 0, :], ALU.mult).then_inc(ffn_taken.sem, 1)
            dve.wait_ge(ffn_taken.sem, ffn_taken.at(it, s))
            nc.vector.tensor_tensor(z[:], z[:], tmp, ALU.add).then_inc(ffn_added.sem, 1)
            dve.wait_ge(ffn_added.sem, ffn_added.at(it, s))
            nc.vector.tensor_tensor(x[:], x[:], z[:], ALU.add).then_inc(resid.sem, 1)

        def qlora_pe(pe, it):
            pe.wait_ge(weff_ready, 1)
            pe.wait_ge(norm_out.sem, norm_out.at(it, "qlora"))
            for i in range(3):
                s = f"block{i}"
                if i:
                    pe.wait_ge(resid.sem, resid.at(it, f"block{i - 1}"))
                nc.tensor.matmul(ps[:, 2, :], weff[:, 2 * i * P:(2 * i + 1) * P], z[:], start=True, stop=True)\
                    .then_inc(lin_ps.sem, 1)
                norm_pe(pe, it, s)
                pe.wait_ge(gelu_ready.sem, gelu_ready.at(it, s))
                nc.tensor.matmul(ps[:, 3, :], weff[:, (2 * i + 1) * P:(2 * i + 2) * P], sq[:], start=True, stop=True)\
                    .then_inc(lin_ps.sem, 1)

        def qlora_act(act, it):
            for i in range(3):
                s = f"block{i}"
                norm_act(act, it, s, "eps5")
                act.wait_ge(norm_out.sem, norm_out.at(it, s))
                nc.scalar.activation(sq[:], xn[:], ACT.Gelu, scale=W("qlora", "gamma")[:, i:i + 1],
                                     bias=W("qlora", "beta")[:, i:i + 1]).then_inc(gelu_ready.sem, 1)

        def qlora_dve(dve, it):
            for i in range(3):
                s = f"block{i}"
                bias = W("qlora", "bias")
                dve.wait_ge(lin_ps.sem, lin_ps.at(it, s, 1))
                nc.vector.tensor_scalar(y[:], ps[:, 2, :], bias[:, 2 * i:2 * i + 1], None, ALU.add)\
                    .then_inc(resid.sem, 1)
                norm_dve(dve, it, s)
                dve.wait_ge(lin_ps.sem, lin_ps.at(it, s, 2))
                if i < 2:
                    nc.vector.scalar_tensor_tensor(out=z[:], in0=ps[:, 3, :], scalar=bias[:, 2 * i + 1:2 * i + 2],
                                                   in1=z[:], op0=ALU.add, op1=ALU.add).then_inc(resid.sem, 1)
                else:
                    nc.vector.scalar_tensor_tensor(out=y[:], in0=ps[:, 3, :], scalar=bias[:, 2 * i + 1:2 * i + 2],
                                                   in1=z[:], op0=ALU.add, op1=ALU.add).then_inc(lin_sum.sem, 1)
                    dve.wait_ge(lin_sum.sem, lin_sum.at(it, s))
                    nc.vector.tensor_tensor(z[:], x[:], y[:], ALU.add).then_inc(resid.sem, 1)

        lin_sum = signal("lin_sum", {"block2": 1})

        @block.sync
        def _(sp):
            def load(s):
                first, end, _ = cols[s]
                into = masks if s == "masks" else wts[:, first - skip:end - skip]
                sp.dma_start(into, w_dram[:, first:end]).then_inc(loaded[s], 16)

            for s in ("masks", "const", "causal0"):
                load(s)
            sp.dma_start(xin[:], x_dram[:, 0:TOK]).then_inc(xin_loaded, 16)
            sp.dma_start(qint, qw_dram).then_inc(qint_loaded, 16)
            load("qlora")
            for s in list(STAGES)[3:-1]:
                load(s)
            with sp.Fori(0, PASSES - 1) as it:
                sp.wait_ge(resid.sem, resid.at(it, "load"))
                sp.sem_inc(wait_carrier)
                sp.dma_start(xin[:], x_dram[:, bass.ds(it * TOK + TOK, TOK)]).then_inc(xin_loaded, 16)
                sp.wait_ge(resid.sem, resid.at(it, "block2"))
                sp.sem_inc(wait_carrier)
                sp.dma_start(out_dram[:, bass.ds(it * TOK, TOK)], z[:]).then_inc(out_stored, 16)
            sp.wait_ge(resid.sem, PASSES * resid.total + 1)
            sp.dma_start(out_dram[:, (PASSES - 1) * TOK:], z[:]).then_inc(out_stored, 16)
            sp.wait_ge(out_stored, (PASSES + 1) * 16)

        @block.gpsimd
        def _(pool):
            nc.gpsimd.memset(v9[:], 1.0).then_inc(consts_ready, 1)
            nc.gpsimd.memset(v33[:], 1.0).then_inc(consts_ready, 1)
            nc.gpsimd.memset(negm[:], 0.0).then_inc(consts_ready, 1)
            nc.gpsimd.memset(z[:], 0.0).then_inc(out_stored, 16)

        CONSTS = 8

        @block.tensor
        def _(pe):
            pe.wait_ge(loaded["const"], 16)
            pe.wait_ge(consts_ready, CONSTS)
            pe.wait_ge(loaded["qlora"], 16)
            for i in range(6):
                last = nc.tensor.matmul(ps[:, i // 4, i % 4 * P:(i % 4 + 1) * P],
                                        W("qlora", "la")[0:RANK, i * P:(i + 1) * P],
                                        W("qlora", "lb")[0:RANK, i * P:(i + 1) * P], start=True, stop=True)
            last.then_inc(lora_ps, 1)
            pe.wait_ge(weff_ready, 1)
            with pe.Fori(0, PASSES) as it:
                norm_pe(pe, it, "causal0")
                headed_pe(pe, it, "causal0")
                norm_pe(pe, it, "moe0")
                moe0_pe(pe, it)
                norm_pe(pe, it, "causal1")
                headed_pe(pe, it, "causal1")
                norm_pe(pe, it, "mqa_in")
                pe.wait_ge(loaded["mqa"], 16)
                norm_pe(pe, it, "mqa")
                mqa_pe(pe, it)
                pe.wait_ge(loaded["moe1"], 16)
                norm_pe(pe, it, "moe1")
                moe1_pe(pe, it)
                norm_pe(pe, it, "linear")
                headed_pe(pe, it, "linear")
                norm_pe(pe, it, "causal2_in")
                pe.wait_ge(loaded["causal2"], 16)
                norm_pe(pe, it, "causal2")
                headed_pe(pe, it, "causal2")
                pe.wait_ge(loaded["mlp"], 16)
                norm_pe(pe, it, "mlp")
                mlp_pe(pe, it)
                norm_pe(pe, it, "arccos")
                arccos_pe(pe, it)
                norm_pe(pe, it, "qlora")
                qlora_pe(pe, it)

        @block.scalar
        def _(act):
            act.wait_ge(loaded["const"], 16)
            act.wait_ge(consts_ready, CONSTS)
            with act.Fori(0, PASSES) as it:
                norm_act(act, it, "causal0", "eps5")
                headed_act(act, it, "causal0")
                norm_act(act, it, "moe0", "eps5")
                moe0_act(act, it)
                norm_act(act, it, "causal1", "eps5")
                headed_act(act, it, "causal1")
                norm_act(act, it, "mqa_in", "eps5")
                norm_act(act, it, "mqa", "eps6")
                mqa_act(act, it)
                norm_act(act, it, "moe1", "eps6")
                moe1_act(act, it)
                norm_act(act, it, "linear", "eps5")
                headed_act(act, it, "linear")
                norm_act(act, it, "causal2_in", "eps5")
                norm_act(act, it, "causal2", "eps6")
                headed_act(act, it, "causal2")
                norm_act(act, it, "mlp", "eps6")
                mlp_act(act, it)
                norm_act(act, it, "arccos", "eps5")
                arccos_act(act, it)
                norm_act(act, it, "qlora", "eps5")
                qlora_act(act, it)

        @block.vector
        def _(dve):
            dve.wait_ge(loaded["const"], 16)
            dve.wait_ge(loaded["masks"], 16)
            nc.vector.tensor_copy(ident_bf[:], C("ident")).then_inc(consts_ready, 1)
            nc.vector.tensor_copy(mask_qk[:], M("mask_qk")).then_inc(consts_ready, 1)
            nc.vector.tensor_copy(mask_kq[:], M("mask_kq")).then_inc(consts_ready, 1)
            nc.vector.tensor_copy(before_bf[:], M("before")).then_inc(consts_ready, 1)
            nc.vector.tensor_copy(ones_bf[:], M("ones")).then_inc(consts_ready, 1)
            dve.wait_ge(qint_loaded, 16)
            nc.vector.tensor_copy(weff[:], qint).then_inc(dequant_step, 1)
            nc.vector.memset(x[:], 0.0).then_inc(resid.sem, 1)
            dve.wait_ge(dequant_step, 1)
            nc.vector.tensor_scalar(weff[:], weff[:], 1.0 / 7.5, -1.0, ALU.mult, ALU.add).then_inc(dequant_step, 1)
            dve.wait_ge(dequant_step, 2)
            dve.wait_ge(loaded["qlora"], 16)
            nc.vector.tensor_tensor(weff[:], weff[:], W("qlora", "scale"), ALU.mult).then_inc(dequant_step, 1)
            dve.wait_ge(dequant_step, 3)
            dve.wait_ge(lora_ps, 1)
            nc.vector.tensor_tensor(weff[:], weff[:], ps[:, 0:2, :].rearrange("p a b -> p (a b)")[:, 0:6 * P], ALU.add)\
                .then_inc(weff_ready, 1)
            with dve.Fori(0, PASSES) as it:
                dve.wait_ge(resid.sem, it * resid.total + 1)
                dve.wait_ge(xin_loaded, it * 16 + 16)
                nc.vector.tensor_copy(x[:], xin[:]).then_inc(resid.sem, 1)
                norm_dve(dve, it, "causal0")
                headed_dve(dve, it, "causal0")
                norm_dve(dve, it, "moe0")
                moe0_dve(dve, it)
                norm_dve(dve, it, "causal1")
                headed_dve(dve, it, "causal1")
                dve.wait_ge(out_stored, it * 16 + 16)
                norm_dve(dve, it, "mqa_in")
                norm_dve(dve, it, "mqa", W("mqa", "g"))
                mqa_dve(dve, it)
                norm_dve(dve, it, "moe1", W("moe1", "g"))
                moe1_dve(dve, it)
                norm_dve(dve, it, "linear")
                headed_dve(dve, it, "linear")
                norm_dve(dve, it, "causal2_in")
                norm_dve(dve, it, "causal2", W("causal2", "g"))
                headed_dve(dve, it, "causal2")
                norm_dve(dve, it, "mlp", W("mlp", "g"))
                mlp_dve(dve, it)
                norm_dve(dve, it, "arccos")
                arccos_dve(dve, it)
                norm_dve(dve, it, "qlora")
                qlora_dve(dve, it)


def _constants():
    p = np.arange(P)
    head, dim = p // HD, p % HD
    esel = np.zeros((P, GROUPS, P), np.float32)
    esel[p, head // HPG, QUAD * (head % HPG) + dim] = 1.0
    later = (p[None, :] > p[:, None])
    zero = np.zeros((P, P), np.float32)
    mask_q = np.where(later, NEG, 0.0).astype(np.float32)
    mask_k = np.ascontiguousarray(mask_q.T)
    keep = (~later.T).astype(np.float32)

    def col(v):
        return np.full((P, 1), v, np.float32)

    return {"ident": np.eye(P, dtype=np.float32), "blk8": (head[:, None] == head[None, :]).astype(np.float32),
            "esel": esel.reshape(P, -1), "mask_qk": np.concatenate([zero, mask_q], 1),
            "mask_kq": np.concatenate([mask_k, zero, mask_k], 1),
            "keep_kq": np.concatenate([keep, zero + 1.0, keep], 1),
            "before": later.astype(np.float32), "ones": zero + 1.0, "mean": zero + 1.0 / P,
            "aug": (p % QUAD == HD).astype(np.float32)[:, None],
            "iota": np.tile(np.arange(EXPERTS, dtype=np.float32), (P, 1)), "eps5": col(1e-5), "eps6": col(1e-6),
            "half": col(0.5), "one": col(1.0), "ln1024": col(np.log(1024.0))}


def _quadrants(w):
    out = np.zeros((P, GROUPS, HPG, QUAD), w.dtype)
    out[:, :, :, :HD] = w.reshape(P, GROUPS, HPG, HD)
    return out.reshape(P, GROUPS * P)


def _rows(v):
    return np.broadcast_to(v.reshape(1, -1), (P, v.size))


def _side(w):
    return w.transpose(1, 0, 2).reshape(w.shape[1], -1)


def _chunks(w):
    n, h, o = w.shape
    return w.reshape(n, h // P, P, o).transpose(2, 0, 1, 3).reshape(P, -1)


def kernel(**inputs):
    import concourse.bacc as bacc
    from concourse.bass_utils import run_bass_kernel_spmd

    a = {k: np.asarray(v) for k, v in inputs.items()}

    def headed(q, k, v, o):
        return {"q": _quadrants(q), "k": _quadrants(k), "v": v, "o": o}

    def tall(w):
        return np.concatenate([w, np.zeros((P - w.shape[0], w.shape[1]), w.dtype)], 0)

    qkv2, lin, qkv3 = a["L2_ffn_qkv_w"].T, a["L2_attn_wqkv"], a["L3_attn_w_qkv"].T
    b3 = a["L3_attn_b_qkv"]
    both = {n: np.concatenate([a[f"L1_ffn_e{n}"], a[f"L1_ffn_s{n}"][None]], 0) for n in ("W1", "W2", "W3")}
    parts = {
        "masks": _constants(),
        "const": _constants(),
        "causal0": headed(a["L0_attn_WQ"].T, a["L0_attn_WK"].T, a["L0_attn_WV"].T, a["L0_attn_WO"].T),
        "moe0": {"router": a["L0_ffn_Wr"], "rbias": _rows(a["L0_ffn_br"]), "w1": _side(a["L0_ffn_W1"]),
                 "b1": a["L0_ffn_b1"].reshape(EXPERTS * CH0, P).T, "w2": _chunks(a["L0_ffn_W2"]), "b2": a["L0_ffn_b2"].T},
        "causal1": headed(a["L1_attn_Wq"].T, a["L1_attn_Wk"].T, a["L1_attn_Wv"].T, a["L1_attn_Wo"].T),
        "mqa": {"g": a["L1_ffn_g1"][:, None], "q": a["L1_ffn_Wq"].T, "k": np.tile(a["L1_ffn_Wkc"].T, (1, MQH)),
                "v": a["L1_ffn_Wvc"].T, "o": a["L1_ffn_Wo"].T},
        "moe1": {"g": a["L1_ffn_g2"][:, None], "router": a["L1_ffn_Wr"].T, "rbias": _rows(a["L1_ffn_expert_bias"]),
                 **{n.lower(): _side(both[n].transpose(0, 2, 1)) for n in ("W1", "W3", "W2")}},
        "linear": headed(lin[:, 0:P], lin[:, P:2 * P], lin[:, 2 * P:], a["L2_attn_wo"]),
        "causal2": {"g": a["L2_ffn_n1_w"][:, None],
                    **headed(qkv2[:, 0:P], qkv2[:, P:2 * P], qkv2[:, 2 * P:], a["L2_ffn_o_w"].T)},
        "mlp": {"g": a["L2_ffn_n2_w"][:, None], "router": a["L2_ffn_gate_w"].T, "up": a["L2_ffn_up_w"].T,
                "down": _chunks(a["L2_ffn_down_w"].T[None])},
        "arccos": {"q": qkv3[:, 0:P], "k": qkv3[:, P:2 * P], "v": qkv3[:, 2 * P:], "o": a["L3_attn_w_out"].T,
                   "bq": b3[0:P, None], "bk": b3[P:2 * P, None], "bv": _rows(b3[2 * P:]), "bo": a["L3_attn_b_out"][:, None]},
        "qlora": {"bias": a["L3_ffn_biases"].T, "gamma": a["L3_ffn_ln_gamma"].T, "beta": a["L3_ffn_ln_beta"].T,
                  "scale": _side(np.repeat(a["L3_ffn_scales"].transpose(0, 2, 1), QGROUP, 1)),
                  "la": tall(_side(a["L3_ffn_lora_a"])), "lb": tall(_side(a["L3_ffn_lora_b"].transpose(0, 2, 1)))},
    }
    blob = np.concatenate([parts[s][n] for s, names in STAGES.items() for n, _ in names], 1)
    arrays = {"x_dram": np.ascontiguousarray(a["L0_attn_x"].reshape(BATCH * SEQ, P).T),
              "w_dram": np.ascontiguousarray(blob),
              "qw_dram": np.ascontiguousarray(_side(a["L3_ffn_qweights"].transpose(0, 2, 1)))}
    nc = bacc.Bacc("TRN2", target_bir_lowering=False, num_devices=1)
    args = [nc.dram_tensor(n, v.shape, mybir.dt.from_np(v.dtype), kind="ExternalInput").ap() for n, v in arrays.items()]
    args.append(nc.dram_tensor("out_dram", (P, BATCH * SEQ), F32, kind="ExternalOutput").ap())
    build(nc, *args)
    r = run_bass_kernel_spmd(nc, [arrays], core_ids=[0])
    got = r.results[0]["out_dram"]
    return np.ascontiguousarray(got.T).reshape(BATCH, SEQ, P)
```

```python
from contextlib import ExitStack

import numpy as np

import concourse.bass as bass
from concourse import mybir

ALU = mybir.AluOpType
ACT = mybir.ActivationFunctionType
F32 = mybir.dt.float32
F32R = mybir.dt.float32r
BF16 = mybir.dt.bfloat16
U32 = mybir.dt.uint32
I32 = mybir.dt.int32
AX = mybir.AxisListType

P = 128
BATCH, SEQ = 16, 256
PAIR = 2
TOK = PAIR * SEQ
TILES = TOK // P
PASSES = BATCH // PAIR
HEADS, HD = 16, 8
GROUPS, QUAD = 4, 32
HPG = HEADS // GROUPS
V1 = HD + 1
EXPERTS = 8
FF0 = 512
CH0 = FF0 // P
CAP = max(1, int(SEQ / EXPERTS * 1.25))
MQH, MQD = 4, 32
MV1 = MQD + 1
BANKS = 4
NEG = -1.0e30
RANK, QGROUP = 32, 16
LIN_EPS = 1e-5
CLIP = float(np.float32(1.0) - np.float32(1e-7))
CLIP_LO = float(np.float32(-1.0) + np.float32(1e-7))
GEO_POWER = -3.2
LN_EXP = "natural_log_exp_and_others"

HEADED = [("q", GROUPS * P), ("k", GROUPS * P), ("v", P), ("o", P)]
STAGES = {
    "masks": [("mask_q", P), ("mask_k", P), ("before", P), ("ones", P)],
    "lora": [("scale", 6 * P), ("la", 6 * P), ("lb", 6 * P)],
    "const": [("ident", P), ("blk8", P), ("esel", GROUPS * P), ("keep_k", P), ("mean", P),
              ("den", P), ("dense", GROUPS * P), ("head_row", 1),
              ("max_rows", GROUPS), ("q_low", 1), ("q_sign", 1), ("k_low", 1), ("k_sign", 1), ("m_low", 1), ("m_sign", 1),
              ("iota", EXPERTS), ("eps5", 1), ("eps6", 1), ("half", 1), ("one", 1), ("ln1024", 1), ("lin_eps", 1)],
    "causal0": HEADED,
    "moe0": [("router", EXPERTS), ("rbias", EXPERTS), ("w1", EXPERTS * FF0), ("b1", EXPERTS * CH0),
             ("w2", EXPERTS * FF0), ("b2", EXPERTS)],
    "causal1": HEADED,
    "mqa": [("g", 1), ("q", P), ("k", P), ("v", MQD), ("o", P)],
    "moe1": [("g", 1), ("router", EXPERTS), ("rbias", EXPERTS), ("w1", (EXPERTS + 1) * P), ("w3", (EXPERTS + 1) * P),
             ("w2", (EXPERTS + 1) * P)],
    "linear": HEADED,
    "causal2": [("g", 1)] + HEADED,
    "mlp": [("g", 1), ("router", EXPERTS), ("up", FF0), ("down", FF0)],
    "arccos": [("q", P), ("k", P), ("v", P), ("o", P), ("bq", 1), ("bk", 1), ("bv", P), ("bo", 1)],
    "qlora": [("bias", 6), ("gamma", 3), ("beta", 3)],
}
ONCE = ("masks", "lora")


def columns():
    out, at = {}, 0
    for stage, parts in STAGES.items():
        first, names = at, {}
        for name, width in parts:
            names[name] = (at, width)
            at += width
        out[stage] = (first, at, names)
    return out, at


class Turn:

    def __init__(self, register, shift):
        self.register, self.shift = register, shift

    def count(self, per_pass, more):
        fixed = self.shift * per_pass + more
        return fixed if self.register is None else self.register * per_pass + fixed


class Signal:

    def __init__(self, sem, counts, ahead=0):
        self.sem, self.base, self.total, self.ahead = sem, {}, 0, ahead
        for stage in sorted(counts, key=ORDER.index):
            self.base[stage] = self.total
            self.total += counts[stage]

    def at(self, turn, stage, n=1):
        return turn.count(self.total, self.ahead + self.base[stage] + n)

    def before(self, turn):
        return turn.count(self.total, self.ahead)


ORDER = ["load", "causal0", "moe0", "causal1", "mqa_in", "mqa", "moe1", "linear", "causal2_in", "causal2", "mlp",
         "arccos", "qlora", "block0_in", "block0", "block1_in", "block1", "block2_in", "block2"]
CAUSAL = ("causal0", "causal1", "causal2")
HEADED_STAGES = ("causal0", "causal1", "linear", "causal2")
ATTENTION = HEADED_STAGES + ("mqa", "arccos")
NORMS = {
    "causal0": ("x", "xn", True, "eps5", ("resid", "load"), None),
    "moe0": ("x", "xn", True, "eps5", ("resid", "causal0"), None),
    "causal1": ("x", "xn", True, "eps5", ("resid", "moe0"), None),
    "mqa_in": ("x", "z", True, "eps5", ("resid", "causal1"), None),
    "mqa": ("z", "xn", False, "eps6", ("norm_out", "mqa_in"), "mqa"),
    "moe1": ("z", "xn", False, "eps6", ("resid", "mqa"), "moe1"),
    "linear": ("x", "xn", True, "eps5", ("handed", "moe1"), None),
    "causal2_in": ("x", "z", True, "eps5", ("resid", "linear"), None),
    "causal2": ("z", "xn", False, "eps6", ("norm_out", "causal2_in"), "causal2"),
    "mlp": ("z", "xn", False, "eps6", ("resid", "causal2"), "mlp"),
    "arccos": ("x", "xn", True, "eps5", ("resid", "mlp"), None),
    "qlora": ("x", "z", True, "eps5", ("resid", "arccos"), None),
    "block0": ("y", "xn", True, "eps5", ("resid", "block0_in"), None),
    "block1": ("y", "xn", True, "eps5", ("resid", "block1_in"), None),
    "block2": ("y", "xn", True, "eps5", ("resid", "block2_in"), None),
}
RESID = ["load", "causal0", "moe0", "causal1", "mqa", "moe1", "linear", "causal2", "mlp", "arccos",
         "block0_in", "block0", "block1_in", "block1", "block2_in", "block2"]
MSETS = PAIR * 3
ESETS = PAIR * HPG
QSETS = PAIR * 2
ASETS = 2 * 2
ARC_STEPS = 6
FSETS = EXPERTS * 2

NORM_ROUNDS = 2
PROJECT = 3
ROUTE = 5
OUT = 3
ROUNDS = {"causal": PROJECT + MSETS + 1 + ESETS + 1 + OUT, "linear": PROJECT + ESETS + 1 + OUT, "mqa": 1 + TILES + 1 + QSETS + 3,
          "moe0": ROUTE + FSETS + 1, "moe1": ROUTE + EXPERTS + 2, "mlp": 5,
          "arccos": 4 + PAIR * (ASETS + ARC_STEPS + 2) + OUT, "block": 3 + NORM_ROUNDS}
SHARES = {"norm": 3, "causal": 55, "linear": 35, "mqa": 35, "moe0": 60, "moe1": 30, "mlp": 10, "arccos": 90, "block": 12}
FRONT = [("norm", "causal0"), ("causal", "causal0"), ("norm", "moe0"), ("moe0", "moe0"), ("norm", "causal1"),
         ("causal", "causal1"), ("norm", "mqa_in"), ("norm", "mqa"), ("mqa", "mqa"), ("norm", "moe1"), ("moe1", "moe1")]
BACK = [("norm", "linear"), ("linear", "linear"), ("norm", "causal2_in"), ("norm", "causal2"), ("causal", "causal2"),
        ("norm", "mlp"), ("mlp", "mlp"), ("norm", "arccos"), ("arccos", "arccos"), ("norm", "qlora"),
        ("block", "block0"), ("block", "block1"), ("block", "block2")]
ROUNDS["norm"] = NORM_ROUNDS


def schedule(halves):
    order = []
    for h, parts in enumerate(halves):
        total, at, r = sum(SHARES[kind] for kind, _ in parts), 0.0, 0
        for kind, _ in parts:
            for i in range(ROUNDS[kind]):
                order.append(((at + SHARES[kind] * (i + 0.5) / ROUNDS[kind]) / total, h, r))
                r += 1
            at += SHARES[kind]
        if parts is FRONT:
            order[-1] = (1.0, h, r - 1)
    return [(h, r) for _, h, r in sorted(order)]


def weave(order, halves):
    ahead = [next(half, None) for half in halves]
    for h, r in order:
        while ahead[h] is not None and ahead[h] <= r:
            ahead[h] = next(halves[h], None)


def in_rounds(parts, turn, stage_of):
    first = 0
    for kind, name in parts:
        for r in stage_of[kind](turn, name):
            yield first + r
        first += ROUNDS[kind]


class Half:

    def __init__(self, nc, ctx, name, parts):
        stages = {n for _, n in parts} | {f"block{i}_in" for i in range(3)} | {"load"}
        self.front = parts is FRONT
        if not self.front:
            stages -= {"load"}
        else:
            stages -= {f"block{i}_in" for i in range(3)}
        norms = [n for kind, n in parts if kind == "norm"] + [n for kind, n in parts if kind == "block"]

        def sb(buf, shape, dt=F32):
            return ctx.enter_context(nc.sbuf_tensor(f"{name}_{buf}", shape, dt))

        def rounded(buf, shape, first=0):
            return nc.alloc_sbuf_tensor_at(f"{name}_{buf}", shape, F32R, offset=last_at[0] + 4 * first)

        def at_last(buf, shape):
            out = sb(buf, shape)
            last_at[0] = nc.sbuf_base - 4 * int(np.prod(shape[1:]))
            return out

        last_at = [0]

        def signal(sig, counts, ahead=0):
            mine = {s: n for s, n in counts.items() if s in stages}
            return Signal(ctx.enter_context(nc.semaphore(f"{name}_{sig}")), mine, ahead) if mine else None

        self.ps = ctx.enter_context(nc.psum_tensor(f"{name}_ps", [P, BANKS, 512], F32))
        self.x = sb("x", [P, TOK])
        self.z = sb("z", [P, TOK])
        self.xn = sb("xn", [P, TOK])
        self.cen = sb("cen", [P, TOK])
        self.sq = sb("sq", [P, TOK])
        self.qk = at_last("qk", [P, 2 * GROUPS, TOK])
        qkr = rounded("qkr", [P, 2 * GROUPS, TOK])
        self.q4, self.k4 = self.qk[:, 0:GROUPS, :], self.qk[:, GROUPS:, :]
        self.q4r, self.k4r = qkr[:, 0:GROUPS, :], qkr[:, GROUPS:, :]
        self.wbc = self.qk
        self.v9 = sb("v9", [P, TILES, HEADS, V1])
        if self.front:
            self.rden = sb("rden", [P, PAIR, 2 * MQH])
            self.v33 = sb("v33", [P, TILES, MV1])
            self.xin = sb("xin", [P, TOK])
            scratch = sb("scratch", [P, 7 * TOK])
            parts = sb("parts", [P, HPG * TOK])
            self.negm, self.maxT = sb("negm", [P, TILES, P]), at_last("maxT", [P, TOK])
            self.maxTr = rounded("maxTr", [P, TOK])
            self.ytok = scratch[:, 6 * TOK:7 * TOK].rearrange("p (t c) -> p t c", t=TILES)
        else:
            self.vs = sb("vs", [P, 2, HEADS, V1])
            self.nsum = sb("nsum", [P, 2, HEADS])
            self.cosines = scratch = at_last("cosines", [P, 2 * HEADS * SEQ])
            self.maxTr = rounded("maxTr", [P, TOK], 13 * TOK)
            self.scratch = scratch
            parts = scratch[:, 8 * TOK:12 * TOK]
            self.negm = scratch[:, 12 * TOK:13 * TOK].rearrange("p (t c) -> p t c", t=TILES)
            self.y = sb("y", [P, TOK])
        self.parts = {s: [parts[:, j * TOK:(j + 1) * TOK] for j in range(HPG)] for s in HEADED_STAGES}
        self.parts["arccos"] = [] if self.front else [self.y[:], self.z[:], self.sq[:], self.cen[:]]
        self.rden4 = {s: scratch[:, 0:HPG * TOK].rearrange("p (j t) -> p j t", j=HPG) for s in HEADED_STAGES}
        self.rden4["arccos"] = self.q4
        self.probs = scratch[:, 0:6 * TOK].rearrange("p (s c) -> p s c", s=2)
        self.high = scratch[:, 0:GROUPS * TOK].rearrange("p (g t) -> p g t", g=GROUPS)
        self.rect = scratch[:, GROUPS * TOK:2 * GROUPS * TOK].rearrange("p (g t) -> p g t", g=GROUPS) if not self.front else None
        self.hid = scratch[:, 0:4 * TOK].rearrange("p (s c t) -> p s c t", s=2, c=2)
        self.tmp = scratch[:, 4 * TOK:5 * TOK]
        self.gate = scratch[:, 5 * TOK:7 * TOK].rearrange("p (s t) -> p s t", s=2)
        self.lg, self.pr, self.t8, self.wtok = (sb(n, [P, TILES, EXPERTS]) for n in ("lg", "pr", "t8", "wtok"))
        if self.front:
            self.ixf, self.oh1, self.oh2, self.ohs = (sb(n, [P, TILES, EXPERTS]) for n in ("ixf", "oh1", "oh2", "ohs"))
            self.ix = sb("ix", [P, TILES, EXPERTS], U32)
            self.ohs_bf = sb("ohs_bf", [P, TILES, EXPERTS], BF16)
        self.s1, self.s2, self.s3, self.s4 = (sb(n, [P, TILES, 1]) for n in ("s1", "s2", "s3", "s4"))
        self.buf = {"x": self.x, "z": self.z, "xn": self.xn, "y": None if self.front else self.y}

        centred = [n for n in norms if NORMS[n][2]]
        self.resid = signal("resid", {r: 1 for r in RESID}, ahead=1)
        self.norm_mean = signal("norm_mean", {n: 1 for n in centred})
        self.norm_cen = signal("norm_cen", {n: 1 for n in centred})
        self.norm_sq = signal("norm_sq", {n: 1 for n in norms})
        self.norm_var = signal("norm_var", {n: 1 for n in norms})
        self.norm_ln = signal("norm_ln", {n: 1 for n in norms})
        self.norm_rstd = signal("norm_rstd", {n: 1 for n in norms})
        self.norm_out = signal("norm_out", {n: 1 for n in norms})
        self.q_ps = signal("q_ps", {s: 1 for s in ATTENTION})
        self.k_ps = signal("k_ps", {s: 1 for s in ATTENTION})
        self.v_ps = signal("v_ps", {s: 1 for s in ATTENTION})
        self.q_high = signal("q_high", {s: 1 for s in HEADED_STAGES + ("arccos",)})
        self.k_high = signal("k_high", {s: 1 for s in HEADED_STAGES + ("arccos",)})
        self.rect_ready = signal("rect_ready", {"linear": 2})
        self.q_ready = signal("q_ready", {s: 1 for s in ATTENTION})
        self.k_ready = signal("k_ready", {s: 1 for s in ATTENTION})
        self.v_ready = signal("v_ready", {s: 1 for s in ATTENTION})
        self.max_ps = signal("max_ps", {s: MSETS for s in CAUSAL} | {"mqa": TILES})
        self.max_done = signal("max_done", {s: MSETS for s in CAUSAL} | {"mqa": TILES})
        self.max_pair = signal("max_pair", {s: 1 for s in CAUSAL})
        self.negm_high = signal("negm_high", {s: 1 for s in CAUSAL})
        self.negm_ps = signal("negm_ps", {s: 1 for s in CAUSAL + ("mqa",)})
        self.negm_ready = signal("negm_ready", {s: 1 for s in CAUSAL + ("mqa",)})
        self.score_ps = signal("score_ps", {s: ESETS for s in HEADED_STAGES} | {"mqa": QSETS, "arccos": PAIR * ASETS})
        self.probs_ready = signal("probs_ready", {s: ESETS for s in HEADED_STAGES} | {"mqa": QSETS})
        self.full_ready = signal("full_ready", {"linear": ESETS})
        self.pv_ps = signal("pv_ps", {s: ESETS for s in HEADED_STAGES} | {"mqa": QSETS, "arccos": PAIR})
        self.part_ready = signal("part_ready", {s: HPG for s in HEADED_STAGES} | {"arccos": PAIR})
        self.den_ps = signal("den_ps", {s: 1 for s in HEADED_STAGES + ("arccos",)})
        self.den_ln = signal("den_ln", {s: 1 for s in HEADED_STAGES + ("arccos",)})
        self.rden_ready = signal("rden_ready", {s: 1 for s in HEADED_STAGES + ("arccos",)})
        self.den_step = signal("den_step", {"mqa": 2 * PAIR})
        self.y_ready = signal("y_ready", {s: 1 for s in HEADED_STAGES + ("arccos",)} | {"mqa": PAIR})
        self.yT_ps = signal("yT_ps", {s: 1 for s in ATTENTION})
        self.yT_ready = signal("yT_ready", {s: 1 for s in ATTENTION})
        self.o_ps = signal("o_ps", {s: 1 for s in ATTENTION})
        routed = ("moe0", "moe1", "mlp")
        self.logits_ps = signal("logits_ps", {s: 1 for s in routed})
        self.route_step = signal("route_step", {"moe0": 18, "moe1": 21, "mlp": 14})
        self.route_shift = signal("route_shift", {s: 1 for s in routed})
        self.route_exp = signal("route_exp", {s: 1 for s in routed})
        self.gap_ready = signal("gap_ready", {"moe1": 1})
        self.gap_exp = signal("gap_exp", {"moe1": 1})
        self.chosen_ready = signal("chosen_ready", {"moe0": 1})
        self.place_ps = signal("place_ps", {"moe0": 1})
        self.weight_ready = signal("weight_ready", {s: 1 for s in routed})
        self.wbc_ps = signal("wbc_ps", {"moe0": 2, "moe1": 2, "mlp": 1})
        self.wbc_ready = signal("wbc_ready", {"moe0": 2, "moe1": 2, "mlp": 1})
        self.hid_ps = signal("hid_ps", {"moe0": EXPERTS * CH0, "moe1": EXPERTS + 1, "mlp": CH0})
        self.gate_ready = signal("gate_ready", {"moe1": EXPERTS + 1})
        self.hid_ready = signal("hid_ready", {"moe0": EXPERTS * CH0, "moe1": EXPERTS + 1, "mlp": CH0})
        self.ffn_ps = signal("ffn_ps", {"moe0": FSETS, "moe1": EXPERTS + 1, "mlp": 1})
        self.ffn_taken = signal("ffn_taken", {"moe0": EXPERTS, "moe1": EXPERTS + 1, "mlp": 1})
        self.ffn_added = signal("ffn_added", {"moe0": EXPERTS - 1, "moe1": EXPERTS + 1, "mlp": 1})
        self.arc_raw = signal("arc_raw", {"arccos": 2})
        self.arc_sq = signal("arc_sq", {"arccos": 2})
        self.arc_norm_ps = signal("arc_norm_ps", {"arccos": 2})
        self.arc_floor = signal("arc_floor", {"arccos": 2})
        self.arc_ln = signal("arc_ln", {"arccos": 2})
        self.arc_rn = signal("arc_rn", {"arccos": 2})
        self.arc_unit = signal("arc_unit", {"arccos": 2})
        self.head_ps = signal("head_ps", {"arccos": 2})
        self.cos_ready = signal("cos_ready", {"arccos": PAIR * ASETS})
        self.arc_pass = signal("arc_pass", {"arccos": PAIR * 2 * ARC_STEPS})
        self.nsum_step = signal("nsum_step", {"arccos": PAIR * 2 * 3})
        self.vs_ready = signal("vs_ready", {"arccos": PAIR})
        self.lin_ps = signal("lin_ps", {f"block{i}": 2 for i in range(3)})
        self.gelu_ready = signal("gelu_ready", {f"block{i}": 1 for i in range(3)})
        self.lin_sum = signal("lin_sum", {"block2": 1})

    def inner(self, stage):
        return self.z if stage in ("mqa", "causal2") else self.x


def build(nc, x_dram, w_dram, qw_dram, out_dram):
    cols, width = columns()
    with ExitStack() as ctx:
        def sb(name, shape, dt=F32):
            return ctx.enter_context(nc.sbuf_tensor(name, shape, dt))

        def sem(name):
            return ctx.enter_context(nc.semaphore(name))

        skip = cols["const"][0]
        wts = sb("wts", [P, width - skip])
        weff = sb("weff", [P, 6 * P])
        ident_bf, mask_q, mask_k, before_bf, ones_bf = (
            sb(n, [P, P], BF16) for n in ("ident_bf", "mask_q", "mask_k", "before_bf", "ones_bf"))
        zero_bf = sb("zero_bf", [P, 1], BF16)
        max_rows = sb("max_rows", [P, GROUPS], F32R)
        front, back = Half(nc, ctx, "front", FRONT), Half(nc, ctx, "back", BACK)
        once = back.scratch[:, 0:skip]
        qint = back.scratch[:, skip:skip + 6 * P].bitcast(I32)

        def W(stage, name):
            at, n = cols[stage][2][name]
            return once[:, at:at + n] if stage in ONCE else wts[:, at - skip:at - skip + n]

        def C(name):
            return W("const", name)

        loaded = {s: sem(f"loaded_{s}") for s in STAGES}
        qint_loaded = sem("qint_loaded")
        consts_ready = sem("consts_ready")
        wait_carrier = sem("wait_carrier")
        dequant_step = sem("dequant_step")
        lora_ps = sem("lora_ps")
        weff_ready = sem("weff_ready")
        xin_loaded = sem("xin_loaded")
        out_stored = sem("out_stored")

        block = ctx.enter_context(nc.Block())

        def source(h, turn, n):
            kind, after = NORMS[n][4]
            sig = {"resid": h.resid, "norm_out": h.norm_out, "handed": front.resid}[kind]
            return sig.sem, sig.at(turn, after)

        def norm_pe(pe, h, turn, n, first=0):
            src, _, centred, _, _, gain = NORMS[n]
            yield first
            if centred:
                pe.wait_ge(*source(h, turn, n))
                nc.tensor.matmul(h.ps[:, 0, :], C("mean"), h.buf[src][:], start=True, stop=True)\
                    .then_inc(h.norm_mean.sem, 1)
            yield first + 1
            if gain:
                pe.wait_ge(loaded[gain], 16)
            pe.wait_ge(h.norm_sq.sem, h.norm_sq.at(turn, n))
            nc.tensor.matmul(h.ps[:, 1, :], C("mean"), h.sq[:], start=True, stop=True).then_inc(h.norm_var.sem, 1)

        def norm_act(act, h, turn, n, first=0):
            src, _, centred, eps, _, _ = NORMS[n]
            yield first
            if centred:
                act.wait_ge(h.norm_cen.sem, h.norm_cen.at(turn, n))
            else:
                act.wait_ge(*source(h, turn, n))
            nc.scalar.activation(h.sq[:], h.cen[:] if centred else h.buf[src][:], ACT.Square).then_inc(h.norm_sq.sem, 1)
            yield first + 1
            table(LN_EXP)
            act.wait_ge(h.norm_var.sem, h.norm_var.at(turn, n))
            nc.scalar.activation(h.sq[:], h.ps[:, 1, :], ACT.Ln, bias=C(eps)).then_inc(h.norm_ln.sem, 1)
            act.wait_ge(h.norm_ln.sem, h.norm_ln.at(turn, n))
            nc.scalar.activation(h.sq[:], h.sq[:], ACT.Exp, scale=-0.5).then_inc(h.norm_rstd.sem, 1)

        def norm_dve(dve, h, turn, n, first=0):
            src, dst, centred, _, _, gain = NORMS[n]
            yield first
            if n == "causal0":
                dve.wait_ge(h.resid.sem, h.resid.before(turn))
                dve.wait_ge(xin_loaded, turn.count(16, 16))
                nc.vector.tensor_copy(h.x[:], h.xin[:]).then_inc(h.resid.sem, 1)
            if n == "causal2_in":
                dve.wait_ge(out_stored, turn.count(16, 16))
            if centred:
                dve.wait_ge(*source(h, turn, n))
                dve.wait_ge(h.norm_mean.sem, h.norm_mean.at(turn, n))
                nc.vector.tensor_tensor(h.cen[:], h.buf[src][:], h.ps[:, 0, :], ALU.subtract).then_inc(h.norm_cen.sem, 1)
            yield first + 1
            dve.wait_ge(h.norm_rstd.sem, h.norm_rstd.at(turn, n))
            if centred:
                nc.vector.tensor_tensor(h.buf[dst][:], h.cen[:], h.sq[:], ALU.mult).then_inc(h.norm_out.sem, 1)
            else:
                nc.vector.scalar_tensor_tensor(out=h.buf[dst][:], in0=h.buf[src][:], scalar=W(gain, "g"), in1=h.sq[:],
                                               op0=ALU.mult, op1=ALU.mult).then_inc(h.norm_out.sem, 1)

        def rows(j, n):
            return slice(QUAD * j, QUAD * j + n)

        def values_pe(h, bank, w, n):
            for t in range(TILES):
                last = nc.tensor.matmul(h.ps[:, bank, t * n:(t + 1) * n], h.xn[:, t * P:(t + 1) * P], w,
                                        start=True, stop=True)
            last.then_inc(h.v_ps.sem, 1)

        def headed_project_pe(pe, h, turn, s):
            yield 0
            pe.wait_ge(loaded[s], 16)
            pe.wait_ge(h.norm_out.sem, h.norm_out.at(turn, s))
            for g in range(GROUPS):
                last = nc.tensor.matmul(h.ps[:, g, :], W(s, "q")[:, g * P:(g + 1) * P], h.xn[:], start=True, stop=True)
            last.then_inc(h.q_ps.sem, 1)
            yield 1
            pe.wait_ge(h.q_ready.sem, h.q_ready.at(turn, s))
            for g in range(GROUPS):
                last = nc.tensor.matmul(h.ps[:, g, :], W(s, "k")[:, g * P:(g + 1) * P], h.xn[:], start=True, stop=True)
            last.then_inc(h.k_ps.sem, 1)
            yield 2
            pe.wait_ge(h.k_ready.sem, h.k_ready.at(turn, s))
            values_pe(h, 0, W(s, "v"), P)

        def high_act(act, ps, high, sign, done):
            nc.scalar.activation(high.bitcast(F32R), ps, ACT.Copy, scale=C(sign)).then_inc(done.sem, 1)

        def split_dve(dve, ps, high, low, out, done):
            nc.vector.scalar_tensor_tensor(out=out, in0=ps, scalar=C(low), in1=high, op0=ALU.mult, op1=ALU.subtract)\
                .then_inc(done.sem, 1)

        def headed_project_act(act, h, turn, s):
            for i, (ps_sig, sign, high) in enumerate(((h.q_ps, "q_sign", h.q_high), (h.k_ps, "k_sign", h.k_high))):
                yield i
                act.wait_ge(ps_sig.sem, ps_sig.at(turn, s))
                if s == "linear":
                    nc.scalar.activation(h.rect, h.ps[:], ACT.Relu).then_inc(h.rect_ready.sem, 1)
                    act.wait_ge(h.rect_ready.sem, h.rect_ready.at(turn, s, i + 1))
                    high_act(act, h.rect, h.high, sign, high)
                else:
                    high_act(act, h.ps[:], h.high, sign, high)
            yield 2
            act.wait_ge(h.v_ps.sem, h.v_ps.at(turn, s))
            nc.scalar.activation(h.v9[:].rearrange("p t h d -> p (t h) d")[:, :, 0:HD],
                                 h.ps[:, 0, :].rearrange("p (h d) -> p h d", d=HD), ACT.Copy).then_inc(h.v_ready.sem, 1)

        def headed_project_dve(dve, h, turn, s):
            src = h.rect if s == "linear" else h.ps[:]
            yield 0
            dve.wait_ge(h.q_high.sem, h.q_high.at(turn, s))
            split_dve(dve, src, h.high, "q_low", h.q4r, h.q_ready)
            yield 1
            dve.wait_ge(h.k_high.sem, h.k_high.at(turn, s))
            split_dve(dve, src, h.high, "k_low", h.k4r, h.k_ready)

        def mset(m):
            b, part = m // 3, m % 3
            return (b, 0, P, 0, GROUPS) if part == 0 else (b, 1, SEQ, 2 * (part - 1), 2)

        def max_pe(pe, h, turn, s):
            for m in range(MSETS):
                yield PROJECT + m
                b, qt, keys, g0, ng = mset(m)
                if m == 0:
                    pe.wait_ge(h.q_ready.sem, h.q_ready.at(turn, s))
                    pe.wait_ge(h.k_ready.sem, h.k_ready.at(turn, s))
                    pe.wait_ge(h.v_ready.sem, h.v_ready.at(turn, s))
                else:
                    pe.wait_ge(h.max_done.sem, h.max_done.at(turn, s, m))
                for gi in range(ng):
                    for j in range(HPG):
                        nc.tensor.matmul(h.ps[:, j, gi * keys:(gi + 1) * keys],
                                         h.q4r[rows(j, QUAD), g0 + gi, b * SEQ + qt * P:b * SEQ + (qt + 1) * P],
                                         h.k4r[rows(j, QUAD), g0 + gi, b * SEQ:b * SEQ + keys],
                                         start=(gi == 0), stop=False, skip_group_check=True)
                for j in range(HPG):
                    diagonal = h.ps[:, j, :].rearrange("p (g k) -> p g k", k=keys)[:, :, keys - P:keys]
                    last = nc.tensor.matmul(diagonal, ident_bf[:], mask_q[:].unsqueeze(1).broadcast_to([P, ng, P]),
                                            start=False, stop=True, skip_group_check=True)
                last.then_inc(h.max_ps.sem, 1)
            yield PROJECT + MSETS
            pe.wait_ge(h.max_pair.sem, h.max_pair.at(turn, s))
            for t in range(TILES):
                last = nc.tensor.transpose(h.ps[:, 0, t * P:(t + 1) * P], h.negm[:, t, :], C("ident"))
            last.then_inc(h.negm_ps.sem, 1)

        def max_columns(h, tiles, i):
            return h.negm[:, tiles, :].rearrange("p t (j r) -> p t j r", r=QUAD)[:, :, :, 0:2 * GROUPS]\
                .rearrange("p t j (g i) -> p t j g i", i=2)[:, :, :, :, i]

        def max_act(act, h, turn, s):
            yield PROJECT + MSETS
            act.wait_ge(h.negm_ps.sem, h.negm_ps.at(turn, s))
            high_act(act, h.ps[:, 0, :], h.high[:, 0, :], "m_sign", h.negm_high)

        def max_dve(dve, h, turn, s):
            for m in range(MSETS):
                yield PROJECT + m
                b, qt, keys, g0, ng = mset(m)
                dve.wait_ge(h.max_ps.sem, h.max_ps.at(turn, s, m + 1))
                into = max_columns(h, slice(2 * b + qt, 2 * b + qt + 1), 0)[:, 0, :, g0:g0 + ng]
                nc.vector.tensor_reduce(into, h.ps[:].rearrange("p j (g k) -> p j g k", k=keys),
                                        AX.X, ALU.max, negate=True).then_inc(h.max_done.sem, 1)
            dve.wait_ge(h.max_done.sem, h.max_done.at(turn, s, MSETS))
            for t in range(TILES):
                last = nc.vector.tensor_copy(max_columns(h, slice(t, t + 1), 1)[:, 0], max_columns(h, slice(t, t + 1), 0)[:, 0])
            last.then_inc(h.max_pair.sem, 1)
            yield PROJECT + MSETS
            dve.wait_ge(h.negm_high.sem, h.negm_high.at(turn, s))
            split_dve(dve, h.ps[:, 0, :], h.high[:, 0, :], "m_low", h.maxTr[:, :], h.negm_ready)

        def scores_first(s):
            return PROJECT + MSETS + 1 if s in CAUSAL else PROJECT

        def diagonal_at(s, g, t):
            at = g * SEQ if s in CAUSAL and t == 0 else t * TOK + g * P + (TOK if s in CAUSAL else 0)
            return slice(at, at + P)

        def full_at(s, g):
            at = g * SEQ + P if s in CAUSAL else 2 * TOK + g * P
            return slice(at, at + P)

        def headed_scores_pe(pe, h, turn, s):
            for e in range(ESETS + 1):
                yield scores_first(s) + e
                if e < ESETS:
                    b, j = e % PAIR, e // PAIR
                    r = rows(j, QUAD)
                    if e > 0:
                        pe.wait_ge(h.probs_ready.sem, h.probs_ready.at(turn, s, e))
                        if s == "linear":
                            pe.wait_ge(h.full_ready.sem, h.full_ready.at(turn, s, e))
                    elif s in CAUSAL:
                        pe.wait_ge(h.negm_ready.sem, h.negm_ready.at(turn, s))
                    else:
                        pe.wait_ge(h.q_ready.sem, h.q_ready.at(turn, s))
                        pe.wait_ge(h.k_ready.sem, h.k_ready.at(turn, s))
                        pe.wait_ge(h.v_ready.sem, h.v_ready.at(turn, s))
                    tile0, tile1 = slice(b * SEQ, b * SEQ + P), slice(b * SEQ + P, (b + 1) * SEQ)
                    if s in CAUSAL:
                        for g in range(GROUPS):
                            minus_max = max_rows[r, g:g + 1].broadcast_to([QUAD, P])
                            out = h.ps[:, g // 2, g % 2 * SEQ:(g % 2 + 1) * SEQ]
                            nc.tensor.matmul(out, h.k4r[r, g, tile0], h.q4r[r, g, b * SEQ:(b + 1) * SEQ],
                                             start=(g % 2 == 0), stop=False, skip_group_check=True)
                            nc.tensor.matmul(out, minus_max, h.maxTr[r, b * SEQ:(b + 1) * SEQ],
                                             start=False, stop=False, skip_group_check=True)
                        for g in range(GROUPS):
                            minus_max = max_rows[r, g:g + 1].broadcast_to([QUAD, P])
                            out = h.ps[:, 2, g * P:(g + 1) * P]
                            nc.tensor.matmul(out, h.k4r[r, g, tile1], h.q4r[r, g, tile1],
                                             start=(g == 0), stop=False, skip_group_check=True)
                            nc.tensor.matmul(out, minus_max, h.maxTr[r, tile1],
                                             start=False, stop=False, skip_group_check=True)
                    else:
                        for bank, kt, qt in ((0, tile0, tile0), (1, tile1, tile1), (2, tile0, tile1)):
                            for g in range(GROUPS):
                                last = nc.tensor.matmul(h.ps[:, bank, g * P:(g + 1) * P], h.k4r[r, g, kt], h.q4r[r, g, qt],
                                                        start=True, stop=True, skip_group_check=True)
                    if s in CAUSAL:
                        for bank in range(2):
                            nc.tensor.matmul(h.ps[:, bank, :].rearrange("p (g q) -> p g q", q=SEQ)[:, :, 0:P], ident_bf[:],
                                             mask_k[:].unsqueeze(1).broadcast_to([P, 2, P]),
                                             start=False, stop=True, skip_group_check=True)
                        last = nc.tensor.matmul(h.ps[:, 2, :].rearrange("p (g q) -> p g q", q=P), ident_bf[:],
                                                mask_k[:].unsqueeze(1).broadcast_to([P, GROUPS, P]),
                                                start=False, stop=True, skip_group_check=True)
                    last.then_inc(h.score_ps.sem, 1)
                if e > 0:
                    headed_pv_pe(pe, h, turn, s, e - 1)

        def clear_ps(bank):
            nc.tensor.matmul(bank, ident_bf[:], zero_bf[:].broadcast_to([P, TOK]), start=True, stop=False,
                             skip_group_check=True)

        def headed_pv_pe(pe, h, turn, s, e):
            b, j = e % PAIR, e // PAIR
            pe.wait_ge(h.probs_ready.sem, h.probs_ready.at(turn, s, e + 1))
            if s == "linear":
                pe.wait_ge(h.full_ready.sem, h.full_ready.at(turn, s, e + 1))
            if b == 0:
                if j > 0:
                    pe.wait_ge(h.part_ready.sem, h.part_ready.at(turn, s, j))
                clear_ps(h.ps[:, 3, :])
            pw = h.probs[:, e % 2, :]
            for g in range(GROUPS):
                hd = HPG * g + j
                out = h.ps[rows(g, V1), 3, b * SEQ:(b + 1) * SEQ]
                first, second = h.v9[:, 2 * b, hd, :], h.v9[:, 2 * b + 1, hd, :]
                if s in CAUSAL:
                    nc.tensor.matmul(out, first, pw[:, g * SEQ:(g + 1) * SEQ], start=False, stop=False,
                                     skip_group_check=True)
                else:
                    nc.tensor.matmul(out[:, 0:P], first, pw[:, diagonal_at(s, g, 0)], start=False, stop=False,
                                     skip_group_check=True)
                    nc.tensor.matmul(out[:, P:SEQ], first, pw[:, full_at(s, g)], start=False, stop=False,
                                     skip_group_check=True)
                last = nc.tensor.matmul(out[:, P:SEQ], second, pw[:, diagonal_at(s, g, 1)], start=False, stop=True,
                                        skip_group_check=True)
            last.then_inc(h.pv_ps.sem, 1)

        def headed_exp_act(act, h, turn, s):
            for e in range(ESETS):
                yield scores_first(s) + e
                table(LN_EXP)
                act.wait_ge(h.score_ps.sem, h.score_ps.at(turn, s, e + 1))
                if e >= 2:
                    act.wait_ge(h.pv_ps.sem, h.pv_ps.at(turn, s, e - 1))
                nc.scalar.activation(h.probs[:, e % 2, :].rearrange("p (b c) -> p b c", b=3), h.ps[:, 0:3, :], ACT.Exp,
                                     scale=float(HD) ** -0.5).then_inc(h.probs_ready.sem, 1)

        def linear_full_act(act, h, turn, s):
            for e in range(ESETS):
                yield scores_first(s) + e
                act.wait_ge(h.score_ps.sem, h.score_ps.at(turn, s, e + 1))
                if e >= 2:
                    act.wait_ge(h.pv_ps.sem, h.pv_ps.at(turn, s, e - 1))
                nc.scalar.activation(h.probs[:, e % 2, 2 * TOK:], h.ps[:, 2, :], ACT.Copy).then_inc(h.full_ready.sem, 1)

        def linear_mask_dve(dve, h, turn, s):
            keep = C("keep_k").unsqueeze(1).broadcast_to([P, 2 * GROUPS, P])
            for e in range(ESETS):
                yield scores_first(s) + e
                dve.wait_ge(h.score_ps.sem, h.score_ps.at(turn, s, e + 1))
                if e >= 2:
                    dve.wait_ge(h.pv_ps.sem, h.pv_ps.at(turn, s, e - 1))
                nc.vector.tensor_tensor(h.probs[:, e % 2, 0:2 * TOK].rearrange("p (n q) -> p n q", q=P),
                                        h.ps[:, 0:2, :].rearrange("p b (g q) -> p (b g) q", q=P), keep, ALU.mult)\
                    .then_inc(h.probs_ready.sem, 1)
                if e >= PAIR and e % PAIR == 0:
                    headed_part_dve(dve, h, turn, s, e // PAIR - 1)

        def headed_part_dve(dve, h, turn, s, j):
            dve.wait_ge(h.pv_ps.sem, h.pv_ps.at(turn, s, PAIR * (j + 1)))
            nc.vector.tensor_copy(h.parts[s][j], h.ps[:, 3, :]).then_inc(h.part_ready.sem, 1)

        def heads_out_pe(pe, h, turn, s, first):
            yield first
            pe.wait_ge(h.part_ready.sem, h.part_ready.at(turn, s, len(h.parts[s]) if s != "arccos" else PAIR))
            for j in range(HPG):
                last = nc.tensor.matmul(h.ps[:, j, :], C("den"), h.parts[s][j], start=True, stop=True)
            last.then_inc(h.den_ps.sem, 1)
            yield first + 1
            pe.wait_ge(h.y_ready.sem, h.y_ready.at(turn, s))
            for j in range(HPG):
                last = nc.tensor.matmul(h.ps[:, 0, :], C("dense")[:, j * P:(j + 1) * P], h.parts[s][j],
                                        start=(j == 0), stop=(j == HPG - 1))
            last.then_inc(h.yT_ps.sem, 1)
            yield first + 2
            pe.wait_ge(h.yT_ready.sem, h.yT_ready.at(turn, s))
            nc.tensor.matmul(h.ps[:, 1, :], W(s, "o"), h.xn[:], start=True, stop=True).then_inc(h.o_ps.sem, 1)

        def heads_out_act(act, h, turn, s, first):
            yield first
            table(LN_EXP)
            act.wait_ge(h.den_ps.sem, h.den_ps.at(turn, s))
            if s == "linear":
                nc.scalar.activation(h.rden4[s], h.ps[:], ACT.Ln, bias=C("lin_eps")).then_inc(h.den_ln.sem, 1)
            else:
                nc.scalar.activation(h.rden4[s], h.ps[:], ACT.Ln).then_inc(h.den_ln.sem, 1)
            act.wait_ge(h.den_ln.sem, h.den_ln.at(turn, s))
            nc.scalar.activation(h.rden4[s], h.rden4[s], ACT.Exp, scale=-1.0).then_inc(h.rden_ready.sem, 1)
            yield first + 1
            act.wait_ge(h.yT_ps.sem, h.yT_ps.at(turn, s))
            nc.scalar.activation(h.xn[:], h.ps[:, 0, :], ACT.Copy).then_inc(h.yT_ready.sem, 1)

        def heads_out_dve(dve, h, turn, s, first):
            yield first
            dve.wait_ge(h.rden_ready.sem, h.rden_ready.at(turn, s))
            for j in range(HPG):
                last = nc.vector.tensor_tensor(h.parts[s][j], h.parts[s][j], h.rden4[s][:, j, :], ALU.mult)
            last.then_inc(h.y_ready.sem, 1)
            yield from residual_dve(dve, h, turn, s, first + 2)

        def residual_dve(dve, h, turn, s, first):
            yield first
            dve.wait_ge(h.o_ps.sem, h.o_ps.at(turn, s))
            r = h.inner(s)
            if s == "arccos":
                nc.vector.scalar_tensor_tensor(out=r[:], in0=h.ps[:, 1, :], scalar=W(s, "bo"), in1=r[:],
                                               op0=ALU.add, op1=ALU.add).then_inc(h.resid.sem, 1)
            else:
                nc.vector.tensor_tensor(r[:], r[:], h.ps[:, 1, :], ALU.add).then_inc(h.resid.sem, 1)

        def headed_pe(pe, h, turn, s):
            yield from headed_project_pe(pe, h, turn, s)
            if s in CAUSAL:
                yield from max_pe(pe, h, turn, s)
            yield from headed_scores_pe(pe, h, turn, s)
            yield from heads_out_pe(pe, h, turn, s, scores_first(s) + ESETS + 1)

        def headed_act(act, h, turn, s):
            yield from headed_project_act(act, h, turn, s)
            if s in CAUSAL:
                yield from max_act(act, h, turn, s)
                yield from headed_exp_act(act, h, turn, s)
            else:
                yield from linear_full_act(act, h, turn, s)
            yield from heads_out_act(act, h, turn, s, scores_first(s) + ESETS + 1)

        def headed_dve(dve, h, turn, s):
            yield from headed_project_dve(dve, h, turn, s)
            if s in CAUSAL:
                yield from max_dve(dve, h, turn, s)
                for j in range(HPG - 1):
                    yield scores_first(s) + PAIR * (j + 1)
                    headed_part_dve(dve, h, turn, s, j)
            else:
                yield from linear_mask_dve(dve, h, turn, s)
            yield scores_first(s) + ESETS
            headed_part_dve(dve, h, turn, s, HPG - 1)
            yield from heads_out_dve(dve, h, turn, s, scores_first(s) + ESETS + 1)

        def mqa_norm_dve(dve, h, turn, s, b):
            heads, dims = MQH, MQD
            dve.wait_ge(h.pv_ps.sem, h.pv_ps.at(turn, s, QSETS // PAIR * (b + 1)))
            o = h.ps[:, 3, 0:2 * heads * (dims + 1)].rearrange("p (h d) -> p h d", d=dims + 1)
            r = h.rden[:, b, :].unsqueeze(2)
            nc.vector.tensor_copy(r, o[:, :, dims:]).then_inc(h.den_step.sem, 1)
            dve.wait_ge(h.den_step.sem, h.den_step.at(turn, s, 2 * b + 1))
            nc.vector.reciprocal(r, r).then_inc(h.den_step.sem, 1)
            dve.wait_ge(h.den_step.sem, h.den_step.at(turn, s, 2 * b + 2))
            nc.vector.tensor_tensor(h.ytok[:, 2 * b:2 * b + 2, :].rearrange("p t (h d) -> p (t h) d", d=dims),
                                    o[:, :, 0:dims], r.broadcast_to([P, 2 * heads, dims]), ALU.mult)\
                .then_inc(h.y_ready.sem, 1)

        def mqa_out_pe(pe, h, turn, s, first):
            yield first
            pe.wait_ge(h.y_ready.sem, h.y_ready.at(turn, s, PAIR))
            for t in range(TILES):
                last = nc.tensor.transpose(h.ps[:, 0, t * P:(t + 1) * P], h.ytok[:, t, :], C("ident"))
            last.then_inc(h.yT_ps.sem, 1)
            yield first + 1
            pe.wait_ge(h.yT_ready.sem, h.yT_ready.at(turn, s))
            nc.tensor.matmul(h.ps[:, 1, :], W(s, "o"), h.xn[:], start=True, stop=True).then_inc(h.o_ps.sem, 1)

        def mqa_out_act(act, h, turn, s, first):
            yield first
            act.wait_ge(h.yT_ps.sem, h.yT_ps.at(turn, s))
            nc.scalar.activation(h.xn[:], h.ps[:, 0, :], ACT.Copy).then_inc(h.yT_ready.sem, 1)

        M_FIRST, Q_FIRST = 1, 1 + TILES + 1

        def mqa_pe(pe, h, turn, s):
            yield 0
            pe.wait_ge(loaded[s], 16)
            pe.wait_ge(h.norm_out.sem, h.norm_out.at(turn, s))
            nc.tensor.matmul(h.ps[:, 0, :], W(s, "q"), h.xn[:], start=True, stop=True).then_inc(h.q_ps.sem, 1)
            nc.tensor.matmul(h.ps[:, 1, :], W(s, "k"), h.xn[:], start=True, stop=True).then_inc(h.k_ps.sem, 1)
            values_pe(h, 2, W(s, "v"), MQD)
            for m in range(TILES):
                yield M_FIRST + m
                if m == 0:
                    pe.wait_ge(h.q_ready.sem, h.q_ready.at(turn, s))
                    pe.wait_ge(h.k_ready.sem, h.k_ready.at(turn, s))
                    pe.wait_ge(h.v_ready.sem, h.v_ready.at(turn, s))
                else:
                    pe.wait_ge(h.max_done.sem, h.max_done.at(turn, s, m))
                for j in range(MQH):
                    last = nc.tensor.matmul(h.ps[:, j, 0:SEQ], h.q4[rows(j, MQD), 0, m * P:(m + 1) * P],
                                            h.k4[rows(j, MQD), 0, m // 2 * SEQ:(m // 2 + 1) * SEQ],
                                            start=True, stop=True)
                last.then_inc(h.max_ps.sem, 1)
            yield M_FIRST + TILES
            pe.wait_ge(h.max_done.sem, h.max_done.at(turn, s, TILES))
            for t in range(TILES):
                last = nc.tensor.transpose(h.ps[:, 0, t * P:(t + 1) * P], h.negm[:, t, :], C("ident"))
            last.then_inc(h.negm_ps.sem, 1)
            for e in range(QSETS + 1):
                yield Q_FIRST + e
                if e < QSETS:
                    b, jp = e // 2, e % 2
                    if e == 0:
                        pe.wait_ge(h.negm_ready.sem, h.negm_ready.at(turn, s))
                    else:
                        pe.wait_ge(h.probs_ready.sem, h.probs_ready.at(turn, s, e))
                    qs = slice(b * SEQ, (b + 1) * SEQ)
                    for kt in range(2):
                        for i in range(2):
                            r = rows(2 * jp + i, MQD)
                            o = h.ps[:, i, kt * SEQ:(kt + 1) * SEQ]
                            nc.tensor.matmul(o, h.k4[r, 0, b * SEQ + kt * P:b * SEQ + (kt + 1) * P], h.q4[r, 0, qs],
                                             start=True, stop=False, skip_group_check=True)
                            last = nc.tensor.matmul(o, C("head_row")[r, :].broadcast_to([MQD, P]), h.maxT[r, qs],
                                                    start=False, stop=True, skip_group_check=True)
                    last.then_inc(h.score_ps.sem, 1)
                if e > 0:
                    b, jp = (e - 1) // 2, (e - 1) % 2
                    pe.wait_ge(h.probs_ready.sem, h.probs_ready.at(turn, s, e))
                    if e - 1 == 2:
                        pe.wait_ge(h.y_ready.sem, h.y_ready.at(turn, s, 1))
                    for i in range(2):
                        for qt in range(2):
                            c = (qt * MQH + 2 * jp + i) * MV1
                            for kt in range(2):
                                w = (i * 2 + kt) * SEQ + qt * P
                                last = nc.tensor.matmul(h.ps[:, 3, c:c + MV1], h.probs[:, (e - 1) % 2, w:w + P],
                                                        h.v33[:, 2 * b + kt, :], start=(kt == 0), stop=(kt == 1),
                                                        skip_group_check=True)
                    last.then_inc(h.pv_ps.sem, 1)
            yield from mqa_out_pe(pe, h, turn, s, Q_FIRST + QSETS + 1)

        def mqa_act(act, h, turn, s):
            yield 0
            act.wait_ge(h.q_ps.sem, h.q_ps.at(turn, s))
            nc.scalar.activation(h.q4[:, 0, :], h.ps[:, 0, :], ACT.Copy, scale=float(MQD) ** -0.5)\
                .then_inc(h.q_ready.sem, 1)
            act.wait_ge(h.v_ps.sem, h.v_ps.at(turn, s))
            nc.scalar.activation(h.v33[:, :, 0:MQD], h.ps[:, 2, 0:TILES * MQD].rearrange("p (t d) -> p t d", d=MQD),
                                 ACT.Copy).then_inc(h.v_ready.sem, 1)
            for e in range(QSETS):
                yield Q_FIRST + e
                table(LN_EXP)
                act.wait_ge(h.score_ps.sem, h.score_ps.at(turn, s, e + 1))
                if e >= 2:
                    act.wait_ge(h.pv_ps.sem, h.pv_ps.at(turn, s, e - 1))
                nc.scalar.activation(h.probs[:, e % 2, 0:2 * TOK].rearrange("p (b c) -> p b c", b=2), h.ps[:, 0:2, :],
                                     ACT.Exp).then_inc(h.probs_ready.sem, 1)
            yield from mqa_out_act(act, h, turn, s, Q_FIRST + QSETS + 1)

        def mqa_dve(dve, h, turn, s):
            yield 0
            dve.wait_ge(h.k_ps.sem, h.k_ps.at(turn, s))
            nc.vector.tensor_copy(h.k4[:, 0, :], h.ps[:, 1, :]).then_inc(h.k_ready.sem, 1)
            for m in range(TILES):
                yield M_FIRST + m
                dve.wait_ge(h.max_ps.sem, h.max_ps.at(turn, s, m + 1))
                nc.vector.tensor_reduce(max_columns(h, slice(m, m + 1), 0)[:, 0, :, 0],
                                        h.ps[:, :, 0:SEQ], AX.X, ALU.max, negate=True).then_inc(h.max_done.sem, 1)
            yield M_FIRST + TILES
            dve.wait_ge(h.negm_ps.sem, h.negm_ps.at(turn, s))
            nc.vector.tensor_copy(h.maxT[:, :], h.ps[:, 0, :]).then_inc(h.negm_ready.sem, 1)
            for b in range(PAIR):
                yield Q_FIRST + 2 * (b + 1)
                mqa_norm_dve(dve, h, turn, s, b)
            yield from residual_dve(dve, h, turn, s, Q_FIRST + QSETS + 2)

        HEADS_FIRST = 2
        SEQ_ROUNDS = ASETS + ARC_STEPS + 2

        def seq_first(b):
            return HEADS_FIRST + 2 + SEQ_ROUNDS * b

        ARC_OUT = seq_first(PAIR)

        def arccos_pe(pe, h, turn, s):
            yield 0
            pe.wait_ge(loaded[s], 16)
            pe.wait_ge(h.norm_out.sem, h.norm_out.at(turn, s))
            nc.tensor.matmul(h.ps[:, 0, :], W(s, "q"), h.xn[:], start=True, stop=True).then_inc(h.q_ps.sem, 1)
            nc.tensor.matmul(h.ps[:, 1, :], W(s, "k"), h.xn[:], start=True, stop=True).then_inc(h.k_ps.sem, 1)
            values_pe(h, 2, W(s, "v"), P)
            yield 1
            for i, (bank, square) in enumerate(((3, h.sq), (0, h.cen))):
                pe.wait_ge(h.arc_sq.sem, h.arc_sq.at(turn, s, i + 1))
                nc.tensor.matmul(h.ps[:, bank, :], C("blk8"), square[:], start=True, stop=True).then_inc(h.arc_norm_ps.sem, 1)
            for i, unit in enumerate((h.y, h.z)):
                yield HEADS_FIRST + i
                pe.wait_ge(h.arc_unit.sem, h.arc_unit.at(turn, s, i + 1))
                if i == 0:
                    pe.wait_ge(h.v_ready.sem, h.v_ready.at(turn, s))
                    pe.wait_ge(h.arc_floor.sem, h.arc_floor.at(turn, s, 2))
                else:
                    pe.wait_ge(h.q_ready.sem, h.q_ready.at(turn, s))
                for g in range(GROUPS):
                    last = nc.tensor.matmul(h.ps[:, g, :], C("esel")[:, g * P:(g + 1) * P], unit[:], start=True, stop=True)
                last.then_inc(h.head_ps.sem, 1)
            for b in range(PAIR):
                for a in range(ASETS):
                    yield seq_first(b) + a
                    kt, gp = a // 2, a % 2
                    if a > 0:
                        pe.wait_ge(h.cos_ready.sem, h.cos_ready.at(turn, s, ASETS * b + a))
                    elif b == 0:
                        pe.wait_ge(h.q_ready.sem, h.q_ready.at(turn, s))
                        pe.wait_ge(h.k_ready.sem, h.k_ready.at(turn, s))
                    else:
                        pe.wait_ge(h.part_ready.sem, h.part_ready.at(turn, s, b))
                    for g2 in range(2):
                        for j in range(HPG):
                            r = rows(j, QUAD)
                            last = nc.tensor.matmul(
                                h.ps[:, j, g2 * SEQ:(g2 + 1) * SEQ],
                                h.k4r[r, 2 * gp + g2, b * SEQ + kt * P:b * SEQ + (kt + 1) * P],
                                h.q4r[r, 2 * gp + g2, b * SEQ:(b + 1) * SEQ], start=True, stop=True, skip_group_check=True)
                    last.then_inc(h.score_ps.sem, 1)
                yield seq_first(b) + SEQ_ROUNDS - 1
                pe.wait_ge(h.vs_ready.sem, h.vs_ready.at(turn, s, b + 1))
                for j in range(HPG):
                    if j % 2 == 0:
                        clear_ps(h.ps[:, 2 + j // 2, :])
                    for kt in range(2):
                        for g in range(GROUPS):
                            w = (((kt * 2 + g // 2) * HPG + j) * 2 + g % 2) * SEQ
                            last = nc.tensor.matmul(h.ps[rows(g, V1), 2 + j // 2, j % 2 * SEQ:(j % 2 + 1) * SEQ],
                                                    h.vs[:, kt, HPG * g + j, :], h.cosines[:, w:w + SEQ],
                                                    start=False, stop=(kt == 1), skip_group_check=True)
                last.then_inc(h.pv_ps.sem, 1)
            yield from heads_out_pe(pe, h, turn, s, ARC_OUT)

        def arccos_act(act, h, turn, s):
            yield 0
            for i, (bias, ps_sig, raw, square) in enumerate((("bq", h.q_ps, h.y, h.sq), ("bk", h.k_ps, h.z, h.cen))):
                act.wait_ge(ps_sig.sem, ps_sig.at(turn, s))
                nc.scalar.activation(raw[:], h.ps[:, i, :], ACT.Identity, bias=W(s, bias)).then_inc(h.arc_raw.sem, 1)
                act.wait_ge(h.arc_raw.sem, h.arc_raw.at(turn, s, i + 1))
                nc.scalar.activation(square[:], raw[:], ACT.Square).then_inc(h.arc_sq.sem, 1)
            yield 1
            table(LN_EXP)
            for i, rn in enumerate((h.sq, h.xn)):
                act.wait_ge(h.arc_floor.sem, h.arc_floor.at(turn, s, i + 1))
                nc.scalar.activation(rn[:], rn[:], ACT.Ln, scale=float(2 ** 20)).then_inc(h.arc_ln.sem, 1)
                act.wait_ge(h.arc_ln.sem, h.arc_ln.at(turn, s, i + 1))
                nc.scalar.activation(rn[:], rn[:], ACT.Exp, scale=-0.5, bias=C("ln1024")).then_inc(h.arc_rn.sem, 1)
            for i, (sign, high) in enumerate((("q_sign", h.q_high), ("k_sign", h.k_high))):
                yield HEADS_FIRST + i
                act.wait_ge(h.head_ps.sem, h.head_ps.at(turn, s, i + 1))
                high_act(act, h.ps[:], h.high, sign, high)
            steps = [(ACT.Ln, 0.5, "half", LN_EXP), (ACT.Tanh, -0.25, None, None), (ACT.Sqrt, 1.0, None, None),
                     (ACT.Arctan, 1.0, None, None), (ACT.Ln, 4.0, "one", LN_EXP), (ACT.Exp, GEO_POWER, None, LN_EXP)]
            for b in range(PAIR):
                for n, (func, scale, bias, in_table) in enumerate(steps):
                    yield seq_first(b) + ASETS + n
                    table(in_table)
                    for kt in range(2):
                        half = h.cosines[:, kt * HEADS * SEQ:(kt + 1) * HEADS * SEQ]
                        k = (b * ARC_STEPS + n) * 2 + kt
                        if n == 0:
                            act.wait_ge(h.cos_ready.sem, h.cos_ready.at(turn, s, ASETS * b + 2 * kt + 2))
                        else:
                            act.wait_ge(h.arc_pass.sem, h.arc_pass.at(turn, s, k - 1))
                        if bias is None:
                            ins = nc.scalar.activation(half, half, func, scale=scale)
                        else:
                            ins = nc.scalar.activation(half, half, func, scale=scale, bias=C(bias))
                        ins.then_inc(h.arc_pass.sem, 1)
            yield from heads_out_act(act, h, turn, s, ARC_OUT)

        def arccos_dve(dve, h, turn, s):
            yield 0
            dve.wait_ge(h.v_ps.sem, h.v_ps.at(turn, s))
            nc.vector.tensor_tensor(h.v9[:, :, :, 0:HD].rearrange("p t h d -> p (t h) d"),
                                    h.ps[:, 2, :].rearrange("p (h d) -> p h d", d=HD),
                                    W(s, "bv").unsqueeze(1).broadcast_to([P, TILES, P])
                                    .rearrange("p t (h d) -> p t h d", d=HD), ALU.add).then_inc(h.v_ready.sem, 1)
            yield 1
            for i, (bank, rn) in enumerate(((3, h.sq), (0, h.xn))):
                dve.wait_ge(h.arc_norm_ps.sem, h.arc_norm_ps.at(turn, s, i + 1))
                nc.vector.tensor_scalar(rn[:], h.ps[:, bank, :], 1e-24, None, ALU.max).then_inc(h.arc_floor.sem, 1)
            for i, (raw, rn) in enumerate(((h.y, h.sq), (h.z, h.xn))):
                dve.wait_ge(h.arc_rn.sem, h.arc_rn.at(turn, s, i + 1))
                nc.vector.tensor_tensor(raw[:], raw[:], rn[:], ALU.mult).then_inc(h.arc_unit.sem, 1)
            yield HEADS_FIRST
            dve.wait_ge(h.q_high.sem, h.q_high.at(turn, s))
            split_dve(dve, h.ps[:], h.high, "q_low", h.q4r, h.q_ready)
            yield HEADS_FIRST + 1
            dve.wait_ge(h.k_high.sem, h.k_high.at(turn, s))
            split_dve(dve, h.ps[:], h.high, "k_low", h.k4r, h.k_ready)
            for b in range(PAIR):
                for a in range(ASETS):
                    yield seq_first(b) + a
                    dve.wait_ge(h.score_ps.sem, h.score_ps.at(turn, s, ASETS * b + a + 1))
                    if b > 0:
                        dve.wait_ge(h.pv_ps.sem, h.pv_ps.at(turn, s, b))
                    nc.vector.tensor_scalar(h.cosines[:, a * 4 * TOK:(a + 1) * 4 * TOK].rearrange("p (j t) -> p j t", j=HPG),
                                            h.ps[:], CLIP, CLIP_LO, ALU.min, ALU.max).then_inc(h.cos_ready.sem, 1)
                for kt in range(2):
                    yield seq_first(b) + ASETS + ARC_STEPS - 1 + kt
                    n = (2 * b + kt) * 3
                    dve.wait_ge(h.arc_pass.sem, h.arc_pass.at(turn, s, (b * ARC_STEPS + ARC_STEPS - 1) * 2 + kt + 1))
                    for gp in range(2):
                        at = (kt * HEADS + 8 * gp) * SEQ
                        nc.vector.tensor_reduce(
                            h.nsum[:, kt, 8 * gp:8 * gp + 8].rearrange("p (g2 j) -> p j g2", g2=2),
                            h.cosines[:, at:at + 8 * SEQ].rearrange("p (j g2 q) -> p j g2 q", g2=2, q=SEQ),
                            AX.X, ALU.add).then_inc(h.nsum_step.sem, 1)
                    dve.wait_ge(h.nsum_step.sem, h.nsum_step.at(turn, s, n + 2))
                    nc.vector.reciprocal(h.nsum[:, kt, :], h.nsum[:, kt, :]).then_inc(h.nsum_step.sem, 1)
                    dve.wait_ge(h.nsum_step.sem, h.nsum_step.at(turn, s, n + 3))
                    dve.wait_ge(h.v_ready.sem, h.v_ready.at(turn, s))
                    last = nc.vector.tensor_tensor(h.vs[:, kt, :, :], h.v9[:, 2 * b + kt, :, :],
                                                   h.nsum[:, kt, :].unsqueeze(2).broadcast_to([P, HEADS, V1]), ALU.mult)
                last.then_inc(h.vs_ready.sem, 1)
                yield seq_first(b) + SEQ_ROUNDS - 1
                dve.wait_ge(h.pv_ps.sem, h.pv_ps.at(turn, s, b + 1))
                for j in range(HPG):
                    last = nc.vector.tensor_copy(h.parts[s][j][:, b * SEQ:(b + 1) * SEQ],
                                                 h.ps[:, 2 + j // 2, j % 2 * SEQ:(j % 2 + 1) * SEQ])
                last.then_inc(h.part_ready.sem, 1)
            yield from heads_out_dve(dve, h, turn, s, ARC_OUT)

        def router_pe(pe, h, turn, s):
            yield 0
            pe.wait_ge(h.norm_out.sem, h.norm_out.at(turn, s))
            pe.wait_ge(loaded[s], 16)
            for t in range(TILES):
                last = nc.tensor.matmul(h.ps[:, 0, t * EXPERTS:(t + 1) * EXPERTS], h.xn[:, t * P:(t + 1) * P],
                                        W(s, "router"), start=True, stop=True)
            last.then_inc(h.logits_ps.sem, 1)
            if s == "moe0":
                yield 2
                pe.wait_ge(h.chosen_ready.sem, h.chosen_ready.at(turn, s))
                for t in range(TILES):
                    o = h.ps[:, 1, t * EXPERTS:(t + 1) * EXPERTS]
                    last = nc.tensor.matmul(o, before_bf[:], h.ohs_bf[:, t, :], start=True, stop=(t % 2 == 0),
                                            skip_group_check=True)
                    if t % 2:
                        last = nc.tensor.matmul(o, ones_bf[:], h.ohs_bf[:, t - 1, :], start=False, stop=True,
                                                skip_group_check=True)
                last.then_inc(h.place_ps.sem, 1)
            n = 1 if s == "mlp" else EXPERTS
            for e in range(n):
                if e % BANKS == 0:
                    yield 2 if s == "mlp" else 3 + e // BANKS
                    if e == 0:
                        pe.wait_ge(h.weight_ready.sem, h.weight_ready.at(turn, s))
                    else:
                        pe.wait_ge(h.wbc_ready.sem, h.wbc_ready.at(turn, s))
                for t in range(TILES):
                    last = nc.tensor.matmul(h.ps[:, e % BANKS if n > 1 else 3, t * P:(t + 1) * P],
                                            h.wtok[:, t, e:e + 1].broadcast_to([P, P]), C("ident"), start=True, stop=True)
                if e % BANKS == BANKS - 1 or e == n - 1:
                    last.then_inc(h.wbc_ps.sem, 1)

        def router_act(act, h, turn, s):
            yield 0
            table(LN_EXP)
            act.wait_ge(h.route_shift.sem, h.route_shift.at(turn, s))
            nc.scalar.activation(h.pr[:], h.lg[:], ACT.Exp).then_inc(h.route_exp.sem, 1)
            if s == "moe1":
                yield 1
                table(LN_EXP)
                act.wait_ge(h.gap_ready.sem, h.gap_ready.at(turn, s))
                nc.scalar.activation(h.s2[:], h.s1[:], ACT.Exp).then_inc(h.gap_exp.sem, 1)
            if s == "mlp":
                yield 2
                act.wait_ge(h.wbc_ps.sem, h.wbc_ps.at(turn, s))
                nc.scalar.activation(h.wbc[:, 0, :], h.ps[:, 3, :], ACT.Copy).then_inc(h.wbc_ready.sem, 1)
            else:
                yield 3
                act.wait_ge(h.wbc_ps.sem, h.wbc_ps.at(turn, s))
                nc.scalar.activation(h.wbc[:, 0:BANKS, :], h.ps[:], ACT.Copy).then_inc(h.wbc_ready.sem, 1)

        def router_dve(dve, h, turn, s):
            n = 0

            def step(ins, then_max=False):
                nonlocal n
                n += 1
                ins.then_inc(h.route_step.sem, 1)
                dve.wait_ge(h.route_step.sem, h.route_step.at(turn, s, n))
                if then_max:
                    dve.sem_inc(wait_carrier)

            full = [P, TILES, EXPERTS]
            lg, pr, t8, s1, s2, s3, s4, wtok = h.lg, h.pr, h.t8, h.s1, h.s2, h.s3, h.s4, h.wtok
            yield 0
            dve.wait_ge(h.logits_ps.sem, h.logits_ps.at(turn, s))
            logits = h.ps[:, 0, 0:TILES * EXPERTS].rearrange("p (t e) -> p t e", e=EXPERTS)
            if s == "mlp":
                step(nc.vector.tensor_copy(lg[:], logits))
            else:
                step(nc.vector.tensor_tensor(lg[:], logits, W(s, "rbias").unsqueeze(1).broadcast_to(full), ALU.add))
            step(nc.vector.tensor_reduce(s1[:], lg[:], AX.X, ALU.max, negate=True))
            nc.vector.tensor_tensor(lg[:], lg[:], s1[:].broadcast_to(full), ALU.add).then_inc(h.route_shift.sem, 1)
            yield 1
            dve.wait_ge(h.route_exp.sem, h.route_exp.at(turn, s))
            step(nc.vector.tensor_reduce(s1[:], pr[:], AX.X, ALU.add))
            step(nc.vector.reciprocal(s2[:], s1[:]))
            step(nc.vector.tensor_tensor(pr[:], pr[:], s2[:].broadcast_to(full), ALU.mult), then_max=True)
            for t in range(TILES):
                nc.vector.max(t8[:, t, :], pr[:, t, :]).then_inc(h.route_step.sem, 1)
            n += TILES
            dve.wait_ge(h.route_step.sem, h.route_step.at(turn, s, n))
            dve.sem_inc(wait_carrier)
            first, second = t8[:, :, 0:1], t8[:, :, 1:2]
            if s == "mlp":
                step(nc.vector.tensor_tensor(s1[:], first, second, ALU.add))
                step(nc.vector.tensor_scalar(s2[:], s1[:], 1e-9, None, ALU.add))
                step(nc.vector.reciprocal(s3[:], s2[:]))
                step(nc.vector.tensor_tensor(s4[:], first, s3[:], ALU.mult))
                step(nc.vector.tensor_tensor(s2[:], second, s3[:], ALU.mult))
                nc.vector.tensor_tensor(wtok[:, :, 0:1], s4[:], s2[:], ALU.add).then_inc(h.weight_ready.sem, 1)
                return
            for t in range(TILES):
                nc.vector.max_index(h.ix[:, t, :], t8[:, t, :], pr[:, t, :]).then_inc(h.route_step.sem, 1)
            n += TILES
            dve.wait_ge(h.route_step.sem, h.route_step.at(turn, s, n))
            step(nc.vector.tensor_copy(h.ixf[:], h.ix[:]))
            iota = C("iota").unsqueeze(1).broadcast_to(full)
            step(nc.vector.tensor_tensor(h.oh1[:], iota, h.ixf[:, :, 0:1].broadcast_to(full), ALU.is_equal))
            step(nc.vector.tensor_tensor(h.oh2[:], iota, h.ixf[:, :, 1:2].broadcast_to(full), ALU.is_equal))
            if s == "moe0":
                step(nc.vector.tensor_tensor(h.ohs[:], h.oh1[:], h.oh2[:], ALU.add))
                nc.vector.tensor_copy(h.ohs_bf[:], h.ohs[:]).then_inc(h.chosen_ready.sem, 1)
                step(nc.vector.tensor_tensor(wtok[:], h.ohs[:], pr[:], ALU.mult))
                yield 2
                dve.wait_ge(h.place_ps.sem, h.place_ps.at(turn, s))
                place = h.ps[:, 1, 0:TILES * EXPERTS].rearrange("p (t e) -> p t e", e=EXPERTS)
                nc.vector.scalar_tensor_tensor(out=wtok[:], in0=place, scalar=float(CAP), in1=wtok[:],
                                               op0=ALU.is_lt, op1=ALU.mult).then_inc(h.weight_ready.sem, 1)
            else:
                nc.vector.tensor_tensor(s1[:], second, first, ALU.subtract).then_inc(h.gap_ready.sem, 1)
                yield 2
                dve.wait_ge(h.gap_exp.sem, h.gap_exp.at(turn, s))
                step(nc.vector.tensor_scalar(s3[:], s2[:], 1.0, None, ALU.add))
                step(nc.vector.reciprocal(s1[:], s3[:]))
                step(nc.vector.tensor_tensor(s4[:], s2[:], s1[:], ALU.mult))
                step(nc.vector.tensor_tensor(h.oh1[:], h.oh1[:], s1[:].broadcast_to(full), ALU.mult))
                step(nc.vector.tensor_tensor(h.oh2[:], h.oh2[:], s4[:].broadcast_to(full), ALU.mult))
                nc.vector.tensor_tensor(wtok[:], h.oh1[:], h.oh2[:], ALU.add).then_inc(h.weight_ready.sem, 1)
            yield 4
            dve.wait_ge(h.wbc_ps.sem, h.wbc_ps.at(turn, s, 2))
            nc.vector.tensor_copy(h.wbc[:, BANKS:, :], h.ps[:]).then_inc(h.wbc_ready.sem, 1)

        def moe0_pe(pe, h, turn, s):
            yield from router_pe(pe, h, turn, s)
            w1, w2 = W(s, "w1"), W(s, "w2")
            for f in range(FSETS + 1):
                yield ROUTE + f
                if f == 0:
                    pe.wait_ge(h.wbc_ready.sem, h.wbc_ready.at(turn, s, 2))
                else:
                    pe.wait_ge(h.hid_ready.sem, h.hid_ready.at(turn, s, 2 * f))
                if f < FSETS:
                    for c in range(2):
                        k = 2 * f + c
                        nc.tensor.matmul(h.ps[:, c, :], w1[:, k * P:(k + 1) * P], h.xn[:], start=True, stop=True)\
                            .then_inc(h.hid_ps.sem, 1)
                if f > 0:
                    e, part = (f - 1) // 2, (f - 1) % 2
                    if e >= 2 and part == 0:
                        pe.wait_ge(h.ffn_taken.sem, h.ffn_taken.at(turn, s, e - 1))
                    for c in range(2):
                        k = 2 * (f - 1) + c
                        last = nc.tensor.matmul(h.ps[:, 2 + e % 2, :], w2[:, k * P:(k + 1) * P], h.hid[:, part, c, :],
                                                start=(part + c == 0), stop=(part + c == 2))
                    last.then_inc(h.ffn_ps.sem, 1)

        def moe0_act(act, h, turn, s):
            yield from router_act(act, h, turn, s)
            for f in range(FSETS):
                yield ROUTE + f
                if f >= 2:
                    act.wait_ge(h.ffn_ps.sem, h.ffn_ps.at(turn, s, f - 1))
                for c in range(2):
                    k = 2 * f + c
                    act.wait_ge(h.hid_ps.sem, h.hid_ps.at(turn, s, k + 1))
                    nc.scalar.activation(h.hid[:, f % 2, c, :], h.ps[:, c, :], ACT.Relu, bias=W(s, "b1")[:, k:k + 1])\
                        .then_inc(h.hid_ready.sem, 1)

        def moe0_dve(dve, h, turn, s):
            yield from router_dve(dve, h, turn, s)
            for e in range(EXPERTS):
                yield ROUTE + 2 * e + 2
                if e == 0:
                    dve.wait_ge(h.wbc_ready.sem, h.wbc_ready.at(turn, s, 2))
                dve.wait_ge(h.ffn_ps.sem, h.ffn_ps.at(turn, s, 2 * e + 2))
                if e >= 1:
                    dve.wait_ge(h.ffn_added.sem, h.ffn_added.at(turn, s, e))
                nc.vector.scalar_tensor_tensor(out=h.tmp, in0=h.ps[:, 2 + e % 2, :], scalar=W(s, "b2")[:, e:e + 1],
                                               in1=h.wbc[:, e, :], op0=ALU.add, op1=ALU.mult).then_inc(h.ffn_taken.sem, 1)
                dve.wait_ge(h.ffn_taken.sem, h.ffn_taken.at(turn, s, e + 1))
                done = h.resid if e == EXPERTS - 1 else h.ffn_added
                nc.vector.tensor_tensor(h.x[:], h.x[:], h.tmp, ALU.add).then_inc(done.sem, 1)

        def moe1_pe(pe, h, turn, s):
            yield from router_pe(pe, h, turn, s)
            for e in range(EXPERTS + 2):
                yield ROUTE + e
                if e == 0:
                    pe.wait_ge(h.wbc_ready.sem, h.wbc_ready.at(turn, s, 2))
                else:
                    pe.wait_ge(h.hid_ready.sem, h.hid_ready.at(turn, s, e))
                if e <= EXPERTS:
                    for i, w in enumerate(("w1", "w3")):
                        last = nc.tensor.matmul(h.ps[:, i, :], W(s, w)[:, e * P:(e + 1) * P], h.xn[:], start=True, stop=True)
                    last.then_inc(h.hid_ps.sem, 1)
                if e > 0:
                    if e >= 3:
                        pe.wait_ge(h.ffn_taken.sem, h.ffn_taken.at(turn, s, e - 2))
                    nc.tensor.matmul(h.ps[:, 2 + (e - 1) % 2, :], W(s, "w2")[:, (e - 1) * P:e * P],
                                     h.hid[:, (e - 1) % 2, 0, :], start=True, stop=True).then_inc(h.ffn_ps.sem, 1)

        def moe1_act(act, h, turn, s):
            yield from router_act(act, h, turn, s)
            for e in range(EXPERTS + 1):
                yield ROUTE + e
                table(None)
                act.wait_ge(h.hid_ps.sem, h.hid_ps.at(turn, s, e + 1))
                if e >= 2:
                    act.wait_ge(h.hid_ready.sem, h.hid_ready.at(turn, s, e - 1))
                nc.scalar.activation(h.gate[:, e % 2, :], h.ps[:, 0, :], ACT.Silu).then_inc(h.gate_ready.sem, 1)

        def moe1_dve(dve, h, turn, s):
            yield from router_dve(dve, h, turn, s)
            for e in range(EXPERTS + 2):
                yield ROUTE + e
                if e == 0:
                    dve.wait_ge(h.wbc_ready.sem, h.wbc_ready.at(turn, s, 2))
                if e <= EXPERTS:
                    dve.wait_ge(h.gate_ready.sem, h.gate_ready.at(turn, s, e + 1))
                    if e >= 2:
                        dve.wait_ge(h.ffn_ps.sem, h.ffn_ps.at(turn, s, e - 1))
                    nc.vector.tensor_tensor(h.hid[:, e % 2, 0, :], h.gate[:, e % 2, :], h.ps[:, 1, :], ALU.mult)\
                        .then_inc(h.hid_ready.sem, 1)
                if e > 0:
                    f = e - 1
                    dve.wait_ge(h.ffn_ps.sem, h.ffn_ps.at(turn, s, f + 1))
                    if f >= 1:
                        dve.wait_ge(h.ffn_added.sem, h.ffn_added.at(turn, s, f))
                    if f < EXPERTS:
                        nc.vector.tensor_tensor(h.tmp, h.ps[:, 2 + f % 2, :], h.wbc[:, f, :], ALU.mult)\
                            .then_inc(h.ffn_taken.sem, 1)
                    else:
                        nc.vector.tensor_copy(h.tmp, h.ps[:, 2 + f % 2, :]).then_inc(h.ffn_taken.sem, 1)
                    dve.wait_ge(h.ffn_taken.sem, h.ffn_taken.at(turn, s, f + 1))
                    nc.vector.tensor_tensor(h.z[:], h.z[:], h.tmp, ALU.add).then_inc(h.ffn_added.sem, 1)
            dve.wait_ge(h.ffn_added.sem, h.ffn_added.at(turn, s, EXPERTS + 1))
            dve.wait_ge(back.resid.sem, back.resid.before(turn))
            nc.vector.tensor_tensor(back.x[:], h.x[:], h.z[:], ALU.add).then_inc(h.resid.sem, 1)

        def mlp_pe(pe, h, turn, s):
            yield from router_pe(pe, h, turn, s)
            for f in range(3):
                yield 2 + f
                if f > 0:
                    pe.wait_ge(h.hid_ready.sem, h.hid_ready.at(turn, s, 2 * f))
                if f < 2:
                    for c in range(2):
                        k = 2 * f + c
                        nc.tensor.matmul(h.ps[:, c, :], W(s, "up")[:, k * P:(k + 1) * P], h.xn[:], start=True, stop=True)\
                            .then_inc(h.hid_ps.sem, 1)
                if f > 0:
                    for c in range(2):
                        k = 2 * (f - 1) + c
                        last = nc.tensor.matmul(h.ps[:, 2, :], W(s, "down")[:, k * P:(k + 1) * P], h.hid[:, f - 1, c, :],
                                                start=(k == 0), stop=(k == CH0 - 1))
            last.then_inc(h.ffn_ps.sem, 1)

        def mlp_act(act, h, turn, s):
            yield from router_act(act, h, turn, s)
            for f in range(2):
                yield 2 + f
                table(None)
                for c in range(2):
                    k = 2 * f + c
                    act.wait_ge(h.hid_ps.sem, h.hid_ps.at(turn, s, k + 1))
                    nc.scalar.activation(h.hid[:, f, c, :], h.ps[:, c, :], ACT.Silu).then_inc(h.hid_ready.sem, 1)

        def mlp_dve(dve, h, turn, s):
            yield from router_dve(dve, h, turn, s)
            yield 4
            dve.wait_ge(h.wbc_ready.sem, h.wbc_ready.at(turn, s))
            dve.wait_ge(h.ffn_ps.sem, h.ffn_ps.at(turn, s))
            nc.vector.tensor_tensor(h.tmp, h.ps[:, 2, :], h.wbc[:, 0, :], ALU.mult).then_inc(h.ffn_taken.sem, 1)
            dve.wait_ge(h.ffn_taken.sem, h.ffn_taken.at(turn, s))
            nc.vector.tensor_tensor(h.z[:], h.z[:], h.tmp, ALU.add).then_inc(h.ffn_added.sem, 1)
            dve.wait_ge(h.ffn_added.sem, h.ffn_added.at(turn, s))
            nc.vector.tensor_tensor(h.x[:], h.x[:], h.z[:], ALU.add).then_inc(h.resid.sem, 1)

        def block_pe(pe, h, turn, s):
            i = int(s[-1])
            yield 0
            if i == 0:
                pe.wait_ge(h.norm_out.sem, h.norm_out.at(turn, "qlora"))
            else:
                pe.wait_ge(h.resid.sem, h.resid.at(turn, f"block{i - 1}"))
            nc.tensor.matmul(h.ps[:, 2, :], weff[:, 2 * i * P:(2 * i + 1) * P], h.z[:], start=True, stop=True)\
                .then_inc(h.lin_ps.sem, 1)
            yield from norm_pe(pe, h, turn, s, 1)
            yield 1 + NORM_ROUNDS + 1
            pe.wait_ge(h.gelu_ready.sem, h.gelu_ready.at(turn, s))
            nc.tensor.matmul(h.ps[:, 3, :], weff[:, (2 * i + 1) * P:(2 * i + 2) * P], h.sq[:], start=True, stop=True)\
                .then_inc(h.lin_ps.sem, 1)

        def block_act(act, h, turn, s):
            i = int(s[-1])
            yield from norm_act(act, h, turn, s, 1)
            yield 1 + NORM_ROUNDS
            table(None)
            act.wait_ge(h.norm_out.sem, h.norm_out.at(turn, s))
            nc.scalar.activation(h.sq[:], h.xn[:], ACT.Gelu, scale=W("qlora", "gamma")[:, i:i + 1],
                                 bias=W("qlora", "beta")[:, i:i + 1]).then_inc(h.gelu_ready.sem, 1)

        def block_dve(dve, h, turn, s):
            i = int(s[-1])
            bias = W("qlora", "bias")
            yield 0
            dve.wait_ge(h.lin_ps.sem, h.lin_ps.at(turn, s, 1))
            nc.vector.tensor_scalar(h.y[:], h.ps[:, 2, :], bias[:, 2 * i:2 * i + 1], None, ALU.add).then_inc(h.resid.sem, 1)
            yield from norm_dve(dve, h, turn, s, 1)
            yield 1 + NORM_ROUNDS + 1
            dve.wait_ge(h.lin_ps.sem, h.lin_ps.at(turn, s, 2))
            out, done = (h.z, h.resid) if i < 2 else (h.y, h.lin_sum)
            nc.vector.scalar_tensor_tensor(out=out[:], in0=h.ps[:, 3, :], scalar=bias[:, 2 * i + 1:2 * i + 2],
                                           in1=h.z[:], op0=ALU.add, op1=ALU.add).then_inc(done.sem, 1)
            if i == 2:
                dve.wait_ge(h.lin_sum.sem, h.lin_sum.at(turn, s))
                nc.vector.tensor_tensor(h.z[:], h.x[:], h.y[:], ALU.add).then_inc(h.resid.sem, 1)

        in_table = [None]

        def table(name):
            if name and in_table[0] != name:
                nc.scalar.preload_act_table_set(name)
            in_table[0] = name

        def run(eng, stage_of):
            def half(h, parts, turn):
                return in_rounds(parts, turn, {kind: lambda t, s, f=f: f(eng, h, t, s) for kind, f in stage_of.items()})

            table(None)
            weave(schedule([FRONT]), [half(front, FRONT, Turn(None, 0))])
            table(None)
            with eng.Fori(0, PASSES - 1) as i:
                weave(schedule([FRONT, BACK]), [half(front, FRONT, Turn(i, 1)), half(back, BACK, Turn(i, 0))])
            table(None)
            weave(schedule([BACK]), [half(back, BACK, Turn(None, PASSES - 1))])

        @block.sync
        def _(sp):
            def load(s):
                first, end, _ = cols[s]
                into = once[:, first:end] if s in ONCE else wts[:, first - skip:end - skip]
                sp.dma_start(into, w_dram[:, first:end]).then_inc(loaded[s], 16)

            def load_x(p, tokens):
                if not isinstance(p, Turn):
                    p = Turn(None, p)
                sp.wait_ge(front.resid.sem, front.resid.at(p, "load"))
                sp.sem_inc(wait_carrier)
                sp.dma_start(front.xin[:], x_dram[:, tokens]).then_inc(xin_loaded, 16)

            def store(p, tokens):
                sp.wait_ge(back.resid.sem, back.resid.at(p, "block2"))
                sp.sem_inc(wait_carrier)
                sp.dma_start(out_dram[:, tokens], back.z[:]).then_inc(out_stored, 16)

            load("masks")
            load("const")
            sp.dma_start(front.xin[:], x_dram[:, 0:TOK]).then_inc(xin_loaded, 16)
            load("causal0")
            load("lora")
            sp.dma_start(qint, qw_dram).then_inc(qint_loaded, 16)
            for s in list(STAGES)[4:]:
                load(s)
            load_x(0, slice(TOK, 2 * TOK))
            with sp.Fori(0, PASSES - 2) as i:
                load_x(Turn(i, 1), bass.ds(i * TOK + 2 * TOK, TOK))
                store(Turn(i, 0), bass.ds(i * TOK, TOK))
            for p in range(PASSES - 2, PASSES):
                store(Turn(None, p), slice(p * TOK, (p + 1) * TOK))
            sp.wait_ge(out_stored, (PASSES + 1) * 16)

        @block.gpsimd
        def _(pool):
            nc.gpsimd.memset(front.v9[:], 1.0).then_inc(consts_ready, 1)
            nc.gpsimd.memset(back.v9[:], 1.0).then_inc(consts_ready, 1)
            nc.gpsimd.memset(zero_bf[:], 0.0).then_inc(consts_ready, 1)
            nc.gpsimd.memset(front.negm[:], 0.0).then_inc(consts_ready, 1)
            nc.gpsimd.memset(back.negm, 0.0).then_inc(consts_ready, 1)
            nc.gpsimd.memset(front.v33[:], 1.0).then_inc(consts_ready, 1)
            nc.gpsimd.memset(back.z[:], 0.0).then_inc(out_stored, 16)

        CONSTS = 12

        @block.tensor
        def _(pe):
            pe.wait_ge(loaded["const"], 16)
            pe.wait_ge(consts_ready, CONSTS)
            pe.wait_ge(loaded["lora"], 16)
            for i in range(6):
                last = nc.tensor.matmul(back.ps[:, i // 4, i % 4 * P:(i % 4 + 1) * P],
                                        W("lora", "la")[0:RANK, i * P:(i + 1) * P],
                                        W("lora", "lb")[0:RANK, i * P:(i + 1) * P], start=True, stop=True)
            last.then_inc(lora_ps, 1)
            pe.wait_ge(weff_ready, 1)
            pe.wait_ge(loaded["qlora"], 16)
            run(pe, {"norm": norm_pe, "causal": headed_pe, "linear": headed_pe, "mqa": mqa_pe, "moe0": moe0_pe,
                     "moe1": moe1_pe, "mlp": mlp_pe, "arccos": arccos_pe, "block": block_pe})

        @block.scalar
        def _(act):
            act.wait_ge(loaded["const"], 16)
            act.wait_ge(consts_ready, CONSTS)
            run(act, {"norm": norm_act, "causal": headed_act, "linear": headed_act, "mqa": mqa_act, "moe0": moe0_act,
                      "moe1": moe1_act, "mlp": mlp_act, "arccos": arccos_act, "block": block_act})

        @block.vector
        def _(dve):
            dve.wait_ge(loaded["const"], 16)
            dve.wait_ge(loaded["masks"], 16)
            nc.vector.tensor_copy(ident_bf[:], C("ident")).then_inc(consts_ready, 1)
            nc.vector.tensor_copy(mask_q[:], W("masks", "mask_q")).then_inc(consts_ready, 1)
            nc.vector.tensor_copy(mask_k[:], W("masks", "mask_k")).then_inc(consts_ready, 1)
            nc.vector.tensor_copy(before_bf[:], W("masks", "before")).then_inc(consts_ready, 1)
            nc.vector.tensor_copy(max_rows[:], C("max_rows")).then_inc(consts_ready, 1)
            nc.vector.tensor_copy(ones_bf[:], W("masks", "ones")).then_inc(consts_ready, 1)
            nc.vector.memset(front.x[:], 0.0).then_inc(front.resid.sem, 1)
            nc.vector.memset(back.x[:], 0.0).then_inc(back.resid.sem, 1)
            dve.wait_ge(qint_loaded, 16)
            nc.vector.tensor_copy(weff[:], qint).then_inc(dequant_step, 1)
            dve.wait_ge(dequant_step, 1)
            nc.vector.tensor_scalar(weff[:], weff[:], 1.0 / 7.5, -1.0, ALU.mult, ALU.add).then_inc(dequant_step, 1)
            dve.wait_ge(dequant_step, 2)
            dve.wait_ge(loaded["lora"], 16)
            nc.vector.tensor_tensor(weff[:], weff[:], W("lora", "scale"), ALU.mult).then_inc(dequant_step, 1)
            dve.wait_ge(dequant_step, 3)
            dve.wait_ge(lora_ps, 1)
            nc.vector.tensor_tensor(weff[:], weff[:], back.ps[:, 0:2, :].rearrange("p a b -> p (a b)")[:, 0:6 * P], ALU.add)\
                .then_inc(weff_ready, 1)
            run(dve, {"norm": norm_dve, "causal": headed_dve, "linear": headed_dve, "mqa": mqa_dve, "moe0": moe0_dve,
                      "moe1": moe1_dve, "mlp": mlp_dve, "arccos": arccos_dve, "block": block_dve})


def _constants():
    p = np.arange(P)
    head, dim = p // HD, p % HD
    esel = np.zeros((P, GROUPS, P), np.float32)
    for i in range(QUAD // HD):
        esel[p, head // HPG, QUAD * (head % HPG) + HD * i + dim] = 1.0
    den = np.zeros((P, P), np.float32)
    den[p // QUAD * QUAD + HD, p] = 1.0
    dense = np.zeros((P, HPG, P), np.float32)
    dense[QUAD * (head // HPG) + dim, head % HPG, p] = 1.0
    later = (p[None, :] > p[:, None])
    zero = np.zeros((P, P), np.float32)
    mask_q = np.where(later, NEG, 0.0).astype(np.float32)
    mask_k = np.ascontiguousarray(mask_q.T)
    keep = (~later.T).astype(np.float32)

    q_low, k_low, m_low = p % QUAD // 16, p % 16 // HD, p % 2

    def col(v):
        return np.broadcast_to(np.asarray(v, np.float32), (P,))[:, None]

    return {"ident": np.eye(P, dtype=np.float32), "blk8": (head[:, None] == head[None, :]).astype(np.float32),
            "esel": esel.reshape(P, -1), "mask_q": mask_q, "mask_k": mask_k, "keep_k": keep,
            "before": later.astype(np.float32), "ones": zero + 1.0, "mean": zero + 1.0 / P,
            "head_row": col(p % QUAD == 0),
            "max_rows": (p[:, None] % QUAD // 2 == np.arange(GROUPS)[None, :]).astype(np.float32),
            "q_low": col(q_low), "q_sign": col(2 * q_low - 1), "k_low": col(k_low), "k_sign": col(2 * k_low - 1),
            "m_low": col(m_low), "m_sign": col(2 * m_low - 1),
            "iota": np.tile(np.arange(EXPERTS, dtype=np.float32), (P, 1)), "eps5": col(1e-5), "eps6": col(1e-6),
            "half": col(0.5), "one": col(1.0), "ln1024": col(np.log(1024.0)), "lin_eps": col(LIN_EPS), "den": den, "dense": dense.reshape(P, -1)}


def _quadrants(w):
    return np.tile(w.reshape(P, GROUPS, HPG, 1, HD), (1, 1, 1, QUAD // HD, 1)).reshape(P, GROUPS * P)


def _rows(v):
    return np.broadcast_to(v.reshape(1, -1), (P, v.size))


def _side(w):
    return w.transpose(1, 0, 2).reshape(w.shape[1], -1)


def _chunks(w):
    n, h, o = w.shape
    return w.reshape(n, h // P, P, o).transpose(2, 0, 1, 3).reshape(P, -1)


def kernel(**inputs):
    import concourse.bacc as bacc
    from concourse.bass_utils import run_bass_kernel_spmd

    a = {k: np.asarray(v) for k, v in inputs.items()}

    def headed(q, k, v, o):
        return {"q": _quadrants(q), "k": _quadrants(k), "v": v, "o": o}

    def tall(w):
        return np.concatenate([w, np.zeros((P - w.shape[0], w.shape[1]), w.dtype)], 0)

    qkv2, lin, qkv3 = a["L2_ffn_qkv_w"].T, a["L2_attn_wqkv"], a["L3_attn_w_qkv"].T
    b3 = a["L3_attn_b_qkv"]
    both = {n: np.concatenate([a[f"L1_ffn_e{n}"], a[f"L1_ffn_s{n}"][None]], 0) for n in ("W1", "W2", "W3")}
    parts = {
        "masks": _constants(),
        "const": _constants(),
        "causal0": headed(a["L0_attn_WQ"].T, a["L0_attn_WK"].T, a["L0_attn_WV"].T, a["L0_attn_WO"].T),
        "moe0": {"router": a["L0_ffn_Wr"], "rbias": _rows(a["L0_ffn_br"]), "w1": _side(a["L0_ffn_W1"]),
                 "b1": a["L0_ffn_b1"].reshape(EXPERTS * CH0, P).T, "w2": _chunks(a["L0_ffn_W2"]), "b2": a["L0_ffn_b2"].T},
        "causal1": headed(a["L1_attn_Wq"].T, a["L1_attn_Wk"].T, a["L1_attn_Wv"].T, a["L1_attn_Wo"].T),
        "mqa": {"g": a["L1_ffn_g1"][:, None], "q": a["L1_ffn_Wq"].T, "k": np.tile(a["L1_ffn_Wkc"].T, (1, MQH)),
                "v": a["L1_ffn_Wvc"].T, "o": a["L1_ffn_Wo"].T},
        "moe1": {"g": a["L1_ffn_g2"][:, None], "router": a["L1_ffn_Wr"].T, "rbias": _rows(a["L1_ffn_expert_bias"]),
                 **{n.lower(): _side(both[n].transpose(0, 2, 1)) for n in ("W1", "W3", "W2")}},
        "linear": headed(lin[:, 0:P], lin[:, P:2 * P], lin[:, 2 * P:], a["L2_attn_wo"]),
        "causal2": {"g": a["L2_ffn_n1_w"][:, None],
                    **headed(qkv2[:, 0:P], qkv2[:, P:2 * P], qkv2[:, 2 * P:], a["L2_ffn_o_w"].T)},
        "mlp": {"g": a["L2_ffn_n2_w"][:, None], "router": a["L2_ffn_gate_w"].T, "up": a["L2_ffn_up_w"].T,
                "down": _chunks(a["L2_ffn_down_w"].T[None])},
        "arccos": {"q": qkv3[:, 0:P], "k": qkv3[:, P:2 * P], "v": qkv3[:, 2 * P:], "o": a["L3_attn_w_out"].T,
                   "bq": b3[0:P, None], "bk": b3[P:2 * P, None], "bv": _rows(b3[2 * P:]), "bo": a["L3_attn_b_out"][:, None]},
        "qlora": {"bias": a["L3_ffn_biases"].T, "gamma": a["L3_ffn_ln_gamma"].T, "beta": a["L3_ffn_ln_beta"].T},
        "lora": {"scale": _side(np.repeat(a["L3_ffn_scales"].transpose(0, 2, 1), QGROUP, 1)),
                 "la": tall(_side(a["L3_ffn_lora_a"])), "lb": tall(_side(a["L3_ffn_lora_b"].transpose(0, 2, 1)))},
    }
    blob = np.concatenate([parts[s][n] for s, names in STAGES.items() for n, _ in names], 1)
    arrays = {"x_dram": np.ascontiguousarray(a["L0_attn_x"].reshape(BATCH * SEQ, P).T),
              "w_dram": np.ascontiguousarray(blob),
              "qw_dram": np.ascontiguousarray(_side(a["L3_ffn_qweights"].transpose(0, 2, 1)))}
    nc = bacc.Bacc("TRN2", target_bir_lowering=False, num_devices=1)
    args = [nc.dram_tensor(n, v.shape, mybir.dt.from_np(v.dtype), kind="ExternalInput").ap() for n, v in arrays.items()]
    args.append(nc.dram_tensor("out_dram", (P, BATCH * SEQ), F32, kind="ExternalOutput").ap())
    build(nc, *args)
    r = run_bass_kernel_spmd(nc, [arrays], core_ids=[0])
    got = r.results[0]["out_dram"]
    return np.ascontiguousarray(got.T).reshape(BATCH, SEQ, P)
```

```python
from contextlib import ExitStack

import numpy as np

import concourse.bass as bass
from concourse import mybir

ALU = mybir.AluOpType
ACT = mybir.ActivationFunctionType
F32 = mybir.dt.float32
F32R = mybir.dt.float32r
BF16 = mybir.dt.bfloat16
U32 = mybir.dt.uint32
I32 = mybir.dt.int32
AX = mybir.AxisListType

P = 128
BATCH, SEQ = 16, 256
PAIR = 2
TOK = PAIR * SEQ
TILES = TOK // P
PASSES = BATCH // PAIR
HEADS, HD = 16, 8
GROUPS, QUAD = 4, 32
HPG = HEADS // GROUPS
V1 = HD + 1
EXPERTS = 8
FF0 = 512
CH0 = FF0 // P
CAP = max(1, int(SEQ / EXPERTS * 1.25))
MQH, MQD = 4, 32
MV1 = MQD + 1
BANKS = 4
NEG = -1.0e30
RANK, QGROUP = 32, 16
LIN_EPS = 1e-5
CLIP = float(np.float32(1.0) - np.float32(1e-7))
CLIP_LO = float(np.float32(-1.0) + np.float32(1e-7))
GEO_POWER = -3.2
LN_EXP = "natural_log_exp_and_others"

HEADED = [("q", GROUPS * P), ("k", GROUPS * P), ("v", P), ("o", P)]
STAGES = {
    "masks": [("mask_q", P), ("before", P), ("ones", P)],
    "lora": [("scale", 6 * P), ("la", 6 * P), ("lb", 6 * P)],
    "const": [("ident", P), ("blk8", P), ("esel", GROUPS * P), ("keep_k", P), ("mean", P),
              ("den", P), ("dense", GROUPS * P),
              ("max_rows", GROUPS), ("q_low", 1), ("q_sign", 1), ("k_low", 1), ("k_sign", 1), ("m_low", 1), ("m_sign", 1),
              ("iota", EXPERTS), ("eps5", 1), ("eps6", 1), ("half", 1), ("one", 1), ("ln1024", 1), ("lin_eps", 1)],
    "causal0": HEADED,
    "moe0": [("router", EXPERTS), ("rbias", EXPERTS), ("w1", EXPERTS * FF0), ("b1", EXPERTS * CH0),
             ("w2", EXPERTS * FF0), ("b2", EXPERTS)],
    "causal1": HEADED,
    "mqa": [("g", 1), ("q", P), ("k", P), ("v", MQD), ("o", P)],
    "moe1": [("g", 1), ("router", EXPERTS), ("rbias", EXPERTS), ("w1", (EXPERTS + 1) * P), ("w3", (EXPERTS + 1) * P),
             ("w2", (EXPERTS + 1) * P)],
    "linear": HEADED,
    "causal2": [("g", 1)] + HEADED,
    "mlp": [("g", 1), ("router", EXPERTS), ("up", FF0), ("down", FF0)],
    "arccos": [("q", P), ("k", P), ("v", P), ("o", P), ("bq", 1), ("bk", 1), ("bv", P), ("bo", 1)],
    "qlora": [("bias", 6), ("gamma", 3), ("beta", 3)],
}
ONCE = ("masks", "lora")


def columns():
    out, at = {}, 0
    for stage, parts in STAGES.items():
        first, names = at, {}
        for name, width in parts:
            names[name] = (at, width)
            at += width
        out[stage] = (first, at, names)
    return out, at


class Turn:

    def __init__(self, register, shift):
        self.register, self.shift = register, shift

    def count(self, per_pass, more):
        fixed = self.shift * per_pass + more
        return fixed if self.register is None else self.register * per_pass + fixed


class Signal:

    def __init__(self, sem, counts, ahead=0):
        self.sem, self.base, self.total, self.ahead = sem, {}, 0, ahead
        for stage in sorted(counts, key=ORDER.index):
            self.base[stage] = self.total
            self.total += counts[stage]

    def at(self, turn, stage, n=1):
        return turn.count(self.total, self.ahead + self.base[stage] + n)

    def before(self, turn):
        return turn.count(self.total, self.ahead)


ORDER = ["load", "causal0", "moe0", "causal1", "mqa_in", "mqa", "moe1", "linear", "causal2_in", "causal2", "mlp",
         "arccos", "qlora", "block0_in", "block0", "block1_in", "block1", "block2_in", "block2"]
CAUSAL = ("causal0", "causal1", "causal2")
HEADED_STAGES = ("causal0", "causal1", "linear", "causal2")
ATTENTION = HEADED_STAGES + ("mqa", "arccos")
NORMS = {
    "causal0": ("x", "xn", True, "eps5", ("resid", "load"), None),
    "moe0": ("x", "xn", True, "eps5", ("resid", "causal0"), None),
    "causal1": ("x", "xn", True, "eps5", ("resid", "moe0"), None),
    "mqa_in": ("x", "z", True, "eps5", ("resid", "causal1"), None),
    "mqa": ("z", "xn", False, "eps6", ("norm_out", "mqa_in"), "mqa"),
    "moe1": ("z", "xn", False, "eps6", ("resid", "mqa"), "moe1"),
    "linear": ("x", "xn", True, "eps5", ("handed", "moe1"), None),
    "causal2_in": ("x", "z", True, "eps5", ("resid", "linear"), None),
    "causal2": ("z", "xn", False, "eps6", ("norm_out", "causal2_in"), "causal2"),
    "mlp": ("z", "xn", False, "eps6", ("resid", "causal2"), "mlp"),
    "arccos": ("x", "xn", True, "eps5", ("resid", "mlp"), None),
    "qlora": ("x", "z", True, "eps5", ("resid", "arccos"), None),
    "block0": ("y", "xn", True, "eps5", ("resid", "block0_in"), None),
    "block1": ("y", "xn", True, "eps5", ("resid", "block1_in"), None),
    "block2": ("y", "xn", True, "eps5", ("resid", "block2_in"), None),
}
RESID = ["load", "causal0", "moe0", "causal1", "mqa", "moe1", "linear", "causal2", "mlp", "arccos",
         "block0_in", "block0", "block1_in", "block1", "block2_in", "block2"]
MROUNDS = PAIR * 3
MSETS = MROUNDS * 2
ESETS = PAIR * HPG
QSETS = PAIR * 2
UNITS = PAIR * 2
UHEADS = HEADS // 2
ARC_STEPS = 6
FSETS = EXPERTS * 2

NORM_ROUNDS = 2
PROJECT = 3
ROUTE = 5
OUT = 3
SHARES = {"norm": 1, "project": 3.14, "maxima": 2.36, "weights": 1.42, "linear": 2, "out": 1.38, "queries": 1.5, "route": 1.8, "experts0": 1.8, "experts1": 1.2, "mlp": 1.2, "arc_in": 2.3, "arc": 2.3, "block": 1}
PHASES = {
    "norm": [(NORM_ROUNDS, "norm")],
    "causal": [(PROJECT, "project"), (MROUNDS + 1, "maxima"), (ESETS + 1, "weights"), (OUT, "out")],
    "linear": [(PROJECT, "project"), (ESETS + 1, "linear"), (OUT, "out")],
    "mqa": [(1, "project"), (TILES + 1, "maxima"), (QSETS, "queries"), (3, "out")],
    "moe0": [(ROUTE, "route"), (FSETS + 1, "experts0")],
    "moe1": [(ROUTE, "route"), (EXPERTS + 2, "experts1")],
    "mlp": [(5, "mlp")],
    "arccos": [(6, "arc_in"), (UNITS * ARC_STEPS + 2, "arc"), (OUT, "out")],
    "block": [(3 + NORM_ROUNDS, "block")],
}
ROUNDS = {kind: sum(n for n, _ in phases) for kind, phases in PHASES.items()}
FRONT = [("norm", "causal0"), ("causal", "causal0"), ("norm", "moe0"), ("moe0", "moe0"), ("norm", "causal1"),
         ("causal", "causal1"), ("norm", "mqa_in"), ("norm", "mqa"), ("mqa", "mqa"), ("norm", "moe1"), ("moe1", "moe1")]
BACK = [("norm", "linear"), ("linear", "linear"), ("norm", "causal2_in"), ("norm", "causal2"), ("causal", "causal2"),
        ("norm", "mlp"), ("mlp", "mlp"), ("norm", "arccos"), ("arccos", "arccos"), ("norm", "qlora"),
        ("block", "block0"), ("block", "block1"), ("block", "block2")]


def schedule(halves):
    order = []
    for h, parts in enumerate(halves):
        times = [SHARES[phase] for kind, _ in parts for n, phase in PHASES[kind] for _ in range(n)]
        at = 0.0
        for r, time in enumerate(times):
            order.append(((at + time / 2) / sum(times), h, r))
            at += time
        if parts is FRONT:
            order[-1] = (1.0, h, r)
    return [(h, r) for _, h, r in sorted(order)]


def weave(order, halves):
    ahead = [next(half, None) for half in halves]
    for h, r in order:
        while ahead[h] is not None and ahead[h] <= r:
            ahead[h] = next(halves[h], None)


def in_rounds(parts, turn, stage_of):
    first = 0
    for kind, name in parts:
        for r in stage_of[kind](turn, name):
            yield first + r
        first += ROUNDS[kind]


class Half:

    def __init__(self, nc, ctx, name, parts):
        stages = {n for _, n in parts} | {f"block{i}_in" for i in range(3)} | {"load"}
        self.front = parts is FRONT
        if not self.front:
            stages -= {"load"}
        else:
            stages -= {f"block{i}_in" for i in range(3)}
        norms = [n for kind, n in parts if kind == "norm"] + [n for kind, n in parts if kind == "block"]

        def sb(buf, shape, dt=F32):
            return ctx.enter_context(nc.sbuf_tensor(f"{name}_{buf}", shape, dt))

        def rounded(buf, shape, first=0):
            return nc.alloc_sbuf_tensor_at(f"{name}_{buf}", shape, F32R, offset=last_at[0] + 4 * first)

        def at_last(buf, shape):
            out = sb(buf, shape)
            last_at[0] = nc.sbuf_base - 4 * int(np.prod(shape[1:]))
            return out

        last_at = [0]

        def signal(sig, counts, ahead=0):
            mine = {s: n for s, n in counts.items() if s in stages}
            return Signal(ctx.enter_context(nc.semaphore(f"{name}_{sig}")), mine, ahead) if mine else None

        self.ps = ctx.enter_context(nc.psum_tensor(f"{name}_ps", [P, BANKS, 512], F32))
        self.x = sb("x", [P, TOK])
        self.z = sb("z", [P, TOK])
        self.xn = sb("xn", [P, TOK])
        self.cen = sb("cen", [P, TOK])
        self.sq = sb("sq", [P, TOK])
        self.qk = at_last("qk", [P, 2 * GROUPS, TOK])
        qkr = rounded("qkr", [P, 2 * GROUPS, TOK])
        self.q4, self.k4 = self.qk[:, 0:GROUPS, :], self.qk[:, GROUPS:, :]
        self.q4r, self.k4r = qkr[:, 0:GROUPS, :], qkr[:, GROUPS:, :]
        self.wbc = self.qk
        self.v9 = sb("v9", [P, TILES, HEADS, V1])
        if self.front:
            self.rden = sb("rden", [P, PAIR, 2 * MQH])
            self.v33 = sb("v33", [P, TILES, MV1])
            self.xin = sb("xin", [P, TOK])
            scratch = sb("scratch", [P, 7 * TOK])
            parts = sb("parts", [P, HPG * TOK])
            self.negm, self.maxTr = sb("negm", [P, TILES, P]), sb("maxTr", [P, TOK], F32R)
            self.ytok = scratch[:, 6 * TOK:7 * TOK].rearrange("p (t c) -> p t c", t=TILES)
        else:
            self.vs = sb("vs", [P, 2, UHEADS, V1])
            self.nsum = sb("nsum", [P, 2, UHEADS])
            scratch = at_last("cosines", [P, 2 * 2 * UHEADS * SEQ])
            self.cosines = scratch[:, :].rearrange("p (u c) -> p u c", u=2)
            self.maxTr = rounded("maxTr", [P, TOK], 13 * TOK)
            self.scratch = scratch
            parts = scratch[:, 8 * TOK:12 * TOK]
            self.negm = scratch[:, 12 * TOK:13 * TOK].rearrange("p (t c) -> p t c", t=TILES)
            self.y = sb("y", [P, TOK])
        self.parts = {s: [parts[:, j * TOK:(j + 1) * TOK] for j in range(HPG)] for s in HEADED_STAGES}
        self.parts["arccos"] = [] if self.front else [self.y[:], self.z[:], self.sq[:], self.cen[:]]
        self.rden4 = {s: scratch[:, 0:HPG * TOK].rearrange("p (j t) -> p j t", j=HPG) for s in HEADED_STAGES}
        self.rden4["arccos"] = self.q4
        self.probs = scratch[:, 0:6 * TOK].rearrange("p (s c) -> p s c", s=2)
        self.high = scratch[:, 0:GROUPS * TOK].rearrange("p (g t) -> p g t", g=GROUPS)
        self.rect = scratch[:, GROUPS * TOK:2 * GROUPS * TOK].rearrange("p (g t) -> p g t", g=GROUPS) if not self.front else None
        self.hid = scratch[:, 0:4 * TOK].rearrange("p (s c t) -> p s c t", s=2, c=2)
        self.tmp = scratch[:, 4 * TOK:5 * TOK]
        self.gate = scratch[:, 5 * TOK:7 * TOK].rearrange("p (s t) -> p s t", s=2)
        self.lg, self.pr, self.t8, self.wtok = (sb(n, [P, TILES, EXPERTS]) for n in ("lg", "pr", "t8", "wtok"))
        if self.front:
            self.ixf, self.oh1, self.oh2, self.ohs = (sb(n, [P, TILES, EXPERTS]) for n in ("ixf", "oh1", "oh2", "ohs"))
            self.ix = sb("ix", [P, TILES, EXPERTS], U32)
            self.ohs_bf = sb("ohs_bf", [P, TILES, EXPERTS], BF16)
        self.s1, self.s2, self.s3, self.s4 = (sb(n, [P, TILES, 1]) for n in ("s1", "s2", "s3", "s4"))
        self.buf = {"x": self.x, "z": self.z, "xn": self.xn, "y": None if self.front else self.y}

        centred = [n for n in norms if NORMS[n][2]]
        self.resid = signal("resid", {r: 1 for r in RESID}, ahead=1)
        self.norm_mean = signal("norm_mean", {n: 1 for n in centred})
        self.norm_cen = signal("norm_cen", {n: 1 for n in centred})
        self.norm_sq = signal("norm_sq", {n: 1 for n in norms})
        self.norm_var = signal("norm_var", {n: 1 for n in norms})
        self.norm_ln = signal("norm_ln", {n: 1 for n in norms})
        self.norm_rstd = signal("norm_rstd", {n: 1 for n in norms})
        self.norm_out = signal("norm_out", {n: 1 for n in norms})
        self.q_ps = signal("q_ps", {s: 2 for s in HEADED_STAGES} | {"mqa": 1, "arccos": 1})
        self.k_ps = signal("k_ps", {s: 2 for s in HEADED_STAGES} | {"mqa": 1, "arccos": 1})
        self.v_ps = signal("v_ps", {s: 1 for s in ATTENTION})
        self.q_high = signal("q_high", {s: 2 for s in HEADED_STAGES + ("arccos",)})
        self.k_high = signal("k_high", {s: 2 for s in HEADED_STAGES + ("arccos",)})
        self.rect_ready = signal("rect_ready", {"linear": 4})
        self.q_ready = signal("q_ready", {s: 2 for s in HEADED_STAGES + ("arccos",)} | {"mqa": 1})
        self.k_ready = signal("k_ready", {s: 2 for s in HEADED_STAGES + ("arccos",)} | {"mqa": 1})
        self.v_ready = signal("v_ready", {s: 1 for s in ATTENTION})
        self.max_ps = signal("max_ps", {s: MSETS for s in CAUSAL} | {"mqa": 2 * TILES})
        self.max_done = signal("max_done", {s: MSETS for s in CAUSAL} | {"mqa": 2 * TILES})
        self.max_pair = signal("max_pair", {s: 1 for s in CAUSAL + ("mqa",)})
        self.negm_high = signal("negm_high", {s: 1 for s in CAUSAL + ("mqa",)})
        self.negm_ps = signal("negm_ps", {s: 1 for s in CAUSAL + ("mqa",)})
        self.negm_ready = signal("negm_ready", {s: 1 for s in CAUSAL + ("mqa",)})
        self.score_ps = signal("score_ps", {s: 2 * ESETS for s in HEADED_STAGES} | {"mqa": QSETS, "arccos": 2 * UNITS})
        self.probs_ready = signal("probs_ready", {s: 2 * ESETS for s in CAUSAL} | {"linear": ESETS, "mqa": QSETS})
        self.masked = signal("masked", {s: 2 * ESETS for s in CAUSAL})
        self.full_ready = signal("full_ready", {"linear": ESETS})
        self.pv_ps = signal("pv_ps", {s: ESETS for s in HEADED_STAGES} | {"mqa": QSETS, "arccos": UNITS})
        self.part_ready = signal("part_ready", {s: HPG for s in HEADED_STAGES} | {"arccos": UNITS})
        self.den_ps = signal("den_ps", {s: 2 for s in HEADED_STAGES + ("arccos",)})
        self.den_ln = signal("den_ln", {s: 2 for s in HEADED_STAGES + ("arccos",)})
        self.rden_ready = signal("rden_ready", {s: 2 for s in HEADED_STAGES + ("arccos",)})
        self.den_step = signal("den_step", {"mqa": 2 * PAIR})
        self.y_ready = signal("y_ready", {s: 2 for s in HEADED_STAGES + ("arccos",)} | {"mqa": PAIR})
        self.yT_ps = signal("yT_ps", {s: 1 for s in ATTENTION})
        self.yT_ready = signal("yT_ready", {s: 1 for s in ATTENTION})
        self.o_ps = signal("o_ps", {s: 1 for s in ATTENTION})
        routed = ("moe0", "moe1", "mlp")
        self.logits_ps = signal("logits_ps", {s: 1 for s in routed})
        self.route_step = signal("route_step", {"moe0": 18, "moe1": 21, "mlp": 14})
        self.route_shift = signal("route_shift", {s: 1 for s in routed})
        self.route_exp = signal("route_exp", {s: 1 for s in routed})
        self.gap_ready = signal("gap_ready", {"moe1": 1})
        self.gap_exp = signal("gap_exp", {"moe1": 1})
        self.chosen_ready = signal("chosen_ready", {"moe0": 1})
        self.place_ps = signal("place_ps", {"moe0": 1})
        self.weight_ready = signal("weight_ready", {s: 1 for s in routed})
        self.wbc_ps = signal("wbc_ps", {"moe0": 2, "moe1": 2, "mlp": 1})
        self.wbc_ready = signal("wbc_ready", {"moe0": 2, "moe1": 2, "mlp": 1})
        self.hid_ps = signal("hid_ps", {"moe0": EXPERTS * CH0, "moe1": EXPERTS + 1, "mlp": CH0})
        self.gate_ready = signal("gate_ready", {"moe1": EXPERTS + 1})
        self.hid_ready = signal("hid_ready", {"moe0": EXPERTS * CH0, "moe1": EXPERTS + 1, "mlp": CH0})
        self.ffn_ps = signal("ffn_ps", {"moe0": FSETS, "moe1": EXPERTS + 1, "mlp": 1})
        self.ffn_taken = signal("ffn_taken", {"moe0": EXPERTS, "moe1": EXPERTS + 1, "mlp": 1})
        self.ffn_added = signal("ffn_added", {"moe0": EXPERTS - 1, "moe1": EXPERTS + 1, "mlp": 1})
        self.arc_raw = signal("arc_raw", {"arccos": 2})
        self.arc_sq = signal("arc_sq", {"arccos": 2})
        self.arc_norm_ps = signal("arc_norm_ps", {"arccos": 2})
        self.arc_floor = signal("arc_floor", {"arccos": 2})
        self.arc_ln = signal("arc_ln", {"arccos": 2})
        self.arc_rn = signal("arc_rn", {"arccos": 2})
        self.arc_unit = signal("arc_unit", {"arccos": 2})
        self.head_ps = signal("head_ps", {"arccos": 4})
        self.cos_ready = signal("cos_ready", {"arccos": 2 * UNITS})
        self.arc_pass = signal("arc_pass", {"arccos": UNITS * ARC_STEPS})
        self.nsum_step = signal("nsum_step", {"arccos": UNITS * 3})
        self.vs_ready = signal("vs_ready", {"arccos": UNITS})
        self.lin_ps = signal("lin_ps", {f"block{i}": 2 for i in range(3)})
        self.gelu_ready = signal("gelu_ready", {f"block{i}": 1 for i in range(3)})
        self.lin_sum = signal("lin_sum", {"block2": 1})

    def inner(self, stage):
        return self.z if stage in ("mqa", "causal2") else self.x


def build(nc, x_dram, w_dram, qw_dram, out_dram):
    cols, width = columns()
    with ExitStack() as ctx:
        def sb(name, shape, dt=F32):
            return ctx.enter_context(nc.sbuf_tensor(name, shape, dt))

        def sem(name):
            return ctx.enter_context(nc.semaphore(name))

        skip = cols["const"][0]
        wts = sb("wts", [P, width - skip])
        weff = sb("weff", [P, 6 * P])
        ident_bf, mask_q, before_bf, ones_bf = (
            sb(n, [P, P], BF16) for n in ("ident_bf", "mask_q", "before_bf", "ones_bf"))
        zero_bf = sb("zero_bf", [P, 1], BF16)
        max_rows = sb("max_rows", [P, GROUPS], F32R)
        front, back = Half(nc, ctx, "front", FRONT), Half(nc, ctx, "back", BACK)
        once = back.scratch[:, 0:skip]
        qint = back.scratch[:, skip:skip + 6 * P].bitcast(I32)

        def W(stage, name):
            at, n = cols[stage][2][name]
            return once[:, at:at + n] if stage in ONCE else wts[:, at - skip:at - skip + n]

        def C(name):
            return W("const", name)

        loaded = {s: sem(f"loaded_{s}") for s in STAGES}
        qint_loaded = sem("qint_loaded")
        consts_ready = sem("consts_ready")
        wait_carrier = sem("wait_carrier")
        dequant_step = sem("dequant_step")
        lora_ps = sem("lora_ps")
        weff_ready = sem("weff_ready")
        xin_loaded = sem("xin_loaded")
        out_stored = sem("out_stored")

        block = ctx.enter_context(nc.Block())

        def source(h, turn, n):
            kind, after = NORMS[n][4]
            sig = {"resid": h.resid, "norm_out": h.norm_out, "handed": front.resid}[kind]
            return sig.sem, sig.at(turn, after)

        def norm_pe(pe, h, turn, n, first=0):
            src, _, centred, _, _, gain = NORMS[n]
            yield first
            if centred:
                pe.wait_ge(*source(h, turn, n))
                nc.tensor.matmul(h.ps[:, 0, :], C("mean"), h.buf[src][:], start=True, stop=True)\
                    .then_inc(h.norm_mean.sem, 1)
            yield first + 1
            if gain:
                pe.wait_ge(loaded[gain], 16)
            pe.wait_ge(h.norm_sq.sem, h.norm_sq.at(turn, n))
            nc.tensor.matmul(h.ps[:, 1, :], C("mean"), h.sq[:], start=True, stop=True).then_inc(h.norm_var.sem, 1)

        def norm_act(act, h, turn, n, first=0):
            src, _, centred, eps, _, _ = NORMS[n]
            yield first
            if centred:
                act.wait_ge(h.norm_cen.sem, h.norm_cen.at(turn, n))
            else:
                act.wait_ge(*source(h, turn, n))
            nc.scalar.activation(h.sq[:], h.cen[:] if centred else h.buf[src][:], ACT.Square).then_inc(h.norm_sq.sem, 1)
            yield first + 1
            table(LN_EXP)
            act.wait_ge(h.norm_var.sem, h.norm_var.at(turn, n))
            nc.scalar.activation(h.sq[:], h.ps[:, 1, :], ACT.Ln, bias=C(eps)).then_inc(h.norm_ln.sem, 1)
            act.wait_ge(h.norm_ln.sem, h.norm_ln.at(turn, n))
            nc.scalar.activation(h.sq[:], h.sq[:], ACT.Exp, scale=-0.5).then_inc(h.norm_rstd.sem, 1)

        def norm_dve(dve, h, turn, n, first=0):
            src, dst, centred, _, _, gain = NORMS[n]
            yield first
            if n == "causal0":
                dve.wait_ge(h.resid.sem, h.resid.before(turn))
                dve.wait_ge(xin_loaded, turn.count(16, 16))
                nc.vector.tensor_copy(h.x[:], h.xin[:]).then_inc(h.resid.sem, 1)
            if n == "causal2_in":
                dve.wait_ge(out_stored, turn.count(16, 16))
            if centred:
                dve.wait_ge(*source(h, turn, n))
                dve.wait_ge(h.norm_mean.sem, h.norm_mean.at(turn, n))
                nc.vector.tensor_tensor(h.cen[:], h.buf[src][:], h.ps[:, 0, :], ALU.subtract).then_inc(h.norm_cen.sem, 1)
            yield first + 1
            dve.wait_ge(h.norm_rstd.sem, h.norm_rstd.at(turn, n))
            if centred:
                nc.vector.tensor_tensor(h.buf[dst][:], h.cen[:], h.sq[:], ALU.mult).then_inc(h.norm_out.sem, 1)
            else:
                nc.vector.scalar_tensor_tensor(out=h.buf[dst][:], in0=h.buf[src][:], scalar=W(gain, "g"), in1=h.sq[:],
                                               op0=ALU.mult, op1=ALU.mult).then_inc(h.norm_out.sem, 1)

        def rows(j, n):
            return slice(QUAD * j, QUAD * j + n)

        def values_pe(h, bank, w, n):
            for t in range(TILES):
                last = nc.tensor.matmul(h.ps[:, bank, t * n:(t + 1) * n], h.xn[:, t * P:(t + 1) * P], w,
                                        start=True, stop=True)
            last.then_inc(h.v_ps.sem, 1)

        def headed_project_pe(pe, h, turn, s):
            yield 0
            pe.wait_ge(loaded[s], 16)
            pe.wait_ge(h.norm_out.sem, h.norm_out.at(turn, s))
            for g in range(GROUPS):
                last = nc.tensor.matmul(h.ps[:, g, :], W(s, "q")[:, g * P:(g + 1) * P], h.xn[:], start=True, stop=True)
                if g % 2:
                    last.then_inc(h.q_ps.sem, 1)
            yield 1
            for g in range(GROUPS):
                if g % 2 == 0:
                    pe.wait_ge(h.q_ready.sem, h.q_ready.at(turn, s, g // 2 + 1))
                last = nc.tensor.matmul(h.ps[:, g, :], W(s, "k")[:, g * P:(g + 1) * P], h.xn[:], start=True, stop=True)
                if g % 2:
                    last.then_inc(h.k_ps.sem, 1)
            yield 2
            pe.wait_ge(h.k_ready.sem, h.k_ready.at(turn, s, 1))
            values_pe(h, 0, W(s, "v"), P)

        def high_act(act, ps, high, sign, done):
            nc.scalar.activation(high.bitcast(F32R), ps, ACT.Copy, scale=C(sign)).then_inc(done.sem, 1)

        def split_dve(dve, ps, high, low, out, done):
            nc.vector.scalar_tensor_tensor(out=out, in0=ps, scalar=C(low), in1=high, op0=ALU.mult, op1=ALU.subtract)\
                .then_inc(done.sem, 1)

        def headed_project_act(act, h, turn, s):
            for i, (ps_sig, sign, high) in enumerate(((h.q_ps, "q_sign", h.q_high), (h.k_ps, "k_sign", h.k_high))):
                yield i
                for c in range(2):
                    two = slice(2 * c, 2 * c + 2)
                    act.wait_ge(ps_sig.sem, ps_sig.at(turn, s, c + 1))
                    if s == "linear":
                        nc.scalar.activation(h.rect[:, two, :], h.ps[:, two, :], ACT.Relu).then_inc(h.rect_ready.sem, 1)
                        act.wait_ge(h.rect_ready.sem, h.rect_ready.at(turn, s, 2 * i + c + 1))
                        high_act(act, h.rect[:, two, :], h.high[:, two, :], sign, high)
                    else:
                        high_act(act, h.ps[:, two, :], h.high[:, two, :], sign, high)
            yield 2
            act.wait_ge(h.v_ps.sem, h.v_ps.at(turn, s))
            nc.scalar.activation(h.v9[:].rearrange("p t h d -> p (t h) d")[:, :, 0:HD],
                                 h.ps[:, 0, :].rearrange("p (h d) -> p h d", d=HD), ACT.Copy).then_inc(h.v_ready.sem, 1)

        def headed_project_dve(dve, h, turn, s):
            src = h.rect if s == "linear" else h.ps
            yield 0
            split_queries_dve(dve, h, turn, s, src)
            yield 1
            split_keys_dve(dve, h, turn, s, src)

        def split_queries_dve(dve, h, turn, s, src):
            for c in range(2):
                two = slice(2 * c, 2 * c + 2)
                dve.wait_ge(h.q_high.sem, h.q_high.at(turn, s, c + 1))
                split_dve(dve, src[:, two, :], h.high[:, two, :], "q_low", h.q4r[:, two, :], h.q_ready)

        def split_keys_dve(dve, h, turn, s, src):
            for c in range(2):
                two = slice(2 * c, 2 * c + 2)
                dve.wait_ge(h.k_high.sem, h.k_high.at(turn, s, c + 1))
                split_dve(dve, src[:, two, :], h.high[:, two, :], "k_low", h.k4r[:, two, :], h.k_ready)

        def mset(m):
            b, part, js = m // 6, m // 2 % 3, slice(2 * (m % 2), 2 * (m % 2) + 2)
            return (b, 0, P, 0, GROUPS, js) if part == 0 else (b, 1, SEQ, 2 * (part - 1), 2, js)

        def max_pe(pe, h, turn, s):
            for m in range(MSETS):
                yield PROJECT + m // 2
                b, qt, keys, g0, ng, js = mset(m)
                if m == 0:
                    pe.wait_ge(h.q_ready.sem, h.q_ready.at(turn, s, 2))
                    pe.wait_ge(h.k_ready.sem, h.k_ready.at(turn, s, 2))
                    pe.wait_ge(h.v_ready.sem, h.v_ready.at(turn, s))
                elif m >= 2:
                    pe.wait_ge(h.max_done.sem, h.max_done.at(turn, s, m - 1))
                for gi in range(ng):
                    for j in range(js.start, js.stop):
                        nc.tensor.matmul(h.ps[:, j, gi * keys:(gi + 1) * keys],
                                         h.q4r[rows(j, QUAD), g0 + gi, b * SEQ + qt * P:b * SEQ + (qt + 1) * P],
                                         h.k4r[rows(j, QUAD), g0 + gi, b * SEQ:b * SEQ + keys],
                                         start=(gi == 0), stop=False, skip_group_check=True)
                for j in range(js.start, js.stop):
                    diagonal = h.ps[:, j, :].rearrange("p (g k) -> p g k", k=keys)[:, :, keys - P:keys]
                    last = nc.tensor.matmul(diagonal, ident_bf[:], mask_q[:].unsqueeze(1).broadcast_to([P, ng, P]),
                                            start=False, stop=True, skip_group_check=True)
                last.then_inc(h.max_ps.sem, 1)
            yield PROJECT + MROUNDS
            pe.wait_ge(h.max_pair.sem, h.max_pair.at(turn, s))
            for t in range(TILES):
                last = nc.tensor.transpose(h.ps[:, 0, t * P:(t + 1) * P], h.negm[:, t, :], C("ident"))
            last.then_inc(h.negm_ps.sem, 1)

        def max_columns(h, tiles, i):
            return h.negm[:, tiles, :].rearrange("p t (j r) -> p t j r", r=QUAD)[:, :, :, 0:2 * GROUPS]\
                .rearrange("p t j (g i) -> p t j g i", i=2)[:, :, :, :, i]

        def max_act(act, h, turn, s, end):
            yield end
            act.wait_ge(h.negm_ps.sem, h.negm_ps.at(turn, s))
            high_act(act, h.ps[:, 0, :], h.high[:, 0, :], "m_sign", h.negm_high)

        def max_dve(dve, h, turn, s):
            for m in range(MSETS):
                yield PROJECT + m // 2
                b, qt, keys, g0, ng, js = mset(m)
                dve.wait_ge(h.max_ps.sem, h.max_ps.at(turn, s, m + 1))
                into = max_columns(h, slice(2 * b + qt, 2 * b + qt + 1), 0)[:, 0, js, g0:g0 + ng]
                nc.vector.tensor_reduce(into, h.ps[:, js, :].rearrange("p j (g k) -> p j g k", k=keys),
                                        AX.X, ALU.max, negate=True).then_inc(h.max_done.sem, 1)
            yield from max_end_dve(dve, h, turn, s, MSETS, PROJECT + MROUNDS)

        def max_end_dve(dve, h, turn, s, sets, end):
            dve.wait_ge(h.max_done.sem, h.max_done.at(turn, s, sets))
            for t in range(TILES):
                last = nc.vector.tensor_copy(max_columns(h, slice(t, t + 1), 1)[:, 0], max_columns(h, slice(t, t + 1), 0)[:, 0])
            last.then_inc(h.max_pair.sem, 1)
            yield end
            dve.wait_ge(h.negm_high.sem, h.negm_high.at(turn, s))
            split_dve(dve, h.ps[:, 0, :], h.high[:, 0, :], "m_low", h.maxTr[:, :], h.negm_ready)

        def scores_first(s):
            return PROJECT + MROUNDS + 1 if s in CAUSAL else PROJECT

        def diagonal_at(s, g, t):
            at = g * SEQ if s in CAUSAL and t == 0 else t * TOK + g * P + (TOK if s in CAUSAL else 0)
            return slice(at, at + P)

        def full_at(s, g):
            at = g * SEQ + P if s in CAUSAL else 2 * TOK + g * P
            return slice(at, at + P)

        def headed_scores_pe(pe, h, turn, s):
            for e in range(ESETS + 1):
                yield scores_first(s) + e
                if e < ESETS:
                    b, j = e % PAIR, e // PAIR
                    r = rows(j, QUAD)
                    if e > 0:
                        n = 2 * e - 1 if s in CAUSAL else e
                        pe.wait_ge(h.probs_ready.sem, h.probs_ready.at(turn, s, n))
                    elif s in CAUSAL:
                        pe.wait_ge(h.negm_ready.sem, h.negm_ready.at(turn, s))
                    else:
                        pe.wait_ge(h.q_ready.sem, h.q_ready.at(turn, s, 2))
                        pe.wait_ge(h.k_ready.sem, h.k_ready.at(turn, s, 2))
                        pe.wait_ge(h.v_ready.sem, h.v_ready.at(turn, s))
                    tile0, tile1 = slice(b * SEQ, b * SEQ + P), slice(b * SEQ + P, (b + 1) * SEQ)
                    if s in CAUSAL:
                        for g in range(GROUPS):
                            minus_max = max_rows[r, g:g + 1].broadcast_to([QUAD, P])
                            out = h.ps[:, g // 2, g % 2 * SEQ:(g % 2 + 1) * SEQ]
                            nc.tensor.matmul(out, h.k4r[r, g, tile0], h.q4r[r, g, b * SEQ:(b + 1) * SEQ],
                                             start=(g % 2 == 0), stop=False, skip_group_check=True)
                            last = nc.tensor.matmul(out, minus_max, h.maxTr[r, b * SEQ:(b + 1) * SEQ],
                                                    start=False, stop=True, skip_group_check=True)
                        last.then_inc(h.score_ps.sem, 1)
                        if e > 0:
                            pe.wait_ge(h.probs_ready.sem, h.probs_ready.at(turn, s, 2 * e))
                        for g in range(GROUPS):
                            minus_max = max_rows[r, g:g + 1].broadcast_to([QUAD, P])
                            out = h.ps[:, 2, g * P:(g + 1) * P]
                            nc.tensor.matmul(out, h.k4r[r, g, tile1], h.q4r[r, g, tile1],
                                             start=(g == 0), stop=False, skip_group_check=True)
                            last = nc.tensor.matmul(out, minus_max, h.maxTr[r, tile1],
                                                    start=False, stop=True, skip_group_check=True)
                    else:
                        for bank, kt, qt in ((0, tile0, tile0), (1, tile1, tile1), (2, tile0, tile1)):
                            if bank == 2 and e > 0:
                                pe.wait_ge(h.full_ready.sem, h.full_ready.at(turn, s, e))
                            for g in range(GROUPS):
                                last = nc.tensor.matmul(h.ps[:, bank, g * P:(g + 1) * P], h.k4r[r, g, kt], h.q4r[r, g, qt],
                                                        start=True, stop=True, skip_group_check=True)
                            if bank == 1:
                                last.then_inc(h.score_ps.sem, 1)
                    last.then_inc(h.score_ps.sem, 1)
                if e > 0:
                    headed_pv_pe(pe, h, turn, s, e - 1)

        def clear_ps(bank):
            nc.tensor.matmul(bank, ident_bf[:], zero_bf[:].broadcast_to([P, TOK]), start=True, stop=False,
                             skip_group_check=True)

        def headed_pv_pe(pe, h, turn, s, e):
            b, j = e % PAIR, e // PAIR
            if s in CAUSAL:
                pe.wait_ge(h.masked.sem, h.masked.at(turn, s, 2 * (e + 1)))
            else:
                pe.wait_ge(h.probs_ready.sem, h.probs_ready.at(turn, s, e + 1))
                pe.wait_ge(h.full_ready.sem, h.full_ready.at(turn, s, e + 1))
            if b == 0:
                if j > 0:
                    pe.wait_ge(h.part_ready.sem, h.part_ready.at(turn, s, j))
                clear_ps(h.ps[:, 3, :])
            pw = h.probs[:, e % 2, :]
            for g in range(GROUPS):
                hd = HPG * g + j
                out = h.ps[rows(g, V1), 3, b * SEQ:(b + 1) * SEQ]
                first, second = h.v9[:, 2 * b, hd, :], h.v9[:, 2 * b + 1, hd, :]
                if s in CAUSAL:
                    nc.tensor.matmul(out, first, pw[:, g * SEQ:(g + 1) * SEQ], start=False, stop=False,
                                     skip_group_check=True)
                else:
                    nc.tensor.matmul(out[:, 0:P], first, pw[:, diagonal_at(s, g, 0)], start=False, stop=False,
                                     skip_group_check=True)
                    nc.tensor.matmul(out[:, P:SEQ], first, pw[:, full_at(s, g)], start=False, stop=False,
                                     skip_group_check=True)
                last = nc.tensor.matmul(out[:, P:SEQ], second, pw[:, diagonal_at(s, g, 1)], start=False, stop=True,
                                        skip_group_check=True)
            last.then_inc(h.pv_ps.sem, 1)

        def headed_exp_act(act, h, turn, s):
            for e in range(ESETS):
                yield scores_first(s) + e
                table(LN_EXP)
                for c, (first, end) in enumerate(((0, 2), (2, 3))):
                    act.wait_ge(h.score_ps.sem, h.score_ps.at(turn, s, 2 * e + c + 1))
                    if e >= 2 and c == 0:
                        act.wait_ge(h.pv_ps.sem, h.pv_ps.at(turn, s, e - 1))
                    nc.scalar.activation(h.probs[:, e % 2, first * TOK:end * TOK].rearrange("p (b c) -> p b c", c=TOK),
                                         h.ps[:, first:end, :], ACT.Exp, scale=float(HD) ** -0.5)\
                        .then_inc(h.probs_ready.sem, 1)

        def causal_mask_dve(dve, h, turn, s):
            keep = C("keep_k").unsqueeze(1).broadcast_to([P, GROUPS, P])
            for e in range(ESETS):
                yield scores_first(s) + e
                if e >= PAIR and e % PAIR == 0:
                    headed_part_dve(dve, h, turn, s, e // PAIR - 1)
                for c in range(2):
                    dve.wait_ge(h.probs_ready.sem, h.probs_ready.at(turn, s, 2 * e + c + 1))
                    if c == 0:
                        blocks = h.probs[:, e % 2, 0:2 * TOK].rearrange("p (g q) -> p g q", q=SEQ)[:, :, 0:P]
                    else:
                        blocks = h.probs[:, e % 2, 2 * TOK:3 * TOK].rearrange("p (g q) -> p g q", q=P)
                    nc.vector.tensor_tensor(blocks, blocks, keep, ALU.min).then_inc(h.masked.sem, 1)

        def linear_full_act(act, h, turn, s):
            for e in range(ESETS):
                yield scores_first(s) + e
                act.wait_ge(h.score_ps.sem, h.score_ps.at(turn, s, 2 * e + 2))
                if e >= 2:
                    act.wait_ge(h.pv_ps.sem, h.pv_ps.at(turn, s, e - 1))
                nc.scalar.activation(h.probs[:, e % 2, 2 * TOK:], h.ps[:, 2, :], ACT.Copy).then_inc(h.full_ready.sem, 1)

        def linear_mask_dve(dve, h, turn, s):
            keep = C("keep_k").unsqueeze(1).broadcast_to([P, 2 * GROUPS, P])
            for e in range(ESETS):
                yield scores_first(s) + e
                dve.wait_ge(h.score_ps.sem, h.score_ps.at(turn, s, 2 * e + 1))
                if e >= 2:
                    dve.wait_ge(h.pv_ps.sem, h.pv_ps.at(turn, s, e - 1))
                nc.vector.tensor_tensor(h.probs[:, e % 2, 0:2 * TOK].rearrange("p (n q) -> p n q", q=P),
                                        h.ps[:, 0:2, :].rearrange("p b (g q) -> p (b g) q", q=P), keep, ALU.mult)\
                    .then_inc(h.probs_ready.sem, 1)
                if e >= PAIR and e % PAIR == 0:
                    headed_part_dve(dve, h, turn, s, e // PAIR - 1)

        def headed_part_dve(dve, h, turn, s, j):
            dve.wait_ge(h.pv_ps.sem, h.pv_ps.at(turn, s, PAIR * (j + 1)))
            nc.vector.tensor_copy(h.parts[s][j], h.ps[:, 3, :]).then_inc(h.part_ready.sem, 1)

        def heads_out_pe(pe, h, turn, s, first):
            yield first
            pe.wait_ge(h.part_ready.sem, h.part_ready.at(turn, s, UNITS if s == "arccos" else HPG))
            for j in range(HPG):
                last = nc.tensor.matmul(h.ps[:, j, :], C("den"), h.parts[s][j], start=True, stop=True)
                if j % 2:
                    last.then_inc(h.den_ps.sem, 1)
            yield first + 1
            for j in range(HPG):
                if j % 2 == 0:
                    pe.wait_ge(h.y_ready.sem, h.y_ready.at(turn, s, j // 2 + 1))
                last = nc.tensor.matmul(h.ps[:, 0, :], C("dense")[:, j * P:(j + 1) * P], h.parts[s][j],
                                        start=(j == 0), stop=(j == HPG - 1))
            last.then_inc(h.yT_ps.sem, 1)
            yield first + 2
            pe.wait_ge(h.yT_ready.sem, h.yT_ready.at(turn, s))
            nc.tensor.matmul(h.ps[:, 1, :], W(s, "o"), h.xn[:], start=True, stop=True).then_inc(h.o_ps.sem, 1)

        def heads_out_act(act, h, turn, s, first):
            yield first
            table(LN_EXP)
            for c in range(2):
                r, den = h.rden4[s][:, 2 * c:2 * c + 2, :], h.ps[:, 2 * c:2 * c + 2, :]
                act.wait_ge(h.den_ps.sem, h.den_ps.at(turn, s, c + 1))
                if s == "linear":
                    nc.scalar.activation(r, den, ACT.Ln, bias=C("lin_eps")).then_inc(h.den_ln.sem, 1)
                else:
                    nc.scalar.activation(r, den, ACT.Ln).then_inc(h.den_ln.sem, 1)
                act.wait_ge(h.den_ln.sem, h.den_ln.at(turn, s, c + 1))
                nc.scalar.activation(r, r, ACT.Exp, scale=-1.0).then_inc(h.rden_ready.sem, 1)
            yield first + 1
            act.wait_ge(h.yT_ps.sem, h.yT_ps.at(turn, s))
            nc.scalar.activation(h.xn[:], h.ps[:, 0, :], ACT.Copy).then_inc(h.yT_ready.sem, 1)

        def heads_out_dve(dve, h, turn, s, first):
            yield first
            for j in range(HPG):
                if j % 2 == 0:
                    dve.wait_ge(h.rden_ready.sem, h.rden_ready.at(turn, s, j // 2 + 1))
                last = nc.vector.tensor_tensor(h.parts[s][j], h.parts[s][j], h.rden4[s][:, j, :], ALU.mult)
                if j % 2:
                    last.then_inc(h.y_ready.sem, 1)
            yield from residual_dve(dve, h, turn, s, first + 2)

        def residual_dve(dve, h, turn, s, first):
            yield first
            dve.wait_ge(h.o_ps.sem, h.o_ps.at(turn, s))
            r = h.inner(s)
            if s == "arccos":
                nc.vector.scalar_tensor_tensor(out=r[:], in0=h.ps[:, 1, :], scalar=W(s, "bo"), in1=r[:],
                                               op0=ALU.add, op1=ALU.add).then_inc(h.resid.sem, 1)
            else:
                nc.vector.tensor_tensor(r[:], r[:], h.ps[:, 1, :], ALU.add).then_inc(h.resid.sem, 1)

        def headed_pe(pe, h, turn, s):
            yield from headed_project_pe(pe, h, turn, s)
            if s in CAUSAL:
                yield from max_pe(pe, h, turn, s)
            yield from headed_scores_pe(pe, h, turn, s)
            yield from heads_out_pe(pe, h, turn, s, scores_first(s) + ESETS + 1)

        def headed_act(act, h, turn, s):
            yield from headed_project_act(act, h, turn, s)
            if s in CAUSAL:
                yield from max_act(act, h, turn, s, PROJECT + MROUNDS)
                yield from headed_exp_act(act, h, turn, s)
            else:
                yield from linear_full_act(act, h, turn, s)
            yield from heads_out_act(act, h, turn, s, scores_first(s) + ESETS + 1)

        def headed_dve(dve, h, turn, s):
            yield from headed_project_dve(dve, h, turn, s)
            if s in CAUSAL:
                yield from max_dve(dve, h, turn, s)
                yield from causal_mask_dve(dve, h, turn, s)
            else:
                yield from linear_mask_dve(dve, h, turn, s)
            yield scores_first(s) + ESETS
            headed_part_dve(dve, h, turn, s, HPG - 1)
            yield from heads_out_dve(dve, h, turn, s, scores_first(s) + ESETS + 1)

        def mqa_norm_dve(dve, h, turn, s, b):
            heads, dims = MQH, MQD
            dve.wait_ge(h.pv_ps.sem, h.pv_ps.at(turn, s, QSETS // PAIR * (b + 1)))
            o = h.ps[:, 3, 0:2 * heads * (dims + 1)].rearrange("p (h d) -> p h d", d=dims + 1)
            r = h.rden[:, b, :].unsqueeze(2)
            nc.vector.tensor_copy(r, o[:, :, dims:]).then_inc(h.den_step.sem, 1)
            dve.wait_ge(h.den_step.sem, h.den_step.at(turn, s, 2 * b + 1))
            nc.vector.reciprocal(r, r).then_inc(h.den_step.sem, 1)
            dve.wait_ge(h.den_step.sem, h.den_step.at(turn, s, 2 * b + 2))
            nc.vector.tensor_tensor(h.ytok[:, 2 * b:2 * b + 2, :].rearrange("p t (h d) -> p (t h) d", d=dims),
                                    o[:, :, 0:dims], r.broadcast_to([P, 2 * heads, dims]), ALU.mult)\
                .then_inc(h.y_ready.sem, 1)

        def mqa_out_pe(pe, h, turn, s, first):
            yield first
            pe.wait_ge(h.y_ready.sem, h.y_ready.at(turn, s, PAIR))
            for t in range(TILES):
                last = nc.tensor.transpose(h.ps[:, 0, t * P:(t + 1) * P], h.ytok[:, t, :], C("ident"))
            last.then_inc(h.yT_ps.sem, 1)
            yield first + 1
            pe.wait_ge(h.yT_ready.sem, h.yT_ready.at(turn, s))
            nc.tensor.matmul(h.ps[:, 1, :], W(s, "o"), h.xn[:], start=True, stop=True).then_inc(h.o_ps.sem, 1)

        def mqa_out_act(act, h, turn, s, first):
            yield first
            act.wait_ge(h.yT_ps.sem, h.yT_ps.at(turn, s))
            nc.scalar.activation(h.xn[:], h.ps[:, 0, :], ACT.Copy).then_inc(h.yT_ready.sem, 1)

        M_FIRST, Q_FIRST = 1, 1 + TILES + 1

        def mqa_pe(pe, h, turn, s):
            yield 0
            pe.wait_ge(loaded[s], 16)
            pe.wait_ge(h.norm_out.sem, h.norm_out.at(turn, s))
            nc.tensor.matmul(h.ps[:, 0, :], W(s, "q"), h.xn[:], start=True, stop=True).then_inc(h.q_ps.sem, 1)
            nc.tensor.matmul(h.ps[:, 1, :], W(s, "k"), h.xn[:], start=True, stop=True).then_inc(h.k_ps.sem, 1)
            values_pe(h, 2, W(s, "v"), MQD)
            for m in range(TILES):
                yield M_FIRST + m
                if m == 0:
                    pe.wait_ge(h.q_ready.sem, h.q_ready.at(turn, s))
                    pe.wait_ge(h.k_ready.sem, h.k_ready.at(turn, s))
                    pe.wait_ge(h.v_ready.sem, h.v_ready.at(turn, s))
                for j in range(MQH):
                    if m > 0 and j % 2 == 0:
                        pe.wait_ge(h.max_done.sem, h.max_done.at(turn, s, 2 * m - 1 + j // 2))
                    last = nc.tensor.matmul(h.ps[:, j, 0:SEQ], h.q4[rows(j, MQD), 0, m * P:(m + 1) * P],
                                            h.k4[rows(j, MQD), 0, m // 2 * SEQ:(m // 2 + 1) * SEQ],
                                            start=True, stop=True)
                    if j % 2:
                        last.then_inc(h.max_ps.sem, 1)
            yield M_FIRST + TILES
            pe.wait_ge(h.max_pair.sem, h.max_pair.at(turn, s))
            for t in range(TILES):
                last = nc.tensor.transpose(h.ps[:, 0, t * P:(t + 1) * P], h.negm[:, t, :], C("ident"))
            last.then_inc(h.negm_ps.sem, 1)
            for e in range(QSETS + 1):
                yield Q_FIRST + e
                if e < QSETS:
                    b, jp = e // 2, e % 2
                    if e == 0:
                        pe.wait_ge(h.negm_ready.sem, h.negm_ready.at(turn, s))
                    else:
                        pe.wait_ge(h.probs_ready.sem, h.probs_ready.at(turn, s, e))
                    qs = slice(b * SEQ, (b + 1) * SEQ)
                    for kt in range(2):
                        for i in range(2):
                            r = rows(2 * jp + i, MQD)
                            o = h.ps[:, i, kt * SEQ:(kt + 1) * SEQ]
                            nc.tensor.matmul(o, h.k4[r, 0, b * SEQ + kt * P:b * SEQ + (kt + 1) * P], h.q4[r, 0, qs],
                                             start=True, stop=False, skip_group_check=True)
                            last = nc.tensor.matmul(o, max_rows[r, 0:1].broadcast_to([MQD, P]), h.maxTr[r, qs],
                                                    start=False, stop=True, skip_group_check=True)
                    last.then_inc(h.score_ps.sem, 1)
                if e > 0:
                    b, jp = (e - 1) // 2, (e - 1) % 2
                    pe.wait_ge(h.probs_ready.sem, h.probs_ready.at(turn, s, e))
                    if e - 1 == 2:
                        pe.wait_ge(h.y_ready.sem, h.y_ready.at(turn, s, 1))
                    for i in range(2):
                        for qt in range(2):
                            c = (qt * MQH + 2 * jp + i) * MV1
                            for kt in range(2):
                                w = (i * 2 + kt) * SEQ + qt * P
                                last = nc.tensor.matmul(h.ps[:, 3, c:c + MV1], h.probs[:, (e - 1) % 2, w:w + P],
                                                        h.v33[:, 2 * b + kt, :], start=(kt == 0), stop=(kt == 1),
                                                        skip_group_check=True)
                    last.then_inc(h.pv_ps.sem, 1)
            yield from mqa_out_pe(pe, h, turn, s, Q_FIRST + QSETS + 1)

        def mqa_act(act, h, turn, s):
            yield 0
            act.wait_ge(h.q_ps.sem, h.q_ps.at(turn, s))
            nc.scalar.activation(h.q4[:, 0, :], h.ps[:, 0, :], ACT.Copy, scale=float(MQD) ** -0.5)\
                .then_inc(h.q_ready.sem, 1)
            act.wait_ge(h.v_ps.sem, h.v_ps.at(turn, s))
            nc.scalar.activation(h.v33[:, :, 0:MQD], h.ps[:, 2, 0:TILES * MQD].rearrange("p (t d) -> p t d", d=MQD),
                                 ACT.Copy).then_inc(h.v_ready.sem, 1)
            yield from max_act(act, h, turn, s, M_FIRST + TILES)
            for e in range(QSETS):
                yield Q_FIRST + e
                table(LN_EXP)
                act.wait_ge(h.score_ps.sem, h.score_ps.at(turn, s, e + 1))
                if e >= 2:
                    act.wait_ge(h.pv_ps.sem, h.pv_ps.at(turn, s, e - 1))
                nc.scalar.activation(h.probs[:, e % 2, 0:2 * TOK].rearrange("p (b c) -> p b c", b=2), h.ps[:, 0:2, :],
                                     ACT.Exp).then_inc(h.probs_ready.sem, 1)
            yield from mqa_out_act(act, h, turn, s, Q_FIRST + QSETS + 1)

        def mqa_dve(dve, h, turn, s):
            yield 0
            dve.wait_ge(h.k_ps.sem, h.k_ps.at(turn, s))
            nc.vector.tensor_copy(h.k4[:, 0, :], h.ps[:, 1, :]).then_inc(h.k_ready.sem, 1)
            for m in range(TILES):
                yield M_FIRST + m
                for c in range(2):
                    js = slice(2 * c, 2 * c + 2)
                    dve.wait_ge(h.max_ps.sem, h.max_ps.at(turn, s, 2 * m + c + 1))
                    nc.vector.tensor_reduce(max_columns(h, slice(m, m + 1), 0)[:, 0, js, 0], h.ps[:, js, 0:SEQ],
                                            AX.X, ALU.max, negate=True).then_inc(h.max_done.sem, 1)
            yield from max_end_dve(dve, h, turn, s, 2 * TILES, M_FIRST + TILES)
            for b in range(PAIR):
                yield Q_FIRST + 2 * (b + 1)
                mqa_norm_dve(dve, h, turn, s, b)
            yield from residual_dve(dve, h, turn, s, Q_FIRST + QSETS + 2)

        HEADS_FIRST = 2
        STEPS_FIRST = HEADS_FIRST + 2 + 2

        def steps_first(u):
            return STEPS_FIRST + ARC_STEPS * u

        def cos_first(u):
            return steps_first(u - 1) + 2 if u else HEADS_FIRST + 2

        ARC_OUT = steps_first(UNITS) + 2

        def arccos_pe(pe, h, turn, s):
            yield 0
            pe.wait_ge(loaded[s], 16)
            pe.wait_ge(h.norm_out.sem, h.norm_out.at(turn, s))
            nc.tensor.matmul(h.ps[:, 0, :], W(s, "q"), h.xn[:], start=True, stop=True).then_inc(h.q_ps.sem, 1)
            nc.tensor.matmul(h.ps[:, 1, :], W(s, "k"), h.xn[:], start=True, stop=True).then_inc(h.k_ps.sem, 1)
            values_pe(h, 2, W(s, "v"), P)
            yield 1
            for i, (bank, square) in enumerate(((3, h.sq), (0, h.cen))):
                pe.wait_ge(h.arc_sq.sem, h.arc_sq.at(turn, s, i + 1))
                nc.tensor.matmul(h.ps[:, bank, :], C("blk8"), square[:], start=True, stop=True).then_inc(h.arc_norm_ps.sem, 1)
            for i, unit in enumerate((h.y, h.z)):
                yield HEADS_FIRST + i
                pe.wait_ge(h.arc_unit.sem, h.arc_unit.at(turn, s, i + 1))
                if i == 0:
                    pe.wait_ge(h.v_ready.sem, h.v_ready.at(turn, s))
                    pe.wait_ge(h.arc_floor.sem, h.arc_floor.at(turn, s, 2))
                for g in range(GROUPS):
                    if i == 1 and g % 2 == 0:
                        pe.wait_ge(h.q_ready.sem, h.q_ready.at(turn, s, g // 2 + 1))
                    last = nc.tensor.matmul(h.ps[:, g, :], C("esel")[:, g * P:(g + 1) * P], unit[:], start=True, stop=True)
                    if g % 2:
                        last.then_inc(h.head_ps.sem, 1)
            for u in range(UNITS):
                if u > 1:
                    yield cos_first(u) - 1
                    arccos_pv_pe(pe, h, turn, s, u - 2)
                for kt in range(2):
                    yield cos_first(u) + kt
                    b, gp = u // 2, u % 2
                    if kt == 1 or u == 1:
                        pe.wait_ge(h.cos_ready.sem, h.cos_ready.at(turn, s, 2 * u + kt))
                    elif u == 0:
                        pe.wait_ge(h.q_ready.sem, h.q_ready.at(turn, s, 2))
                        pe.wait_ge(h.k_ready.sem, h.k_ready.at(turn, s, 2))
                    else:
                        pe.wait_ge(h.part_ready.sem, h.part_ready.at(turn, s, u - 1))
                    for g2 in range(2):
                        for j in range(HPG):
                            r = rows(j, QUAD)
                            last = nc.tensor.matmul(
                                h.ps[:, j, g2 * SEQ:(g2 + 1) * SEQ],
                                h.k4r[r, 2 * gp + g2, b * SEQ + kt * P:b * SEQ + (kt + 1) * P],
                                h.q4r[r, 2 * gp + g2, b * SEQ:(b + 1) * SEQ], start=True, stop=True, skip_group_check=True)
                    last.then_inc(h.score_ps.sem, 1)
            for u in range(UNITS - 2, UNITS):
                yield steps_first(u + 1) + 1
                arccos_pv_pe(pe, h, turn, s, u)
            yield from heads_out_pe(pe, h, turn, s, ARC_OUT)

        def arccos_pv_pe(pe, h, turn, s, u):
            pe.wait_ge(h.vs_ready.sem, h.vs_ready.at(turn, s, u + 1))
            for j in range(HPG):
                if j % 2 == 0:
                    clear_ps(h.ps[:, 2 + j // 2, :])
                for kt in range(2):
                    for g2 in range(2):
                        w = ((kt * HPG + j) * 2 + g2) * SEQ
                        last = nc.tensor.matmul(h.ps[rows(2 * (u % 2) + g2, V1), 2 + j // 2, j % 2 * SEQ:(j % 2 + 1) * SEQ],
                                                h.vs[:, kt, HPG * g2 + j, :], h.cosines[:, u % 2, w:w + SEQ],
                                                start=False, stop=(kt == 1), skip_group_check=True)
            last.then_inc(h.pv_ps.sem, 1)

        def arccos_act(act, h, turn, s):
            yield 0
            for i, (bias, ps_sig, raw, square) in enumerate((("bq", h.q_ps, h.y, h.sq), ("bk", h.k_ps, h.z, h.cen))):
                act.wait_ge(ps_sig.sem, ps_sig.at(turn, s))
                nc.scalar.activation(raw[:], h.ps[:, i, :], ACT.Identity, bias=W(s, bias)).then_inc(h.arc_raw.sem, 1)
                act.wait_ge(h.arc_raw.sem, h.arc_raw.at(turn, s, i + 1))
                nc.scalar.activation(square[:], raw[:], ACT.Square).then_inc(h.arc_sq.sem, 1)
            yield 1
            table(LN_EXP)
            for i, rn in enumerate((h.sq, h.xn)):
                act.wait_ge(h.arc_floor.sem, h.arc_floor.at(turn, s, i + 1))
                nc.scalar.activation(rn[:], rn[:], ACT.Ln, scale=float(2 ** 20)).then_inc(h.arc_ln.sem, 1)
                act.wait_ge(h.arc_ln.sem, h.arc_ln.at(turn, s, i + 1))
                nc.scalar.activation(rn[:], rn[:], ACT.Exp, scale=-0.5, bias=C("ln1024")).then_inc(h.arc_rn.sem, 1)
            for i, (sign, high) in enumerate((("q_sign", h.q_high), ("k_sign", h.k_high))):
                yield HEADS_FIRST + i
                for c in range(2):
                    two = slice(2 * c, 2 * c + 2)
                    act.wait_ge(h.head_ps.sem, h.head_ps.at(turn, s, 2 * i + c + 1))
                    high_act(act, h.ps[:, two, :], h.high[:, two, :], sign, high)
            steps = [(ACT.Ln, 0.5, "half", LN_EXP), (ACT.Tanh, -0.25, None, None), (ACT.Sqrt, 1.0, None, None),
                     (ACT.Arctan, 1.0, None, None), (ACT.Ln, 4.0, "one", LN_EXP), (ACT.Exp, GEO_POWER, None, LN_EXP)]
            for u in range(UNITS):
                cosines = h.cosines[:, u % 2, :]
                for n, (func, scale, bias, in_table) in enumerate(steps):
                    yield steps_first(u) + n
                    table(in_table)
                    if n == 0:
                        act.wait_ge(h.cos_ready.sem, h.cos_ready.at(turn, s, 2 * u + 2))
                    else:
                        act.wait_ge(h.arc_pass.sem, h.arc_pass.at(turn, s, ARC_STEPS * u + n))
                    if bias is None:
                        nc.scalar.activation(cosines, cosines, func, scale=scale).then_inc(h.arc_pass.sem, 1)
                    else:
                        nc.scalar.activation(cosines, cosines, func, scale=scale, bias=C(bias)).then_inc(h.arc_pass.sem, 1)
            yield from heads_out_act(act, h, turn, s, ARC_OUT)

        def arccos_sums_dve(dve, h, turn, s, u):
            dve.wait_ge(h.arc_pass.sem, h.arc_pass.at(turn, s, ARC_STEPS * (u + 1)))
            for kt in range(2):
                nc.vector.tensor_reduce(
                    h.nsum[:, kt, :].rearrange("p (g2 j) -> p j g2", g2=2),
                    h.cosines[:, u % 2, kt * 4 * TOK:(kt + 1) * 4 * TOK].rearrange("p (j g2 q) -> p j g2 q", g2=2, q=SEQ),
                    AX.X, ALU.add).then_inc(h.nsum_step.sem, 1)
            dve.wait_ge(h.nsum_step.sem, h.nsum_step.at(turn, s, 3 * u + 2))
            nc.vector.reciprocal(h.nsum[:], h.nsum[:]).then_inc(h.nsum_step.sem, 1)
            dve.wait_ge(h.nsum_step.sem, h.nsum_step.at(turn, s, 3 * u + 3))
            dve.wait_ge(h.v_ready.sem, h.v_ready.at(turn, s))
            for kt in range(2):
                last = nc.vector.tensor_tensor(
                    h.vs[:, kt, :, :], h.v9[:, u // 2 * 2 + kt, u % 2 * UHEADS:(u % 2 + 1) * UHEADS, :],
                    h.nsum[:, kt, :].unsqueeze(2).broadcast_to([P, UHEADS, V1]), ALU.mult)
            last.then_inc(h.vs_ready.sem, 1)

        def arccos_dve(dve, h, turn, s):
            yield 0
            dve.wait_ge(h.v_ps.sem, h.v_ps.at(turn, s))
            nc.vector.tensor_tensor(h.v9[:, :, :, 0:HD].rearrange("p t h d -> p (t h) d"),
                                    h.ps[:, 2, :].rearrange("p (h d) -> p h d", d=HD),
                                    W(s, "bv").unsqueeze(1).broadcast_to([P, TILES, P])
                                    .rearrange("p t (h d) -> p t h d", d=HD), ALU.add).then_inc(h.v_ready.sem, 1)
            yield 1
            for i, (bank, rn) in enumerate(((3, h.sq), (0, h.xn))):
                dve.wait_ge(h.arc_norm_ps.sem, h.arc_norm_ps.at(turn, s, i + 1))
                nc.vector.tensor_scalar(rn[:], h.ps[:, bank, :], 1e-24, None, ALU.max).then_inc(h.arc_floor.sem, 1)
            for i, (raw, rn) in enumerate(((h.y, h.sq), (h.z, h.xn))):
                dve.wait_ge(h.arc_rn.sem, h.arc_rn.at(turn, s, i + 1))
                nc.vector.tensor_tensor(raw[:], raw[:], rn[:], ALU.mult).then_inc(h.arc_unit.sem, 1)
            yield HEADS_FIRST
            split_queries_dve(dve, h, turn, s, h.ps)
            yield HEADS_FIRST + 1
            split_keys_dve(dve, h, turn, s, h.ps)
            for u in range(UNITS + 2):
                if u > 1:
                    arccos_sums_dve(dve, h, turn, s, u - 2)
                    yield steps_first(u - 1) + 1
                    v, gp = u - 2, u % 2
                    dve.wait_ge(h.pv_ps.sem, h.pv_ps.at(turn, s, v + 1))
                    r, cs = slice(2 * QUAD * gp, 2 * QUAD * (gp + 1)), slice(v // 2 * SEQ, (v // 2 + 1) * SEQ)
                    for j in range(HPG):
                        last = nc.vector.tensor_copy(h.parts[s][j][r, cs], h.ps[r, 2 + j // 2, j % 2 * SEQ:(j % 2 + 1) * SEQ])
                    last.then_inc(h.part_ready.sem, 1)
                if u < UNITS:
                    for kt in range(2):
                        yield cos_first(u) + kt
                        dve.wait_ge(h.score_ps.sem, h.score_ps.at(turn, s, 2 * u + kt + 1))
                        if u > 1:
                            dve.wait_ge(h.pv_ps.sem, h.pv_ps.at(turn, s, u - 1))
                        nc.vector.tensor_scalar(
                            h.cosines[:, u % 2, kt * 4 * TOK:(kt + 1) * 4 * TOK].rearrange("p (j t) -> p j t", j=HPG),
                            h.ps[:], CLIP, CLIP_LO, ALU.min, ALU.max).then_inc(h.cos_ready.sem, 1)
                if 0 < u <= UNITS:
                    yield steps_first(u)
            yield from heads_out_dve(dve, h, turn, s, ARC_OUT)

        def router_pe(pe, h, turn, s):
            yield 0
            pe.wait_ge(h.norm_out.sem, h.norm_out.at(turn, s))
            pe.wait_ge(loaded[s], 16)
            for t in range(TILES):
                last = nc.tensor.matmul(h.ps[:, 0, t * EXPERTS:(t + 1) * EXPERTS], h.xn[:, t * P:(t + 1) * P],
                                        W(s, "router"), start=True, stop=True)
            last.then_inc(h.logits_ps.sem, 1)
            if s == "moe0":
                yield 2
                pe.wait_ge(h.chosen_ready.sem, h.chosen_ready.at(turn, s))
                for t in range(TILES):
                    o = h.ps[:, 1, t * EXPERTS:(t + 1) * EXPERTS]
                    last = nc.tensor.matmul(o, before_bf[:], h.ohs_bf[:, t, :], start=True, stop=(t % 2 == 0),
                                            skip_group_check=True)
                    if t % 2:
                        last = nc.tensor.matmul(o, ones_bf[:], h.ohs_bf[:, t - 1, :], start=False, stop=True,
                                                skip_group_check=True)
                last.then_inc(h.place_ps.sem, 1)
            n = 1 if s == "mlp" else EXPERTS
            for e in range(n):
                if e % BANKS == 0:
                    yield 2 if s == "mlp" else 3 + e // BANKS
                    if e == 0:
                        pe.wait_ge(h.weight_ready.sem, h.weight_ready.at(turn, s))
                    else:
                        pe.wait_ge(h.wbc_ready.sem, h.wbc_ready.at(turn, s))
                for t in range(TILES):
                    last = nc.tensor.matmul(h.ps[:, e % BANKS if n > 1 else 3, t * P:(t + 1) * P],
                                            h.wtok[:, t, e:e + 1].broadcast_to([P, P]), C("ident"), start=True, stop=True)
                if e % BANKS == BANKS - 1 or e == n - 1:
                    last.then_inc(h.wbc_ps.sem, 1)

        def router_act(act, h, turn, s):
            yield 0
            table(LN_EXP)
            act.wait_ge(h.route_shift.sem, h.route_shift.at(turn, s))
            nc.scalar.activation(h.pr[:], h.lg[:], ACT.Exp).then_inc(h.route_exp.sem, 1)
            if s == "moe1":
                yield 1
                table(LN_EXP)
                act.wait_ge(h.gap_ready.sem, h.gap_ready.at(turn, s))
                nc.scalar.activation(h.s2[:], h.s1[:], ACT.Exp).then_inc(h.gap_exp.sem, 1)
            if s == "mlp":
                yield 2
                act.wait_ge(h.wbc_ps.sem, h.wbc_ps.at(turn, s))
                nc.scalar.activation(h.wbc[:, 0, :], h.ps[:, 3, :], ACT.Copy).then_inc(h.wbc_ready.sem, 1)
            else:
                yield 3
                act.wait_ge(h.wbc_ps.sem, h.wbc_ps.at(turn, s))
                nc.scalar.activation(h.wbc[:, 0:BANKS, :], h.ps[:], ACT.Copy).then_inc(h.wbc_ready.sem, 1)

        def router_dve(dve, h, turn, s):
            n = 0

            def step(ins, then_max=False):
                nonlocal n
                n += 1
                ins.then_inc(h.route_step.sem, 1)
                dve.wait_ge(h.route_step.sem, h.route_step.at(turn, s, n))
                if then_max:
                    dve.sem_inc(wait_carrier)

            full = [P, TILES, EXPERTS]
            lg, pr, t8, s1, s2, s3, s4, wtok = h.lg, h.pr, h.t8, h.s1, h.s2, h.s3, h.s4, h.wtok
            yield 0
            dve.wait_ge(h.logits_ps.sem, h.logits_ps.at(turn, s))
            logits = h.ps[:, 0, 0:TILES * EXPERTS].rearrange("p (t e) -> p t e", e=EXPERTS)
            if s == "mlp":
                step(nc.vector.tensor_copy(lg[:], logits))
            else:
                step(nc.vector.tensor_tensor(lg[:], logits, W(s, "rbias").unsqueeze(1).broadcast_to(full), ALU.add))
            step(nc.vector.tensor_reduce(s1[:], lg[:], AX.X, ALU.max, negate=True))
            nc.vector.tensor_tensor(lg[:], lg[:], s1[:].broadcast_to(full), ALU.add).then_inc(h.route_shift.sem, 1)
            yield 1
            dve.wait_ge(h.route_exp.sem, h.route_exp.at(turn, s))
            step(nc.vector.tensor_reduce(s1[:], pr[:], AX.X, ALU.add))
            step(nc.vector.reciprocal(s2[:], s1[:]))
            step(nc.vector.tensor_tensor(pr[:], pr[:], s2[:].broadcast_to(full), ALU.mult), then_max=True)
            for t in range(TILES):
                nc.vector.max(t8[:, t, :], pr[:, t, :]).then_inc(h.route_step.sem, 1)
            n += TILES
            dve.wait_ge(h.route_step.sem, h.route_step.at(turn, s, n))
            dve.sem_inc(wait_carrier)
            first, second = t8[:, :, 0:1], t8[:, :, 1:2]
            if s == "mlp":
                step(nc.vector.tensor_tensor(s1[:], first, second, ALU.add))
                step(nc.vector.tensor_scalar(s2[:], s1[:], 1e-9, None, ALU.add))
                step(nc.vector.reciprocal(s3[:], s2[:]))
                step(nc.vector.tensor_tensor(s4[:], first, s3[:], ALU.mult))
                step(nc.vector.tensor_tensor(s2[:], second, s3[:], ALU.mult))
                nc.vector.tensor_tensor(wtok[:, :, 0:1], s4[:], s2[:], ALU.add).then_inc(h.weight_ready.sem, 1)
                return
            for t in range(TILES):
                nc.vector.max_index(h.ix[:, t, :], t8[:, t, :], pr[:, t, :]).then_inc(h.route_step.sem, 1)
            n += TILES
            dve.wait_ge(h.route_step.sem, h.route_step.at(turn, s, n))
            step(nc.vector.tensor_copy(h.ixf[:], h.ix[:]))
            iota = C("iota").unsqueeze(1).broadcast_to(full)
            step(nc.vector.tensor_tensor(h.oh1[:], iota, h.ixf[:, :, 0:1].broadcast_to(full), ALU.is_equal))
            step(nc.vector.tensor_tensor(h.oh2[:], iota, h.ixf[:, :, 1:2].broadcast_to(full), ALU.is_equal))
            if s == "moe0":
                step(nc.vector.tensor_tensor(h.ohs[:], h.oh1[:], h.oh2[:], ALU.add))
                nc.vector.tensor_copy(h.ohs_bf[:], h.ohs[:]).then_inc(h.chosen_ready.sem, 1)
                step(nc.vector.tensor_tensor(wtok[:], h.ohs[:], pr[:], ALU.mult))
                yield 2
                dve.wait_ge(h.place_ps.sem, h.place_ps.at(turn, s))
                place = h.ps[:, 1, 0:TILES * EXPERTS].rearrange("p (t e) -> p t e", e=EXPERTS)
                nc.vector.scalar_tensor_tensor(out=wtok[:], in0=place, scalar=float(CAP), in1=wtok[:],
                                               op0=ALU.is_lt, op1=ALU.mult).then_inc(h.weight_ready.sem, 1)
            else:
                nc.vector.tensor_tensor(s1[:], second, first, ALU.subtract).then_inc(h.gap_ready.sem, 1)
                yield 2
                dve.wait_ge(h.gap_exp.sem, h.gap_exp.at(turn, s))
                step(nc.vector.tensor_scalar(s3[:], s2[:], 1.0, None, ALU.add))
                step(nc.vector.reciprocal(s1[:], s3[:]))
                step(nc.vector.tensor_tensor(s4[:], s2[:], s1[:], ALU.mult))
                step(nc.vector.tensor_tensor(h.oh1[:], h.oh1[:], s1[:].broadcast_to(full), ALU.mult))
                step(nc.vector.tensor_tensor(h.oh2[:], h.oh2[:], s4[:].broadcast_to(full), ALU.mult))
                nc.vector.tensor_tensor(wtok[:], h.oh1[:], h.oh2[:], ALU.add).then_inc(h.weight_ready.sem, 1)
            yield 4
            dve.wait_ge(h.wbc_ps.sem, h.wbc_ps.at(turn, s, 2))
            nc.vector.tensor_copy(h.wbc[:, BANKS:, :], h.ps[:]).then_inc(h.wbc_ready.sem, 1)

        def moe0_pe(pe, h, turn, s):
            yield from router_pe(pe, h, turn, s)
            w1, w2 = W(s, "w1"), W(s, "w2")
            for f in range(FSETS + 1):
                yield ROUTE + f
                if f == 0:
                    pe.wait_ge(h.wbc_ready.sem, h.wbc_ready.at(turn, s, 2))
                else:
                    pe.wait_ge(h.hid_ready.sem, h.hid_ready.at(turn, s, 2 * f))
                if f < FSETS:
                    for c in range(2):
                        k = 2 * f + c
                        nc.tensor.matmul(h.ps[:, c, :], w1[:, k * P:(k + 1) * P], h.xn[:], start=True, stop=True)\
                            .then_inc(h.hid_ps.sem, 1)
                if f > 0:
                    e, part = (f - 1) // 2, (f - 1) % 2
                    if e >= 2 and part == 0:
                        pe.wait_ge(h.ffn_taken.sem, h.ffn_taken.at(turn, s, e - 1))
                    for c in range(2):
                        k = 2 * (f - 1) + c
                        last = nc.tensor.matmul(h.ps[:, 2 + e % 2, :], w2[:, k * P:(k + 1) * P], h.hid[:, part, c, :],
                                                start=(part + c == 0), stop=(part + c == 2))
                    last.then_inc(h.ffn_ps.sem, 1)

        def moe0_act(act, h, turn, s):
            yield from router_act(act, h, turn, s)
            for f in range(FSETS):
                yield ROUTE + f
                if f >= 2:
                    act.wait_ge(h.ffn_ps.sem, h.ffn_ps.at(turn, s, f - 1))
                for c in range(2):
                    k = 2 * f + c
                    act.wait_ge(h.hid_ps.sem, h.hid_ps.at(turn, s, k + 1))
                    nc.scalar.activation(h.hid[:, f % 2, c, :], h.ps[:, c, :], ACT.Relu, bias=W(s, "b1")[:, k:k + 1])\
                        .then_inc(h.hid_ready.sem, 1)

        def moe0_dve(dve, h, turn, s):
            yield from router_dve(dve, h, turn, s)
            for e in range(EXPERTS):
                yield ROUTE + 2 * e + 2
                if e == 0:
                    dve.wait_ge(h.wbc_ready.sem, h.wbc_ready.at(turn, s, 2))
                dve.wait_ge(h.ffn_ps.sem, h.ffn_ps.at(turn, s, 2 * e + 2))
                if e >= 1:
                    dve.wait_ge(h.ffn_added.sem, h.ffn_added.at(turn, s, e))
                nc.vector.scalar_tensor_tensor(out=h.tmp, in0=h.ps[:, 2 + e % 2, :], scalar=W(s, "b2")[:, e:e + 1],
                                               in1=h.wbc[:, e, :], op0=ALU.add, op1=ALU.mult).then_inc(h.ffn_taken.sem, 1)
                dve.wait_ge(h.ffn_taken.sem, h.ffn_taken.at(turn, s, e + 1))
                done = h.resid if e == EXPERTS - 1 else h.ffn_added
                nc.vector.tensor_tensor(h.x[:], h.x[:], h.tmp, ALU.add).then_inc(done.sem, 1)

        def moe1_pe(pe, h, turn, s):
            yield from router_pe(pe, h, turn, s)
            for e in range(EXPERTS + 2):
                yield ROUTE + e
                if e == 0:
                    pe.wait_ge(h.wbc_ready.sem, h.wbc_ready.at(turn, s, 2))
                else:
                    pe.wait_ge(h.hid_ready.sem, h.hid_ready.at(turn, s, e))
                if e <= EXPERTS:
                    for i, w in enumerate(("w1", "w3")):
                        last = nc.tensor.matmul(h.ps[:, i, :], W(s, w)[:, e * P:(e + 1) * P], h.xn[:], start=True, stop=True)
                    last.then_inc(h.hid_ps.sem, 1)
                if e > 0:
                    if e >= 3:
                        pe.wait_ge(h.ffn_taken.sem, h.ffn_taken.at(turn, s, e - 2))
                    nc.tensor.matmul(h.ps[:, 2 + (e - 1) % 2, :], W(s, "w2")[:, (e - 1) * P:e * P],
                                     h.hid[:, (e - 1) % 2, 0, :], start=True, stop=True).then_inc(h.ffn_ps.sem, 1)

        def moe1_act(act, h, turn, s):
            yield from router_act(act, h, turn, s)
            for e in range(EXPERTS + 1):
                yield ROUTE + e
                table(None)
                act.wait_ge(h.hid_ps.sem, h.hid_ps.at(turn, s, e + 1))
                if e >= 2:
                    act.wait_ge(h.hid_ready.sem, h.hid_ready.at(turn, s, e - 1))
                nc.scalar.activation(h.gate[:, e % 2, :], h.ps[:, 0, :], ACT.Silu).then_inc(h.gate_ready.sem, 1)

        def moe1_dve(dve, h, turn, s):
            yield from router_dve(dve, h, turn, s)
            for e in range(EXPERTS + 2):
                yield ROUTE + e
                if e == 0:
                    dve.wait_ge(h.wbc_ready.sem, h.wbc_ready.at(turn, s, 2))
                if e <= EXPERTS:
                    dve.wait_ge(h.gate_ready.sem, h.gate_ready.at(turn, s, e + 1))
                    if e >= 2:
                        dve.wait_ge(h.ffn_ps.sem, h.ffn_ps.at(turn, s, e - 1))
                    nc.vector.tensor_tensor(h.hid[:, e % 2, 0, :], h.gate[:, e % 2, :], h.ps[:, 1, :], ALU.mult)\
                        .then_inc(h.hid_ready.sem, 1)
                if e > 0:
                    f = e - 1
                    dve.wait_ge(h.ffn_ps.sem, h.ffn_ps.at(turn, s, f + 1))
                    if f >= 1:
                        dve.wait_ge(h.ffn_added.sem, h.ffn_added.at(turn, s, f))
                    if f < EXPERTS:
                        nc.vector.tensor_tensor(h.tmp, h.ps[:, 2 + f % 2, :], h.wbc[:, f, :], ALU.mult)\
                            .then_inc(h.ffn_taken.sem, 1)
                    else:
                        nc.vector.tensor_copy(h.tmp, h.ps[:, 2 + f % 2, :]).then_inc(h.ffn_taken.sem, 1)
                    dve.wait_ge(h.ffn_taken.sem, h.ffn_taken.at(turn, s, f + 1))
                    nc.vector.tensor_tensor(h.z[:], h.z[:], h.tmp, ALU.add).then_inc(h.ffn_added.sem, 1)
            dve.wait_ge(h.ffn_added.sem, h.ffn_added.at(turn, s, EXPERTS + 1))
            dve.wait_ge(back.resid.sem, back.resid.before(turn))
            nc.vector.tensor_tensor(back.x[:], h.x[:], h.z[:], ALU.add).then_inc(h.resid.sem, 1)

        def mlp_pe(pe, h, turn, s):
            yield from router_pe(pe, h, turn, s)
            for f in range(3):
                yield 2 + f
                if f > 0:
                    pe.wait_ge(h.hid_ready.sem, h.hid_ready.at(turn, s, 2 * f))
                if f < 2:
                    for c in range(2):
                        k = 2 * f + c
                        nc.tensor.matmul(h.ps[:, c, :], W(s, "up")[:, k * P:(k + 1) * P], h.xn[:], start=True, stop=True)\
                            .then_inc(h.hid_ps.sem, 1)
                if f > 0:
                    for c in range(2):
                        k = 2 * (f - 1) + c
                        last = nc.tensor.matmul(h.ps[:, 2, :], W(s, "down")[:, k * P:(k + 1) * P], h.hid[:, f - 1, c, :],
                                                start=(k == 0), stop=(k == CH0 - 1))
            last.then_inc(h.ffn_ps.sem, 1)

        def mlp_act(act, h, turn, s):
            yield from router_act(act, h, turn, s)
            for f in range(2):
                yield 2 + f
                table(None)
                for c in range(2):
                    k = 2 * f + c
                    act.wait_ge(h.hid_ps.sem, h.hid_ps.at(turn, s, k + 1))
                    nc.scalar.activation(h.hid[:, f, c, :], h.ps[:, c, :], ACT.Silu).then_inc(h.hid_ready.sem, 1)

        def mlp_dve(dve, h, turn, s):
            yield from router_dve(dve, h, turn, s)
            yield 4
            dve.wait_ge(h.wbc_ready.sem, h.wbc_ready.at(turn, s))
            dve.wait_ge(h.ffn_ps.sem, h.ffn_ps.at(turn, s))
            nc.vector.tensor_tensor(h.tmp, h.ps[:, 2, :], h.wbc[:, 0, :], ALU.mult).then_inc(h.ffn_taken.sem, 1)
            dve.wait_ge(h.ffn_taken.sem, h.ffn_taken.at(turn, s))
            nc.vector.tensor_tensor(h.z[:], h.z[:], h.tmp, ALU.add).then_inc(h.ffn_added.sem, 1)
            dve.wait_ge(h.ffn_added.sem, h.ffn_added.at(turn, s))
            nc.vector.tensor_tensor(h.x[:], h.x[:], h.z[:], ALU.add).then_inc(h.resid.sem, 1)

        def block_pe(pe, h, turn, s):
            i = int(s[-1])
            yield 0
            if i == 0:
                pe.wait_ge(h.norm_out.sem, h.norm_out.at(turn, "qlora"))
            else:
                pe.wait_ge(h.resid.sem, h.resid.at(turn, f"block{i - 1}"))
            nc.tensor.matmul(h.ps[:, 2, :], weff[:, 2 * i * P:(2 * i + 1) * P], h.z[:], start=True, stop=True)\
                .then_inc(h.lin_ps.sem, 1)
            yield from norm_pe(pe, h, turn, s, 1)
            yield 1 + NORM_ROUNDS + 1
            pe.wait_ge(h.gelu_ready.sem, h.gelu_ready.at(turn, s))
            nc.tensor.matmul(h.ps[:, 3, :], weff[:, (2 * i + 1) * P:(2 * i + 2) * P], h.sq[:], start=True, stop=True)\
                .then_inc(h.lin_ps.sem, 1)

        def block_act(act, h, turn, s):
            i = int(s[-1])
            yield from norm_act(act, h, turn, s, 1)
            yield 1 + NORM_ROUNDS
            table(None)
            act.wait_ge(h.norm_out.sem, h.norm_out.at(turn, s))
            nc.scalar.activation(h.sq[:], h.xn[:], ACT.Gelu, scale=W("qlora", "gamma")[:, i:i + 1],
                                 bias=W("qlora", "beta")[:, i:i + 1]).then_inc(h.gelu_ready.sem, 1)

        def block_dve(dve, h, turn, s):
            i = int(s[-1])
            bias = W("qlora", "bias")
            yield 0
            dve.wait_ge(h.lin_ps.sem, h.lin_ps.at(turn, s, 1))
            nc.vector.tensor_scalar(h.y[:], h.ps[:, 2, :], bias[:, 2 * i:2 * i + 1], None, ALU.add).then_inc(h.resid.sem, 1)
            yield from norm_dve(dve, h, turn, s, 1)
            yield 1 + NORM_ROUNDS + 1
            dve.wait_ge(h.lin_ps.sem, h.lin_ps.at(turn, s, 2))
            out, done = (h.z, h.resid) if i < 2 else (h.y, h.lin_sum)
            nc.vector.scalar_tensor_tensor(out=out[:], in0=h.ps[:, 3, :], scalar=bias[:, 2 * i + 1:2 * i + 2],
                                           in1=h.z[:], op0=ALU.add, op1=ALU.add).then_inc(done.sem, 1)
            if i == 2:
                dve.wait_ge(h.lin_sum.sem, h.lin_sum.at(turn, s))
                nc.vector.tensor_tensor(h.z[:], h.x[:], h.y[:], ALU.add).then_inc(h.resid.sem, 1)

        in_table = [None]

        def table(name):
            if name and in_table[0] != name:
                nc.scalar.preload_act_table_set(name)
            in_table[0] = name

        def run(eng, stage_of):
            def half(h, parts, turn):
                return in_rounds(parts, turn, {kind: lambda t, s, f=f: f(eng, h, t, s) for kind, f in stage_of.items()})

            table(None)
            weave(schedule([FRONT]), [half(front, FRONT, Turn(None, 0))])
            table(None)
            with eng.Fori(0, PASSES - 1) as i:
                weave(schedule([FRONT, BACK]), [half(front, FRONT, Turn(i, 1)), half(back, BACK, Turn(i, 0))])
            table(None)
            weave(schedule([BACK]), [half(back, BACK, Turn(None, PASSES - 1))])

        @block.sync
        def _(sp):
            def load(s):
                first, end, _ = cols[s]
                into = once[:, first:end] if s in ONCE else wts[:, first - skip:end - skip]
                sp.dma_start(into, w_dram[:, first:end]).then_inc(loaded[s], 16)

            def load_x(p, tokens):
                if not isinstance(p, Turn):
                    p = Turn(None, p)
                sp.wait_ge(front.resid.sem, front.resid.at(p, "load"))
                sp.sem_inc(wait_carrier)
                sp.dma_start(front.xin[:], x_dram[:, tokens]).then_inc(xin_loaded, 16)

            def store(p, tokens):
                sp.wait_ge(back.resid.sem, back.resid.at(p, "block2"))
                sp.sem_inc(wait_carrier)
                sp.dma_start(out_dram[:, tokens], back.z[:]).then_inc(out_stored, 16)

            load("masks")
            load("const")
            sp.dma_start(front.xin[:], x_dram[:, 0:TOK]).then_inc(xin_loaded, 16)
            load("causal0")
            load("lora")
            sp.dma_start(qint, qw_dram).then_inc(qint_loaded, 16)
            for s in list(STAGES)[4:]:
                load(s)
            load_x(0, slice(TOK, 2 * TOK))
            with sp.Fori(0, PASSES - 2) as i:
                load_x(Turn(i, 1), bass.ds(i * TOK + 2 * TOK, TOK))
                store(Turn(i, 0), bass.ds(i * TOK, TOK))
            for p in range(PASSES - 2, PASSES):
                store(Turn(None, p), slice(p * TOK, (p + 1) * TOK))
            sp.wait_ge(out_stored, (PASSES + 1) * 16)

        @block.gpsimd
        def _(pool):
            nc.gpsimd.memset(front.v9[:], 1.0).then_inc(consts_ready, 1)
            nc.gpsimd.memset(back.v9[:], 1.0).then_inc(consts_ready, 1)
            nc.gpsimd.memset(zero_bf[:], 0.0).then_inc(consts_ready, 1)
            nc.gpsimd.memset(front.negm[:], 0.0).then_inc(consts_ready, 1)
            nc.gpsimd.memset(back.negm, 0.0).then_inc(consts_ready, 1)
            nc.gpsimd.memset(front.v33[:], 1.0).then_inc(consts_ready, 1)
            nc.gpsimd.memset(back.z[:], 0.0).then_inc(out_stored, 16)

        CONSTS = 11

        @block.tensor
        def _(pe):
            pe.wait_ge(loaded["const"], 16)
            pe.wait_ge(consts_ready, CONSTS)
            pe.wait_ge(loaded["lora"], 16)
            for i in range(6):
                last = nc.tensor.matmul(back.ps[:, i // 4, i % 4 * P:(i % 4 + 1) * P],
                                        W("lora", "la")[0:RANK, i * P:(i + 1) * P],
                                        W("lora", "lb")[0:RANK, i * P:(i + 1) * P], start=True, stop=True)
            last.then_inc(lora_ps, 1)
            pe.wait_ge(weff_ready, 1)
            pe.wait_ge(loaded["qlora"], 16)
            run(pe, {"norm": norm_pe, "causal": headed_pe, "linear": headed_pe, "mqa": mqa_pe, "moe0": moe0_pe,
                     "moe1": moe1_pe, "mlp": mlp_pe, "arccos": arccos_pe, "block": block_pe})

        @block.scalar
        def _(act):
            act.wait_ge(loaded["const"], 16)
            act.wait_ge(consts_ready, CONSTS)
            run(act, {"norm": norm_act, "causal": headed_act, "linear": headed_act, "mqa": mqa_act, "moe0": moe0_act,
                      "moe1": moe1_act, "mlp": mlp_act, "arccos": arccos_act, "block": block_act})

        @block.vector
        def _(dve):
            dve.wait_ge(loaded["const"], 16)
            dve.wait_ge(loaded["masks"], 16)
            nc.vector.tensor_copy(ident_bf[:], C("ident")).then_inc(consts_ready, 1)
            nc.vector.tensor_copy(mask_q[:], W("masks", "mask_q")).then_inc(consts_ready, 1)
            nc.vector.tensor_copy(before_bf[:], W("masks", "before")).then_inc(consts_ready, 1)
            nc.vector.tensor_copy(max_rows[:], C("max_rows")).then_inc(consts_ready, 1)
            nc.vector.tensor_copy(ones_bf[:], W("masks", "ones")).then_inc(consts_ready, 1)
            nc.vector.memset(front.x[:], 0.0).then_inc(front.resid.sem, 1)
            nc.vector.memset(back.x[:], 0.0).then_inc(back.resid.sem, 1)
            dve.wait_ge(qint_loaded, 16)
            nc.vector.tensor_copy(weff[:], qint).then_inc(dequant_step, 1)
            dve.wait_ge(dequant_step, 1)
            nc.vector.tensor_scalar(weff[:], weff[:], 1.0 / 7.5, -1.0, ALU.mult, ALU.add).then_inc(dequant_step, 1)
            dve.wait_ge(dequant_step, 2)
            dve.wait_ge(loaded["lora"], 16)
            nc.vector.tensor_tensor(weff[:], weff[:], W("lora", "scale"), ALU.mult).then_inc(dequant_step, 1)
            dve.wait_ge(dequant_step, 3)
            dve.wait_ge(lora_ps, 1)
            nc.vector.tensor_tensor(weff[:], weff[:], back.ps[:, 0:2, :].rearrange("p a b -> p (a b)")[:, 0:6 * P], ALU.add)\
                .then_inc(weff_ready, 1)
            run(dve, {"norm": norm_dve, "causal": headed_dve, "linear": headed_dve, "mqa": mqa_dve, "moe0": moe0_dve,
                      "moe1": moe1_dve, "mlp": mlp_dve, "arccos": arccos_dve, "block": block_dve})


def _constants():
    p = np.arange(P)
    head, dim = p // HD, p % HD
    esel = np.zeros((P, GROUPS, P), np.float32)
    for i in range(QUAD // HD):
        esel[p, head // HPG, QUAD * (head % HPG) + HD * i + dim] = 1.0
    den = np.zeros((P, P), np.float32)
    den[p // QUAD * QUAD + HD, p] = 1.0
    dense = np.zeros((P, HPG, P), np.float32)
    dense[QUAD * (head // HPG) + dim, head % HPG, p] = 1.0
    later = (p[None, :] > p[:, None])
    zero = np.zeros((P, P), np.float32)
    mask_q = np.where(later, NEG, 0.0).astype(np.float32)
    keep = (~later.T).astype(np.float32)

    q_low, k_low, m_low = p % QUAD // 16, p % 16 // HD, p % 2

    def col(v):
        return np.broadcast_to(np.asarray(v, np.float32), (P,))[:, None]

    return {"ident": np.eye(P, dtype=np.float32), "blk8": (head[:, None] == head[None, :]).astype(np.float32),
            "esel": esel.reshape(P, -1), "mask_q": mask_q, "keep_k": keep,
            "before": later.astype(np.float32), "ones": zero + 1.0, "mean": zero + 1.0 / P,
            "max_rows": (p[:, None] % QUAD // 2 == np.arange(GROUPS)[None, :]).astype(np.float32),
            "q_low": col(q_low), "q_sign": col(2 * q_low - 1), "k_low": col(k_low), "k_sign": col(2 * k_low - 1),
            "m_low": col(m_low), "m_sign": col(2 * m_low - 1),
            "iota": np.tile(np.arange(EXPERTS, dtype=np.float32), (P, 1)), "eps5": col(1e-5), "eps6": col(1e-6),
            "half": col(0.5), "one": col(1.0), "ln1024": col(np.log(1024.0)), "lin_eps": col(LIN_EPS), "den": den, "dense": dense.reshape(P, -1)}


def _quadrants(w):
    return np.tile(w.reshape(P, GROUPS, HPG, 1, HD), (1, 1, 1, QUAD // HD, 1)).reshape(P, GROUPS * P)


def _rows(v):
    return np.broadcast_to(v.reshape(1, -1), (P, v.size))


def _side(w):
    return w.transpose(1, 0, 2).reshape(w.shape[1], -1)


def _chunks(w):
    n, h, o = w.shape
    return w.reshape(n, h // P, P, o).transpose(2, 0, 1, 3).reshape(P, -1)


def kernel(**inputs):
    import concourse.bacc as bacc
    from concourse.bass_utils import run_bass_kernel_spmd

    a = {k: np.asarray(v) for k, v in inputs.items()}

    def headed(q, k, v, o):
        return {"q": _quadrants(q), "k": _quadrants(k), "v": v, "o": o}

    def tall(w):
        return np.concatenate([w, np.zeros((P - w.shape[0], w.shape[1]), w.dtype)], 0)

    qkv2, lin, qkv3 = a["L2_ffn_qkv_w"].T, a["L2_attn_wqkv"], a["L3_attn_w_qkv"].T
    b3 = a["L3_attn_b_qkv"]
    both = {n: np.concatenate([a[f"L1_ffn_e{n}"], a[f"L1_ffn_s{n}"][None]], 0) for n in ("W1", "W2", "W3")}
    parts = {
        "masks": _constants(),
        "const": _constants(),
        "causal0": headed(a["L0_attn_WQ"].T, a["L0_attn_WK"].T, a["L0_attn_WV"].T, a["L0_attn_WO"].T),
        "moe0": {"router": a["L0_ffn_Wr"], "rbias": _rows(a["L0_ffn_br"]), "w1": _side(a["L0_ffn_W1"]),
                 "b1": a["L0_ffn_b1"].reshape(EXPERTS * CH0, P).T, "w2": _chunks(a["L0_ffn_W2"]), "b2": a["L0_ffn_b2"].T},
        "causal1": headed(a["L1_attn_Wq"].T, a["L1_attn_Wk"].T, a["L1_attn_Wv"].T, a["L1_attn_Wo"].T),
        "mqa": {"g": a["L1_ffn_g1"][:, None], "q": a["L1_ffn_Wq"].T, "k": np.tile(a["L1_ffn_Wkc"].T, (1, MQH)),
                "v": a["L1_ffn_Wvc"].T, "o": a["L1_ffn_Wo"].T},
        "moe1": {"g": a["L1_ffn_g2"][:, None], "router": a["L1_ffn_Wr"].T, "rbias": _rows(a["L1_ffn_expert_bias"]),
                 **{n.lower(): _side(both[n].transpose(0, 2, 1)) for n in ("W1", "W3", "W2")}},
        "linear": headed(lin[:, 0:P], lin[:, P:2 * P], lin[:, 2 * P:], a["L2_attn_wo"]),
        "causal2": {"g": a["L2_ffn_n1_w"][:, None],
                    **headed(qkv2[:, 0:P], qkv2[:, P:2 * P], qkv2[:, 2 * P:], a["L2_ffn_o_w"].T)},
        "mlp": {"g": a["L2_ffn_n2_w"][:, None], "router": a["L2_ffn_gate_w"].T, "up": a["L2_ffn_up_w"].T,
                "down": _chunks(a["L2_ffn_down_w"].T[None])},
        "arccos": {"q": qkv3[:, 0:P], "k": qkv3[:, P:2 * P], "v": qkv3[:, 2 * P:], "o": a["L3_attn_w_out"].T,
                   "bq": b3[0:P, None], "bk": b3[P:2 * P, None], "bv": _rows(b3[2 * P:]), "bo": a["L3_attn_b_out"][:, None]},
        "qlora": {"bias": a["L3_ffn_biases"].T, "gamma": a["L3_ffn_ln_gamma"].T, "beta": a["L3_ffn_ln_beta"].T},
        "lora": {"scale": _side(np.repeat(a["L3_ffn_scales"].transpose(0, 2, 1), QGROUP, 1)),
                 "la": tall(_side(a["L3_ffn_lora_a"])), "lb": tall(_side(a["L3_ffn_lora_b"].transpose(0, 2, 1)))},
    }
    blob = np.concatenate([parts[s][n] for s, names in STAGES.items() for n, _ in names], 1)
    arrays = {"x_dram": np.ascontiguousarray(a["L0_attn_x"].reshape(BATCH * SEQ, P).T),
              "w_dram": np.ascontiguousarray(blob),
              "qw_dram": np.ascontiguousarray(_side(a["L3_ffn_qweights"].transpose(0, 2, 1)))}
    nc = bacc.Bacc("TRN2", target_bir_lowering=False, num_devices=1)
    args = [nc.dram_tensor(n, v.shape, mybir.dt.from_np(v.dtype), kind="ExternalInput").ap() for n, v in arrays.items()]
    args.append(nc.dram_tensor("out_dram", (P, BATCH * SEQ), F32, kind="ExternalOutput").ap())
    build(nc, *args)
    r = run_bass_kernel_spmd(nc, [arrays], core_ids=[0])
    got = r.results[0]["out_dram"]
    return np.ascontiguousarray(got.T).reshape(BATCH, SEQ, P)
```
